# Optimizing a Trainium2 kernel written in Bass

```python
import numpy as np
import jax
import jax.numpy as jnp

def _softmax(x, axis=-1):
    return jax.nn.softmax(x, axis=axis)

def _gelu(x):
    return jax.nn.gelu(x, approximate=True)

def _silu(x):
    return jax.nn.silu(x)

def _sigmoid(x):
    return jax.nn.sigmoid(x)

def _layernorm(x, axis=-1, eps=1e-05):
    m = jnp.mean(x, axis=axis, keepdims=True)
    v = jnp.var(x, axis=axis, keepdims=True)
    return (x - m) / jnp.sqrt(v + eps)

def _scatter_add(tgt, idx, src, axis=0):
    return tgt.at[idx].add(src)

def _segment_sum(src, seg, n):
    return jax.ops.segment_sum(src, seg, n)
kernel_name = 'mk_gnn_resnorm_d2_gnn_r32_c39702'

def setup_inputs(seed: int=0):
    np.random.seed(seed)
    _w = jnp.asarray

    def _rec_inputs():
        import jax
        import jax.numpy as jnp
        _gk = jax.random.key(seed)
        x = -8.776e-05 + 1 * jax.random.normal(jax.random.fold_in(_gk, 1), (3125, 256), jnp.float32)
        _s = jax.random.randint(jax.random.fold_in(_gk, 2), (25000,), 0, 3125, jnp.int32)
        _d = jax.random.randint(jax.random.fold_in(_gk, 3), (25000,), 0, 3125, jnp.int32)
        _loop = jnp.arange(3125, dtype=jnp.int32)
        src = jnp.concatenate([_s, _d, _loop])
        dst = jnp.concatenate([_d, _s, _loop])
        _o = jnp.argsort(dst, stable=True)
        src = src[_o]
        dst = dst[_o]
        edge_attr_128 = 0.000167468 + 1.0002 * jax.random.normal(jax.random.fold_in(_gk, 11), (53125, 128), jnp.float32)
        edge_weight = jax.random.uniform(jax.random.fold_in(_gk, 13), (53125,), jnp.float32, 0.0, 0.999998)
        return (x, src, dst, edge_attr_128, edge_weight)
    x, src, dst, edge_attr_128, edge_weight = _rec_inputs()

    def _L0_gnn_setup():
        import jax, jax.numpy as jnp
        import numpy as np
        N, E, D, H, C = (625, 10000, 256, 8, 32)
        NEG_SLOPE = 0.2
        key = jax.random.key(seed)
        ks = jax.random.split(key, 9)
        s = 1.0 / np.sqrt(D)
        x = jax.random.normal(ks[0], (N, D), dtype=jnp.float32)
        edge_index = jax.random.randint(ks[1], (2, E), 0, N, dtype=jnp.int32)
        edge_attr = jax.random.uniform(ks[2], (E,), dtype=jnp.float32, minval=0.05, maxval=1.0)
        W_l = jax.random.normal(ks[3], (D, H * C), dtype=jnp.float32) * s
        b_l = jax.random.normal(ks[4], (H * C,), dtype=jnp.float32) * 0.01
        W_r = jax.random.normal(ks[5], (D, H * C), dtype=jnp.float32) * s
        b_r = jax.random.normal(ks[6], (H * C,), dtype=jnp.float32) * 0.01
        att = jax.random.normal(ks[7], (H, C), dtype=jnp.float32) * (1.0 / np.sqrt(C))
        bias = jax.random.normal(ks[8], (H * C,), dtype=jnp.float32) * 0.01
        return {'x': x, 'edge_index': edge_index, 'edge_attr': edge_attr, 'W_l': W_l, 'b_l': b_l, 'W_r': W_r, 'b_r': b_r, 'att': att, 'bias': bias}
    _L0_gnn_all = _L0_gnn_setup()
    _L0_gnn_in = {k: v for k, v in _L0_gnn_all.items() if k in ('W_l', 'b_l', 'W_r', 'b_r', 'att', 'bias')}
    del _L0_gnn_all

    def _L1_gnn_setup():
        import jax, jax.numpy as jnp
        import numpy as np
        N = 625
        E = 10000
        D = 256
        ED = 128
        L = 5
        BN_EPS = 1e-05
        key = jax.random.key(seed)
        ks = jax.random.split(key, 12)
        inp = {'input_feature': jax.random.normal(ks[0], (N, D), jnp.float32), 'edge_index': jax.random.randint(ks[1], (2, E), 0, N, jnp.int64) if jax.config.jax_enable_x64 else jax.random.randint(ks[1], (2, E), 0, N, jnp.int32), 'edge_attr': jax.random.normal(ks[2], (E, ED), jnp.float32), 'W': jax.random.normal(ks[3], (L, D, D), jnp.float32) * (1.0 / np.sqrt(D)), 'b': jax.random.normal(ks[4], (L, D), jnp.float32) * 0.02, 'root': jax.random.normal(ks[5], (L, D), jnp.float32) * 0.02, 'We': jax.random.normal(ks[6], (L, ED, D), jnp.float32) * (1.0 / np.sqrt(ED)), 'be': jax.random.normal(ks[7], (L, D), jnp.float32) * 0.02, 'gamma': jnp.ones((L, D), jnp.float32), 'beta': jnp.zeros((L, D), jnp.float32)}
        return inp
    _L1_gnn_all = _L1_gnn_setup()
    _L1_gnn_in = {k: v for k, v in _L1_gnn_all.items() if k in ('W', 'b', 'root', 'We', 'be', 'gamma', 'beta')}
    del _L1_gnn_all
    return {'x': x, 'src': src, 'dst': dst, 'edge_attr_128': edge_attr_128, 'edge_weight': edge_weight, 'L0_gnn_W_l': _L0_gnn_in['W_l'], 'L0_gnn_b_l': _L0_gnn_in['b_l'], 'L0_gnn_W_r': _L0_gnn_in['W_r'], 'L0_gnn_b_r': _L0_gnn_in['b_r'], 'L0_gnn_att': _L0_gnn_in['att'], 'L0_gnn_bias': _L0_gnn_in['bias'], 'L1_gnn_W': _L1_gnn_in['W'], 'L1_gnn_b': _L1_gnn_in['b'], 'L1_gnn_root': _L1_gnn_in['root'], 'L1_gnn_We': _L1_gnn_in['We'], 'L1_gnn_be': _L1_gnn_in['be'], 'L1_gnn_gamma': _L1_gnn_in['gamma'], 'L1_gnn_beta': _L1_gnn_in['beta']}

def reference(x, src, dst, edge_attr_128, edge_weight, L0_gnn_W_l, L0_gnn_b_l, L0_gnn_W_r, L0_gnn_b_r, L0_gnn_att, L0_gnn_bias, L1_gnn_W, L1_gnn_b, L1_gnn_root, L1_gnn_We, L1_gnn_be, L1_gnn_gamma, L1_gnn_beta):
    import jax
    import jax.numpy as jnp

    def _L0_gnn_ref(x, edge_index, edge_attr, W_l, b_l, W_r, b_r, att, bias):
        import jax, jax.numpy as jnp
        import numpy as np
        N, E, D, H, C = (625, 10000, 256, 8, 32)
        NEG_SLOPE = 0.2
        n = x.shape[0]
        x_l = (x @ W_l + b_l).reshape(n, H, C)
        x_r = (x @ W_r + b_r).reshape(n, H, C)
        src, dst = (edge_index[0], edge_index[1])
        x_j = x_l[src]
        g = jax.nn.leaky_relu(x_r[dst] + x_j, NEG_SLOPE)
        alpha = jnp.einsum('ehc,hc->eh', g, att)
        alpha = alpha + jnp.log(edge_attr)[:, None]
        amax = jax.ops.segment_max(alpha, dst, num_segments=n)
        ex = jnp.exp(alpha - amax[dst])
        denom = jax.ops.segment_sum(ex, dst, num_segments=n)
        alpha = ex / (denom[dst] + 1e-16)
        out = jax.ops.segment_sum(x_j * alpha[..., None], dst, num_segments=n)
        return out.reshape(n, H * C) + bias

    def _L1_gnn_ref(input_feature, edge_index, edge_attr, W, b, root, We, be, gamma, beta):
        import jax, jax.numpy as jnp
        import numpy as np
        N = 625
        E = 10000
        D = 256
        ED = 128
        L = 5
        BN_EPS = 1e-05
        row, col = (edge_index[0], edge_index[1])
        n = input_feature.shape[0]
        deg = jnp.zeros((n,), input_feature.dtype).at[row].add(1.0) + 1.0
        dinv = deg ** (-0.5)
        norm = (dinv[row] * dinv[col])[:, None]
        h = input_feature
        for l in range(L):
            xl = h @ W[l] + b[l]
            ee = edge_attr @ We[l] + be[l]
            msg = norm * jax.nn.relu(xl[row] + ee)
            agg = jnp.zeros_like(xl).at[col].add(msg)
            conv = agg + jax.nn.relu(xl + root[l]) / deg[:, None]
            mean = conv.mean(axis=0)
            var = conv.var(axis=0)
            hbn = (conv - mean) * jax.lax.rsqrt(var + BN_EPS) * gamma[l] + beta[l]
            if l < L - 1:
                hbn = jax.nn.relu(hbn)
            h = hbn + h
        return h
    edge_index = jnp.stack([src, dst])
    x = _layernorm(x + _L0_gnn_ref(x, edge_index, edge_weight, L0_gnn_W_l, L0_gnn_b_l, L0_gnn_W_r, L0_gnn_b_r, L0_gnn_att, L0_gnn_bias), axis=-1)
    x = _layernorm(x + _L1_gnn_ref(x, edge_index, edge_attr_128, L1_gnn_W, L1_gnn_b, L1_gnn_root, L1_gnn_We, L1_gnn_be, L1_gnn_gamma, L1_gnn_beta), axis=-1)
    return x

_drawn_inputs = setup_inputs


def setup_inputs(seed=0):
    import zlib

    import numpy as np

    out = dict(_drawn_inputs(seed))
    spreads = {'L1_gnn_gamma': (1.0, 0.2), 'L1_gnn_beta': (0.0, 0.1)}
    factors = {'L0_gnn_b_l': 7.303,
     'L0_gnn_b_r': 53.806,
     'L0_gnn_bias': 7.477,
     'L1_gnn_b': 8.0,
     'L1_gnn_root': 26.998,
     'L1_gnn_be': 8.0}
    for name, (base, spread) in spreads.items():
        noise = np.random.default_rng([zlib.crc32(name.encode()), seed]).standard_normal(out[name].shape)
        drawn = base * np.exp(spread * noise) if base else spread * noise
        out[name] = jnp.asarray(drawn.astype(out[name].dtype))
    for name, factor in factors.items():
        out[name] = (out[name] * factor).astype(out[name].dtype)
    return out
```

```python
from contextlib import ExitStack

import numpy as np

import concourse.bass as bass
from concourse import mybir

F32, I32, BF16 = mybir.dt.float32, mybir.dt.int32, mybir.dt.bfloat16
ALU = mybir.AluOpType
ACT = mybir.ActivationFunctionType
DVE = mybir.EngineType.DVE
SP = mybir.EngineType.SP

P = 128
N, E, D, ED, H, C, L = 3125, 53125, 256, 128, 8, 32, 5
HALVES = D // P
NC = P // H
KT = -(-E // (P * NC))
NT = NC * KT
CH = KT * P
FULL = E // P
TAIL = E - FULL * P
RB = NT // 4
NP = -(-(N + P) // P) * P
NTILE = NP // P
JC = 2 * P
JT = NP // JC
G = 4
NG = NC // G
RING = 4
S_RING = 8
RESET = -1e38
NO_EDGE = -1e30
LN2_96 = 66.54212933375474
EPS = 1e-5
FAR = 1000000
GW = D + 1
PRM = ["att", "bias", "b", "be", "root", "gamma", "beta"]
PROWS = [2, 2, 2 * L, 2 * L, 2 * L, 2 * L, 2 * L]
PCOL = {n: sum(PROWS[:i]) for i, n in enumerate(PRM)}
NPRM = sum(PROWS)


def pipelined(eng, stages):
    most = max(lead for lead, _ in stages)
    for t in range(-most, 0):
        for lead, stage in stages:
            if t + lead >= 0:
                stage(0, t + lead)

    def body(k, last):
        for c in range(NC):
            for lead, stage in stages:
                if c + lead < NC:
                    stage(k, c + lead)
                elif not last:
                    stage(k + 1, c + lead - NC)

    with eng.Fori(0, KT - 1) as k:
        body(k, False)
    body(KT - 1, True)


def program(nc, x, src, dst, edge_attr, edge_weight, W_l, b_l, W_r, b_r, att, bias,
            W, b, root, We, be, gamma, beta, out):
    ds = bass.ds
    ctx = ExitStack()
    with ctx:
        ctx.enter_context(nc.allow_non_contiguous_dma(reason="single elements at the chunks' borders"))

        def sb(name, shape, dt=F32):
            return ctx.enter_context(nc.sbuf_tensor(name, shape, dt))

        def sem(name):
            return ctx.enter_context(nc.semaphore(name))

        primed = []

        def ring_sem(name, slots=RING):
            s = sem(name)
            primed.append((s, slots))
            return s

        xl_table = nc.dram_tensor("xl_table", (NP, GW), F32).ap()
        x_l_rows = nc.dram_tensor("x_l_rows", (NP, D), F32).ap()
        xr_table = nc.dram_tensor("xr_table", (NP, D), F32).ap()
        gcn_table = nc.dram_tensor("gcn_table", (NP, D), F32).ap()
        attr_T = nc.dram_tensor("attr_T", (NT // G, P, G * P), F32).ap()

        hT = sb("hT", [P, HALVES, NP])
        acc = sb("acc", [P, HALVES, NP])
        conv0 = sb("conv0", [P, HALVES, NP])
        x1T = sb("x1T", [P, HALVES, NP + 2])
        dinv_b = sb("dinv_b", [P, NP + 2])
        invdeg_b = sb("invdeg_b", [P, NP])
        scores = conv0[:, 0, :]
        scoresT = conv0[:, 1, :]
        x1flat = x1T[:].rearrange("p a n -> p (a n)")
        breaks = x1flat[:, 0:CH + 1]
        fwd_max = x1flat[:, CH + 2:2 * CH + 2]
        bwd_max = invdeg_b[:, 0:CH]
        chunk_dst = dinv_b[:, 0:CH + 2].bitcast(I32)
        den = dinv_b[0:H, 0:NP]

        src_idx = sb("src_idx", [P, NT + NC], I32)
        src_hi = sb("src_hi", [P, NT])
        src_lo = sb("src_lo", [P, NT])
        dst_rel = sb("dst_rel", [P, NT])
        log_w = sb("log_w", [P, NT])
        dinv_src = sb("dinv_src", [P, NT])
        base_f = sb("base_f", [1, NT])
        base_i = sb("base_i", [1, NT], I32)

        xg = sb("xg", [P, NC, GW])
        idx = sb("idx", [P, NC], I32)
        S = sb("S", [P, RING, P])
        ring_a = sb("ring_a", [P, RING, D])
        ring_b = sb("ring_b", [P, RING, D])
        ring_c = sb("ring_c", [P, RING, P])
        fifths = sb("fifths", [P, RING, D])
        attr_in = sb("attr_in", [P, NG, G, P])
        attr_out = sb("attr_out", [P, 2, G * P])
        ex_g = sb("ex_g", [P, NG, H, G])
        tiles = sb("tiles", [P, 2, HALVES, P])
        stage = sb("stage", [P, 2, 2 * D])

        wA = sb("wA", [P, HALVES, D])
        wB = sb("wB", [P, HALVES, D])
        rowbias = sb("rowbias", [P, 2, D])
        prm_rows = sb("prm_rows", [NPRM, P])
        prm = sb("prm", [P, NPRM])
        b_root = sb("b_root", [P, 2 * L])
        floor_l = sb("floor_l", [P, L])
        ident = sb("ident", [P, P])
        ones = sb("ones", [P, P])
        mean_w = sb("mean_w", [P, P])
        iota_i = sb("iota_i", [P, P], I32)
        iota_f = sb("iota_f", [P, P])
        head_of = sb("head_of", [H, D])
        att_w = sb("att_w", [P, HALVES, H])
        spare = fwd_max.bitcast(BF16)
        onehot_lo = spare[:, 0:NC * P].rearrange("p (c n) -> p c n", c=NC)
        onehot_hi = spare[:, NC * P:NC * (P + NTILE)].rearrange("p (c n) -> p c n", c=NC)
        counts = sb("counts", [P, NTILE])
        dinv_n = sb("dinv_n", [P, NTILE])
        invdeg_n = sb("invdeg_n", [P, NTILE])
        small = sb("small", [P, 64])
        carry = ring_b[0:1, :, :].rearrange("p r d -> p (r d)").rearrange("p (i n) -> p i n", i=8)
        stats = sb("stats", [P, HALVES, 8, 6])
        mv = sb("mv", [P, HALVES, 2])
        eps = sb("eps", [P, 1])

        ps = [ctx.enter_context(nc.psum_tensor(f"ps{i}", [P, 512], F32)) for i in range(8)]

        def halves(bank, n):
            return ps[bank][:, 0:HALVES * n].rearrange("p (a n) -> p a n", a=HALVES)

        def of(n, slots=RING):
            return n + 1 + slots

        def reuse(n):
            return n + 1

        def bases(eng_type, k):
            return nc.values_load_multi_w_load_instructions(base_i[0:1, ds(k * NC, NC)], engines=(eng_type,),
                                                            min_val=0, max_val=N - 1)[1]

        def gathers(pool, table, width, idx_ready, arrived, layer):
            with pool.Fori(0, KT) as k:
                for g in range(NG):
                    for c in range(g * G, g * G + G):
                        if c == g * G:
                            wait_apart(pool, idx_ready, (layer * (KT + 1) + k) * NG + g + 1)
                        pool.indirect_dma_start(xg[:, c, 0:width], None, table,
                                                bass.IndirectOffsetOnAxis(ap=idx[:, c:c + 1], axis=0)
                                                ).then_inc(arrived[g], 16)

        def first_indices(idx_ready):
            for g in range(NG):
                nc.vector.tensor_copy(idx[:, g * G:g * G + G], src_idx[:, g * G:g * G + G]).then_inc(idx_ready, 1)

        def next_indices(k, g, idx_ready):
            nc.vector.tensor_copy(idx[:, g * G:g * G + G],
                                  src_idx[:, ds((k + 1) * NC + g * G, G)]).then_inc(idx_ready, 1)

        def wait_apart(eng, s, value):
            value = value if isinstance(value, int) else eng.to_reg(value)
            eng.wait_ge(consts, 1)
            eng.wait_ge(s, value)

        gw_in, gx_in = sem("gw_in"), [sem(f"gx_in{q}") for q in range(2)]
        gx_T, gx_copy, gt_mm, gt_row = [ring_sem(n, 2) for n in ("gx_T", "gx_copy", "gt_mm", "gt_row")]
        gt_out = [ring_sem(f"gt_out{q}", 48) for q in range(2)]

        aidx_ready, axg_in = sem("aidx_ready"), [sem(f"axg_in{g}") for g in range(NG)]
        axr_in = [sem(f"axr_in{c}") for c in range(NC)]
        aS_ready, aT_done, aST_ready, afifth, alk_ready, asc_done = [
            ring_sem(n) for n in ("aS_ready", "aT_done", "aST_ready", "afifth", "alk_ready", "asc_done")]
        gx_done = ring_sem("gx_done", NC)
        asc_copied = ring_sem("asc_copied", 2)
        hist_in, hist_mm, hist_added = sem("hist_in"), ring_sem("hist_mm", 1), ring_sem("hist_added", 1)

        sm_T, sm_copy, sm_ends, sm_rows, sm_carry, sm_cols, sm_diff, sm_ex, own_s = [
            sem(n) for n in ("sm_T", "sm_copy", "sm_ends", "sm_rows", "sm_carry", "sm_cols", "sm_diff", "sm_ex", "own_s")]
        deg_done, root_done, dinv_done, dinv_out = [sem(n) for n in ("deg_done", "root_done", "dinv_done", "dinv_out")]

        bidx_ready, bxg_in = sem("bidx_ready"), [sem(f"bxg_in{g}") for g in range(NG)]
        bat_in = [sem(f"bat_in{g}") for g in range(NG)]
        b_ready, b_mm, b_acc = [ring_sem(n) for n in ("b_ready", "b_mm", "b_acc")]
        bex_ready = sem("bex_ready")
        bat_T, bat_copy = ring_sem("bat_T", NG), ring_sem("bat_copy", 2)
        bat_out = [ring_sem(f"bat_out{i}", 16) for i in range(2)]

        bc_mm, bc_copy, rden_done, own_n = [sem(n) for n in ("bc_mm", "bc_copy", "rden_done", "own_n")]
        ln_den, ln_z, ln_mean, ln_d, ln_sq, ln_var, ln_sd = [
            sem(n) for n in ("ln_den", "ln_z", "ln_mean", "ln_d", "ln_sq", "ln_var", "ln_sd")]

        lw_in, lbias = sem("lw_in"), sem("lbias")
        lt_tile, lt_mm, lt_row, lr_mm, lr_relu = [
            ring_sem(n, 2) for n in ("lt_tile", "lt_mm", "lt_row", "lr_mm", "lr_relu")]
        lt_out = [ring_sem(f"lt_out{q}", 16) for q in range(2)]
        cidx_ready, cxg_in = sem("cidx_ready"), [sem(f"cxg_in{g}") for g in range(NG)]
        cat_in = [sem(f"cat_in{g}") for g in range(NG)]
        c_ee = ring_sem("c_ee", NC)
        c_sum, c_msg, c_mm, c_acc = [ring_sem(n) for n in ("c_sum", "c_msg", "c_mm", "c_acc")]
        own_bn, bn_var, bn_sd, bn_shift, bn_norm = [sem(n) for n in ("own_bn", "bn_var", "bn_sd", "bn_shift", "bn_norm")]

        f_tile, f_T, f_row = [ring_sem(n, 2) for n in ("f_tile", "f_T", "f_row")]
        f_out = [ring_sem(f"f_out{q}", 16) for q in range(2)]
        own_f, f_var, f_sd = sem("own_f"), sem("f_var"), sem("f_sd")

        rows_i = hT[:].rearrange("p a n -> p (a n)").bitcast(I32)
        rows_f = acc[:].rearrange("p a n -> p (a n)")
        SROW, DROW, WROW = 0, 512, 1024
        rows_in, rows_clear, chunk_in = sem("rows_in"), sem("rows_clear"), sem("chunk_in")
        consts, own_v, rows_T, base_b = sem("consts"), sem("own_v"), sem("rows_T"), sem("base_b")
        log_done, own_p = sem("log_done"), sem("own_p")
        iota_done, rows_float, base_done, scaled_w = sem("iota_done"), sem("rows_float"), sem("base_done"), sem("scaled_w")
        with nc.Block() as block:
            @block.sync
            def _(sp):
                sp.wait_ge(rows_clear, 2)
                for col, a, view in ((SROW, src, rows_i), (DROW, dst, rows_i), (WROW, edge_weight, rows_f)):
                    rows = view[0:RB, col:col + 512].rearrange("p (q e) -> p q e", q=4)
                    whole = a[0:3 * RB * P].rearrange("(q p e) -> p q e", p=RB, e=P)
                    sp.dma_start(rows[:, 0:3, :], whole).then_inc(rows_in, 16)
                    rest = a[3 * RB * P:FULL * P].rearrange("(p e) -> p e", e=P)
                    sp.dma_start(rows[0:RB - 1, 3, :], rest).then_inc(rows_in, 16)
                    last = a[FULL * P:E].rearrange("(a e) -> a e", a=1)
                    sp.dma_start(rows[RB - 1:RB, 3, 0:TAIL], last).then_inc(rows_in, 16)
                lh = "l (h p) -> (l h) p"
                for name, a in zip(PRM, (att.rearrange("(a h) c -> a (h c)", h=4),
                                         bias.rearrange("(a p) -> a p", p=P),
                                         b.rearrange(lh, p=P), be.rearrange(lh, p=P), root.rearrange(lh, p=P),
                                         gamma.rearrange(lh, p=P), beta.rearrange(lh, p=P))):
                    r = PCOL[name]
                    sp.dma_start(prm_rows[r:r + a.shape[0], :], a).then_inc(rows_in, 16)

            ROWS_IN = 16 * (9 + len(PRM))

            @block.scalar
            def _(act):
                act.wait_ge(rows_clear, 2)
                for h in range(H):
                    q = h * NC
                    act.dma_start(chunk_dst[q:q + NC - 1, 1:CH + 1],
                                  dst[0:(NC - 1) * CH].rearrange("(c x) -> c x", x=CH)).then_inc(chunk_in, 16)
                    act.dma_start(chunk_dst[q + NC - 1:q + NC, 1:1 + E - (NC - 1) * CH],
                                  dst[(NC - 1) * CH:E].rearrange("(a x) -> a x", a=1)).then_inc(chunk_in, 16)
                    act.dma_start(chunk_dst[q + 1:q + NC, 0:1],
                                  dst[0:(NC - 1) * CH].rearrange("(c x) -> c x", x=CH)[:, CH - 1:CH]
                                  ).then_inc(chunk_in, 16)
                    act.dma_start(chunk_dst[q:q + NC - 2, CH + 1:CH + 2],
                                  dst[CH:(NC - 1) * CH].rearrange("(c x) -> c x", x=CH)[:, 0:1]
                                  ).then_inc(chunk_in, 16)
                    act.dma_start(chunk_dst[q + NC - 2:q + NC - 1, CH + 1:CH + 2],
                                  dst[(NC - 1) * CH:(NC - 1) * CH + 1].rearrange("(a x) -> a x", a=1)
                                  ).then_inc(chunk_in, 16)
                act.wait_ge(scaled_w, 1)
                nc.scalar.activation(log_w[:], log_w[:], ACT.Ln).then_inc(log_done, 1)

            @block.gpsimd
            def _(pool):
                nc.gpsimd.iota(iota_i[:], pattern=[[1, P]], base=0, channel_multiplier=0).then_inc(iota_done, 1)
                nc.gpsimd.memset(ident[:], 0.0).then_inc(own_p, 1)
                nc.gpsimd.memset(head_of[:], 1.0).then_inc(own_p, 1)
                nc.gpsimd.memset(ones[:], 1.0)
                nc.gpsimd.memset(mean_w[:], 1.0 / D)
                nc.gpsimd.memset(eps[:], EPS)
                nc.gpsimd.memset(floor_l[:, 0:L - 1], 0.0)
                nc.gpsimd.memset(floor_l[:, L - 1:L], -3e38)
                pool.wait_ge(own_p, 2)
                nc.gpsimd.affine_select(out=ident[:], in_=ident[:], compare_op=ALU.not_equal, fill=1.0, base=0,
                                        pattern=[[-1, P]], channel_multiplier=1)
                nc.gpsimd.affine_select(out=head_of[:], in_=head_of[:], compare_op=ALU.is_ge, fill=0.0, base=0,
                                        pattern=[[1, D]], channel_multiplier=-C).then_inc(own_p, 1)
                pool.wait_ge(own_p, 3)
                nc.gpsimd.affine_select(out=head_of[:], in_=head_of[:], compare_op=ALU.is_ge, fill=0.0, base=C - 1,
                                        pattern=[[-1, D]], channel_multiplier=C).then_inc(consts, 1)

            @block.tensor
            def _(pe):
                pe.wait_ge(consts, 1)
                pe.wait_ge(rows_in, ROWS_IN)
                pe.wait_ge(rows_float, 1)
                for i, col in enumerate((SROW, DROW, WROW)):
                    for q in range(4):
                        nc.tensor.transpose(ps[i][:, q * RB:q * RB + RB],
                                            rows_f[0:RB, col + q * P:col + q * P + P], ident[0:RB, 0:RB])
                nc.tensor.transpose(ps[3][:, 0:NPRM], prm_rows[:], ident[0:NPRM, 0:NPRM])
                for a in range(HALVES):
                    last = nc.tensor.transpose(ps[3][:, 64 + a * H:64 + a * H + H], head_of[:, a * P:a * P + P],
                                               ident[0:H, 0:H])
                last.then_inc(rows_T, 1)
                pe.wait_ge(base_done, 1)
                nc.tensor.matmul(ps[4][:, 0:NT], ones[0:1, :], base_f[:], start=True, stop=True).then_inc(base_b, 1)
            @block.vector
            def _(dve):
                chain = [0]

                def link(ins):
                    chain[0] += 1
                    ins.then_inc(own_v, 1)
                    dve.wait_ge(own_v, chain[0])

                link(nc.vector.memset(rows_i[0:RB, SROW:SROW + 512], NTILE * P + P - 1))
                link(nc.vector.memset(rows_i[0:RB, DROW:DROW + 512], FAR))
                nc.vector.memset(rows_f[0:RB, WROW:WROW + 512], 1.0).then_inc(rows_clear, 1)
                nc.vector.memset(chunk_dst, -1).then_inc(rows_clear, 1)
                nc.vector.memset(ring_a[:], 0.0)
                dve.wait_ge(rows_in, ROWS_IN)
                nc.vector.tensor_copy(rows_f[0:RB, SROW:SROW + 512], rows_i[0:RB, SROW:SROW + 512])
                nc.vector.tensor_copy(rows_f[0:RB, DROW:DROW + 512],
                                      rows_i[0:RB, DROW:DROW + 512]).then_inc(rows_float, 1)
                dve.wait_ge(iota_done, 1)
                nc.vector.tensor_copy(iota_f[:], iota_i[:])

                def kc(t):
                    return t.rearrange("p (k c) -> p k c", c=NC)

                def from_ps(i, p=P):
                    return ps[i][0:p, 0:NT].rearrange("p (c k) -> p k c", c=NC)

                raw = rows_i[:, 2048:2048 + NT]
                hi_i = rows_i[:, 2560:2560 + NT]
                lo_i = rows_i[:, 3072:3072 + NT]
                tiny, zero = fwd_max[:, 0:NT], fwd_max[:, 512:512 + NT]
                lifted, weight = fwd_max[:, 1024:1024 + NT], fwd_max[:, 1536:1536 + NT]
                dve.wait_ge(rows_T, 1)
                nc.vector.tensor_copy(kc(dst_rel[:]), from_ps(1))
                link(nc.vector.tensor_copy(kc(base_f[:]), from_ps(1, 1)))
                nc.vector.tensor_copy(base_i[:], base_f[:]).then_inc(base_done, 1)
                nc.vector.tensor_scalar(kc(src_idx[:, 0:NT]), from_ps(0), float(N - 1), None, ALU.min)
                nc.vector.memset(src_idx[:, NT:NT + NC], 0)
                link(nc.vector.tensor_copy(kc(raw), from_ps(0)))
                link(nc.vector.tensor_scalar(hi_i, raw, 7, None, ALU.arith_shift_right))
                link(nc.vector.tensor_scalar(lo_i, raw, P - 1, None, ALU.bitwise_and))
                nc.vector.tensor_copy(src_hi[:], hi_i)
                nc.vector.tensor_copy(src_lo[:], lo_i)
                link(nc.vector.tensor_copy(kc(weight), from_ps(2)))
                link(nc.vector.tensor_scalar(tiny, weight, 2.0 ** -64, None, ALU.is_lt))
                link(nc.vector.tensor_scalar(zero, weight, 0.0, NO_EDGE, ALU.is_equal, ALU.mult))
                link(nc.vector.scalar_tensor_tensor(lifted, tiny, 2.0 ** 96, weight, ALU.mult, ALU.mult))
                link(nc.vector.scalar_tensor_tensor(log_w[:], tiny, 0.0, weight, ALU.is_equal, ALU.mult))
                link(nc.vector.tensor_tensor(log_w[:], log_w[:], lifted, ALU.add))
                nc.vector.tensor_scalar(log_w[:], log_w[:], 2.0 ** -64, None, ALU.max).then_inc(scaled_w, 1)
                dve.wait_ge(base_b, 1)
                link(nc.vector.tensor_tensor(dst_rel[:], dst_rel[:], ps[4][:, 0:NT], ALU.subtract))
                link(nc.vector.tensor_copy(prm[:], ps[3][:, 0:NPRM]))
                for a in range(HALVES):
                    nc.vector.tensor_scalar(att_w[:, a, :], ps[3][:, 64 + a * H:64 + a * H + H],
                                            prm[:, a:a + 1], None, ALU.mult)
                nc.vector.tensor_tensor(b_root[:], prm[:, PCOL["b"]:PCOL["b"] + 2 * L],
                                        prm[:, PCOL["root"]:PCOL["root"] + 2 * L], ALU.add)
                dve.wait_ge(log_done, 1)
                link(nc.vector.scalar_tensor_tensor(log_w[:], tiny, -LN2_96, log_w[:], ALU.mult, ALU.add))
                link(nc.vector.tensor_tensor(log_w[:], log_w[:], zero, ALU.add))
                dve.wait_ge(chunk_in, 16 * 5 * H)
                link(nc.vector.tensor_tensor(breaks, chunk_dst[:, 1:CH + 2], chunk_dst[:, 0:CH + 1], ALU.not_equal))
                link(nc.vector.tensor_scalar(breaks, breaks, RESET, None, ALU.mult))
                link(nc.vector.memset(counts[:], 0.0))

            @block.sync
            def _(sp):
                for s, slots in primed:
                    sp.sem_inc(s, slots)

        with nc.Block() as block:
            @block.sync
            def _(sp):
                for w, a in ((wA, W_l), (wB, W_r)):
                    sp.dma_start(w[:], a.rearrange("(h p) n -> p h n", p=P)).then_inc(gw_in, 16)
                for i, a in enumerate((b_l, b_r)):
                    sp.dma_start(rowbias[:, i, :],
                                 a.rearrange("(a n) -> a n", a=1).to_broadcast([P, D])).then_inc(gw_in, 16)

                def store(j, q):
                    sp.wait_ge(gt_row, of(2 * j + q, 2))
                    rows = ds((2 * j + q) * P, P)
                    sp.dma_start(xl_table[rows, 0:D], stage[:, q, 0:D]).then_inc(gt_out[q], 16)
                    sp.dma_start(x_l_rows[rows, :], stage[:, q, 0:D]).then_inc(gt_out[q], 16)
                    sp.dma_start(xr_table[rows, :], stage[:, q, D:2 * D]).then_inc(gt_out[q], 16)

                with sp.Fori(0, JT) as j:
                    for q in range(2):
                        store(j, q)
                for q in range(2):
                    sp.wait_ge(gt_out[q], 48 * (JT + 1))

            @block.gpsimd
            def _(pool):
                def load(j, q, rows=P):
                    pool.wait_ge(gx_T, reuse(2 * j + q))
                    pool.dma_start(ring_a[0:rows, q, :], x[ds((2 * j + q) * P, rows), :]).then_inc(gx_in[q], 16)

                with pool.Fori(0, JT - 1) as j:
                    for q in range(2):
                        load(j, q)
                load(JT - 1, 0, N - N // P * P)
                nc.gpsimd.memset(acc[:], 0.0)

            @block.tensor
            def _(pe):
                pe.wait_ge(gw_in, 64)

                def turn(j, q):
                    pe.wait_ge(gx_in[q], 16 * (j + 1))
                    for a in range(HALVES):
                        last = nc.tensor.transpose(ps[q][:, a * P:a * P + P], ring_a[:, q, a * P:a * P + P], ident[:])
                    last.then_inc(gx_T, 1)

                def products(j, q):
                    pe.wait_ge(gx_copy, of(2 * j + q, 2))
                    pe.wait_ge(gt_row, reuse(2 * j + q))
                    for i, w in enumerate((wA, wB)):
                        for a in range(HALVES):
                            last = nc.tensor.matmul(ps[2 + q][:, i * D:i * D + D], tiles[:, q, a, :], w[:, a, :],
                                                    start=(a == 0), stop=(a == HALVES - 1))
                    last.then_inc(gt_mm, 1)

                turn(0, 0)
                with pe.Fori(0, JT - 1) as j:
                    turn(j, 1)
                    products(j, 0)
                    turn(j + 1, 0)
                    products(j, 1)
                products(JT - 1, 0)
                products(JT - 1, 1)

            @block.scalar
            def _(act):
                def copies(j, q):
                    act.wait_ge(gx_T, of(2 * j + q, 2))
                    act.wait_ge(gt_mm, reuse(2 * j + q))
                    nc.scalar.copy(tiles[:, q, :, :], ps[q][:, 0:D].rearrange("p (a n) -> p a n", a=HALVES))
                    nc.scalar.copy(hT[:, :, ds((2 * j + q) * P, P)],
                                   ps[q][:, 0:D].rearrange("p (a n) -> p a n", a=HALVES)).then_inc(gx_copy, 1)

                with act.Fori(0, JT - 1) as j:
                    copies(j, 0)
                    copies(j, 1)
                copies(JT - 1, 0)
                act.wait_ge(gt_mm, reuse(2 * JT - 1))
                nc.scalar.memzero(hT[:, :, (NTILE - 1) * P:NTILE * P])
                nc.scalar.memzero(tiles[:, 1, :, :]).then_inc(gx_copy, 1)

            @block.vector
            def _(dve):
                dve.wait_ge(gw_in, 64)
                both = rowbias[:].rearrange("p i d -> p (i d)")
                with dve.Fori(0, JT) as j:
                    for q in range(2):
                        dve.wait_ge(gt_mm, of(2 * j + q, 2))
                        dve.wait_ge(gt_out[q], 48 * (j + 1))
                        nc.vector.tensor_tensor(stage[:, q, :], ps[2 + q][:], both, ALU.add).then_inc(gt_row, 1)

        acc_flat = acc[:].rearrange("p a n -> p (a n)")
        xr_ring = acc_flat[:, 0:NC * D].rearrange("p (s d) -> p s d", s=NC)
        S_a = scoresT[:, 0:S_RING * P].rearrange("p (s n) -> p s n", s=S_RING)
        ST_a = scoresT[:, S_RING * P:2 * S_RING * P].rearrange("p (s n) -> p s n", s=S_RING)
        with nc.Block() as block:
            @block.gpsimd
            def _(pool):
                gathers(pool, x_l_rows, D, aidx_ready, axg_in, 0)

            @block.sync
            def _(sp):
                with sp.Fori(0, KT) as k:
                    base = bases(SP, k)
                    for c in range(NC):
                        sp.wait_ge(gx_done, reuse(k * NC + c))
                        sp.dma_start(xr_ring[:, c, :], xr_table[ds(base[c], P), :]).then_inc(axr_in[c], 16)

            @block.tensor
            def _(pe):
                def turn(k, c):
                    n = k * NC + c
                    pe.wait_ge(aS_ready, of(n))
                    pe.wait_ge(aST_ready, of(n - 2))
                    nc.tensor.transpose(ps[c % 2][:, 0:P], S_a[:, c % S_RING, :], ident[:]).then_inc(aT_done, 1)

                def sums(k, c):
                    n = k * NC + c
                    pe.wait_ge(aST_ready, of(n))
                    pe.wait_ge(axr_in[c], 16 * (k + 1))
                    pe.wait_ge(axg_in[c // G], 16 * G * (k + 1))
                    o = ps[2 + c % RING]
                    for a in range(HALVES):
                        nc.tensor.matmul(o[:, a * P:a * P + P], xg[:, c, a * P:a * P + P], ident[:],
                                         start=True, stop=False, is_transpose=True)
                        last = nc.tensor.matmul(o[:, a * P:a * P + P], xr_ring[:, c, a * P:a * P + P],
                                                ST_a[:, c % S_RING, :], start=False, stop=True)
                    last.then_inc(gx_done, 1)

                def score(k, c):
                    pe.wait_ge(alk_ready, of(k * NC + c))
                    if c % 8 == 0:
                        pe.wait_ge(asc_copied, reuse(2 * k + c // 8))
                    if c == 0:
                        pe.wait_ge(hist_added, k + 1)
                    for a in range(HALVES):
                        last = nc.tensor.matmul(ps[6 + c // 8][:, c * H:c * H + H],
                                                ring_a[:, c % RING, a * P:a * P + P], att_w[:, a, :],
                                                start=(a == 0), stop=(a == HALVES - 1))
                    last.then_inc(asc_done, 1)

                def histogram(k, c):
                    if c == 12:
                        pe.wait_ge(hist_in, k + 1)
                        for i in range(NC):
                            last = nc.tensor.matmul(ps[6][:, 256:256 + NTILE], onehot_lo[:, i, :], onehot_hi[:, i, :],
                                                    start=(i == 0), stop=(i == NC - 1))
                        last.then_inc(hist_mm, 1)

                pipelined(pe, [(5, turn), (3, sums), (0, score), (0, histogram)])

            @block.scalar
            def _(act):
                def onehot_T(k, c):
                    act.wait_ge(aT_done, of(k * NC + c))
                    nc.scalar.copy(ST_a[:, c % S_RING, :],
                                   ps[c % 2][:, 0:P]).then_inc(aST_ready, 1)

                def fifth(k, c):
                    act.wait_ge(gx_done, of(k * NC + c, NC))
                    nc.scalar.mul(fifths[:, c % RING, :], ps[2 + c % RING][:, 0:D], 0.2).then_inc(afifth, 1)

                pipelined(act, [(5, onehot_T), (2, fifth)])

            @block.vector
            def _(dve):
                def onehot(k, c):
                    dve.wait_ge(gx_done, of(k * NC + c - S_RING, NC))
                    nc.vector.tensor_scalar(S_a[:, c % S_RING, :], iota_f[:], dst_rel[:, ds(k * NC + c, 1)], None,
                                            ALU.is_equal).then_inc(aS_ready, 1)

                def leaky(k, c):
                    dve.wait_ge(afifth, of(k * NC + c))
                    nc.vector.tensor_tensor(ring_a[:, c % RING, :], ps[2 + c % RING][:, 0:D],
                                            fifths[:, c % RING, :], ALU.max).then_inc(alk_ready, 1)

                def refill(k, c):
                    if c % G == G - 1:
                        next_indices(k, c // G, aidx_ready)

                def keep_scores(k, c):
                    if c % 8 == 7:
                        n, first, cols = k * NC + c, c - 7, ds(k * NC + c - 7, 8)
                        dve.wait_ge(asc_done, of(n))
                        to = scores[:, ds(k * P, P)].rearrange("p (h c) -> p h c", h=H)[:, :, first:first + 8]
                        got = ps[6 + c // 8][:, first * H:first * H + 8 * H].rearrange("p (c h) -> p h c", h=H)
                        nc.vector.tensor_tensor(to, got, log_w[:, cols].unsqueeze(1).to_broadcast([P, H, 8]),
                                                ALU.add).then_inc(asc_copied, 1)

                def histogram(k, c):
                    if c == 4:
                        dve.wait_ge(hist_mm, k + 1)
                        for to, part, wd in ((onehot_lo, src_lo, P), (onehot_hi, src_hi, NTILE)):
                            last = nc.vector.tensor_tensor(
                                to, part[:, ds(k * NC, NC)].unsqueeze(2).to_broadcast([P, NC, wd]),
                                iota_f[:, 0:wd].unsqueeze(1).to_broadcast([P, NC, wd]), ALU.is_equal)
                        last.then_inc(hist_in, 1)
                    if c == 15:
                        dve.wait_ge(hist_mm, k + 2)
                        nc.vector.tensor_tensor(counts[:], counts[:], ps[6][:, 256:256 + NTILE],
                                                ALU.add).then_inc(hist_added, 1)

                first_indices(aidx_ready)
                pipelined(dve, [(7, onehot), (1, leaky), (1, refill), (0, keep_scores), (0, histogram)])

        def chunk_group(g):
            return slice(g * 4 * P, min((g + 1) * 4, KT) * P)

        CG = -(-KT // 4)
        with nc.Block() as block:
            @block.tensor
            def _(pe):
                def turn(source, g, first):
                    if g + first >= 2:
                        pe.wait_ge(sm_copy, g + first - 1)
                    for k in range(4 * g, min(4 * g + 4, KT)):
                        last = nc.tensor.transpose(ps[(g + first) % 2][:, k % 4 * P:k % 4 * P + P],
                                                   source[:, k * P:k * P + P], ident[:])
                    last.then_inc(sm_T, 1)

                for g in range(CG):
                    turn(scores, g, 0)
                pe.wait_ge(sm_ends, 1)
                for i in range(4):
                    last = nc.tensor.transpose(ps[2][0:1, i * P:i * P + P], small[:, i:i + 1], ident[:])
                last.then_inc(sm_rows, 1)
                pe.wait_ge(sm_carry, 1)
                for i in range(2):
                    last = nc.tensor.transpose(ps[3][:, i:i + 1], carry[:, 6 + i, :], ident[0:1, 0:1])
                last.then_inc(sm_cols, 1)
                pe.wait_ge(sm_ex, 1)
                for g in range(CG):
                    turn(scoresT, g, CG)

            @block.scalar
            def _(act):
                act.wait_ge(deg_done, 1)
                nc.scalar.activation(dinv_n[:], invdeg_n[:], ACT.Sqrt).then_inc(root_done, 1)
                act.wait_ge(sm_diff, 1)
                nc.scalar.activation(scoresT, scoresT, ACT.Exp).then_inc(sm_ex, 1)

            @block.gpsimd
            def _(pool):
                nc.gpsimd.memset(acc[:], 0.0)
                nc.gpsimd.memset(den, 0.0)

            @block.vector
            def _(dve):
                chain = [0]

                def link(ins):
                    chain[0] += 1
                    ins.then_inc(own_s, 1)
                    dve.wait_ge(own_s, chain[0])

                degree, t = small[:, 8:8 + NTILE], small[:, 36:36 + NTILE]
                link(nc.vector.tensor_scalar(degree, counts[:], 1.0, None, ALU.add))
                nc.vector.reciprocal(invdeg_n[:], degree).then_inc(deg_done, 1)
                dve.wait_ge(root_done, 1)
                link(nc.vector.tensor_tensor(t, dinv_n[:], dinv_n[:], ALU.mult))
                link(nc.vector.tensor_tensor(t, t, degree, ALU.mult))
                link(nc.vector.tensor_scalar(t, t, -0.5, 1.5, ALU.mult, ALU.add))
                nc.vector.tensor_tensor(dinv_n[:], dinv_n[:], t, ALU.mult).then_inc(dinv_done, 1)

                for g in range(CG):
                    dve.wait_ge(sm_T, g + 1)
                    cols = chunk_group(g)
                    nc.vector.tensor_copy(scoresT[:, cols], ps[g % 2][:, 0:cols.stop - cols.start]).then_inc(sm_copy, 1)
                dve.wait_ge(sm_copy, CG)

                def scans(first_f, first_b):
                    nc.vector.tensor_tensor_scan(out=fwd_max, data0=breaks[:, 0:CH], data1=scoresT,
                                                 initial=first_f, op0=ALU.add, op1=ALU.max)
                    link(nc.vector.tensor_tensor_scan(out=bwd_max[:, ::-1], data0=breaks[:, 1:CH + 1][:, ::-1],
                                                      data1=scoresT[:, ::-1], initial=first_b,
                                                      op0=ALU.add, op1=ALU.max))

                scans(RESET, RESET)
                nc.vector.tensor_copy(small[:, 0:1], fwd_max[:, CH - 1:CH])
                nc.vector.tensor_copy(small[:, 1:2], bwd_max[:, 0:1])
                nc.vector.tensor_reduce(small[:, 2:3], breaks[:, 0:CH], mybir.AxisListType.X, ALU.min)
                nc.vector.tensor_reduce(small[:, 3:4], breaks[:, 1:CH + 1], mybir.AxisListType.X,
                                        ALU.min).then_inc(sm_ends, 1)
                dve.wait_ge(sm_rows, 1)
                link(nc.vector.tensor_copy(carry[:, 0:4, :], ps[2][0:1, :].rearrange("p (i n) -> p i n", i=4)))
                nc.vector.memset(carry[:, 6, 0:1], RESET)
                link(nc.vector.memset(carry[:, 7, P - 1:P], RESET))
                link(nc.vector.tensor_tensor_scan(out=carry[:, 4, :], data0=carry[:, 2, :], data1=carry[:, 0, :],
                                                  initial=RESET, op0=ALU.add, op1=ALU.max))
                link(nc.vector.tensor_tensor_scan(out=carry[:, 5, ::-1], data0=carry[:, 3, ::-1],
                                                  data1=carry[:, 1, ::-1], initial=RESET, op0=ALU.add, op1=ALU.max))
                nc.vector.tensor_copy(carry[:, 6, 1:P], carry[:, 4, 0:P - 1])
                nc.vector.tensor_copy(carry[:, 7, 0:P - 1], carry[:, 5, 1:P]).then_inc(sm_carry, 1)
                dve.wait_ge(sm_cols, 1)
                link(nc.vector.tensor_copy(small[:, 4:6], ps[3][:, 0:2]))
                scans(small[:, 4:5], small[:, 5:6])
                link(nc.vector.tensor_tensor(fwd_max, fwd_max, bwd_max, ALU.max))
                nc.vector.tensor_tensor(scoresT, scoresT, fwd_max, ALU.subtract).then_inc(sm_diff, 1)
                for g in range(CG):
                    dve.wait_ge(sm_T, CG + g + 1)
                    cols = chunk_group(g)
                    nc.vector.tensor_copy(scores[:, cols],
                                          ps[(g + CG) % 2][:, 0:cols.stop - cols.start]).then_inc(sm_copy, 1)

            @block.sync
            def _(sp):
                sp.wait_ge(dinv_done, 1)
                sp.dma_start(xl_table[:, D:GW].rearrange("(i p) w -> p i w", p=P),
                             dinv_n[:].unsqueeze(2)).then_inc(dinv_out, 16)
                sp.wait_ge(dinv_out, 16)

        with nc.Block() as block:
            @block.gpsimd
            def _(pool):
                gathers(pool, xl_table, GW, bidx_ready, bxg_in, 0)

            @block.sync
            def _(sp):
                by_chunk = edge_attr[0:(NC - 1) * CH, :].rearrange("(c k p) f -> k p c f", k=KT, p=P)

                def loads(k, last):
                    for g in range(NG):
                        sp.wait_ge(bat_T, reuse(k * NG + g))
                        whole = G if g < NG - 1 else G - 1
                        sp.dma_start(attr_in[:, g, 0:whole, :],
                                     by_chunk[ds(k, 1), :, g * G:g * G + whole, :].rearrange("k p c f -> (k p) c f")
                                     ).then_inc(bat_in[g], 16)
                    rows = TAIL if last else P
                    sp.dma_start(attr_in[0:rows, NG - 1, G - 1, :],
                                 edge_attr[ds(((NC - 1) * KT + k) * P, rows), :]).then_inc(bat_in[NG - 1], 16)

                with sp.Fori(0, KT - 1) as k:
                    loads(k, False)
                loads(KT - 1, True)

            @block.tensor
            def _(pe):
                def turn(k, c):
                    if c % G == 1:
                        g = c // G
                        pe.wait_ge(bat_in[g], (32 if g == NG - 1 else 16) * (k + 1))
                        pe.wait_ge(bat_copy, reuse(k * NG + g))
                        for j in range(G):
                            last = nc.tensor.transpose(ps[RING + g % 2][:, j * P:j * P + P], attr_in[:, g, j, :], ident[:])
                        last.then_inc(bat_T, 1)

                def product(k, c):
                    n = k * NC + c
                    pe.wait_ge(b_ready, of(n))
                    pe.wait_ge(b_acc, reuse(n))
                    o = ps[c % RING]
                    for a in range(HALVES):
                        nc.tensor.matmul(o[:, a * P:a * P + P], ring_a[:, c % RING, a * P:a * P + P],
                                         S[:, c % RING, :], start=True, stop=True)
                    nc.tensor.matmul(ps[c % RING][0:H, D:D + P], ex_g[:, c // G, :, c % G],
                                     S[:, c % RING, :], start=True, stop=True).then_inc(b_mm, 1)

                pipelined(pe, [(0, turn), (0, product)])

            @block.scalar
            def _(act):
                def keep(k, c):
                    if c % G == 1:
                        g = c // G
                        n = k * NG + g
                        act.wait_ge(bat_T, of(n, NG))
                        act.wait_ge(bat_out[g % 2], 16 * (2 * k + g // 2 + 1))
                        nc.scalar.copy(attr_out[:, g % 2, :], ps[RING + g % 2][:]).then_inc(bat_copy, 1)
                        act.wait_ge(bat_copy, of(n, 2))
                        act.dma_start(attr_T[ds(k * NG + g, 1), :, :].rearrange("k p e -> (k p) e"),
                                      attr_out[:, g % 2, :]).then_inc(bat_out[g % 2], 16)

                pipelined(act, [(0, keep)])
                for i in range(2):
                    act.wait_ge(bat_out[i], 16 * (2 * KT + 1))

            @block.vector
            def _(dve):
                def weigh(k, c):
                    n, g = k * NC + c, c // G
                    wait_apart(dve, b_mm, reuse(n))
                    if c % G == 0:
                        nc.vector.tensor_copy(
                            ex_g[:, g, :, :],
                            scores[:, ds(k * P, P)].rearrange("p (h c) -> p h c", h=H)[:, :, c:c + G]
                        ).then_inc(bex_ready, 1)
                        dve.wait_ge(bxg_in[g], 16 * G * (k + 1))
                        dve.wait_ge(bex_ready, k * NG + g + 1)
                    nc.vector.tensor_scalar(S[:, c % RING, :], iota_f[:], dst_rel[:, ds(k * NC + c, 1)], None, ALU.is_equal)
                    nc.vector.tensor_tensor(ring_a[:, c % RING, :].rearrange("p (h d) -> p h d", h=H),
                                            xg[:, c, 0:D].rearrange("p (h d) -> p h d", h=H),
                                            ex_g[:, g, :, c % G].unsqueeze(2).to_broadcast([P, H, C]),
                                            ALU.mult).then_inc(b_ready, 1)
                    if c % G == G - 1:
                        nc.vector.tensor_copy(dinv_src[:, ds(k * NC + g * G, G)].unsqueeze(2),
                                              xg[:, g * G:g * G + G, D:GW])
                        next_indices(k, g, bidx_ready)

                def add(k, c):
                    n = k * NC + c
                    dve.wait_ge(b_mm, of(n))
                    dve.wait_ge(b_acc, of(n - 1))
                    to = acc[:, :, ds(base_of[c], P)]
                    nc.vector.tensor_tensor(to, to, halves(c % RING, P),
                                            ALU.add)
                    to = den[:, ds(base_of[c], P)]
                    nc.vector.tensor_tensor(to, to, ps[c % RING][0:H, D:D + P],
                                            ALU.add).then_inc(b_acc, 1)

                base_of = [None] * NC

                def load_bases(k, c):
                    if c == 0:
                        base_of[:] = bases(DVE, k)

                first_indices(bidx_ready)
                pipelined(dve, [(2, weigh), (0, load_bases), (0, add)])

        with nc.Block() as block:
            @block.tensor
            def _(pe):
                pe.wait_ge(rden_done, 1)
                with pe.Fori(0, JT) as j:
                    cols = ds(j * JC, JC)
                    for a in range(HALVES):
                        last = nc.tensor.matmul(ps[0][:, a * JC:a * JC + JC], head_of[:, a * P:a * P + P],
                                                den[:, cols], start=True, stop=True)
                    last.then_inc(ln_den, 1)
                    pe.wait_ge(ln_z, j + 1)
                    for a in range(HALVES):
                        last = nc.tensor.matmul(ps[1][:, 0:JC], mean_w[:], acc[:, a, cols],
                                                start=(a == 0), stop=(a == HALVES - 1))
                    last.then_inc(ln_mean, 1)
                    pe.wait_ge(ln_sq, j + 1)
                    for a in range(HALVES):
                        last = nc.tensor.matmul(ps[2][:, 0:JC], mean_w[:], ring_a[:, a, :],
                                                start=(a == 0), stop=(a == HALVES - 1))
                    last.then_inc(ln_var, 1)
                n = 0
                for what in (dinv_n, invdeg_n):
                    for g in range(CG):
                        if n >= 2:
                            pe.wait_ge(bc_copy, n - 1)
                        for i in range(4 * g, min(4 * g + 4, NTILE)):
                            last = nc.tensor.matmul(ps[3 + n % 2][:, i % 4 * P:i % 4 * P + P],
                                                    what[:, i:i + 1].to_broadcast([P, P]), ident[:],
                                                    start=True, stop=True)
                        last.then_inc(bc_mm, 1)
                        n += 1

            @block.scalar
            def _(act):
                with act.Fori(0, JT) as j:
                    wait_apart(act, ln_d, j + 1)
                    nc.scalar.activation(ring_a[:, 0:HALVES, :], x1T[:, :, ds(j * JC, JC)], ACT.Square).then_inc(ln_sq, 1)
                    act.wait_ge(ln_var, j + 1)
                    nc.scalar.activation(ring_b[:, 0, :], ps[2][:, 0:JC], ACT.Sqrt, bias=eps[:]).then_inc(ln_sd, 1)

            @block.vector
            def _(dve):
                nc.vector.tensor_scalar(den, den, 1e-16, None, ALU.add).then_inc(own_n, 1)
                dve.wait_ge(own_n, 1)
                nc.vector.reciprocal(den, den).then_inc(rden_done, 1)
                OWN = 4
                with dve.Fori(0, JT) as j:
                    cols = ds(j * JC, JC)
                    z, d = acc[:, :, cols], x1T[:, :, cols]
                    dve.wait_ge(ln_den, j + 1)
                    nc.vector.tensor_tensor(z, z, ps[0][:].rearrange("p (a n) -> p a n", a=HALVES),
                                            ALU.mult).then_inc(own_n, 1)
                    dve.wait_ge(own_n, OWN * j + 2)
                    for a in range(HALVES):
                        col = PCOL["bias"] + a
                        last = nc.vector.scalar_tensor_tensor(acc[:, a, cols], acc[:, a, cols], prm[:, col:col + 1],
                                                              hT[:, a, cols], ALU.add, ALU.add)
                    last.then_inc(ln_z, 1)
                    dve.wait_ge(ln_mean, j + 1)
                    nc.vector.tensor_tensor(d, z, ps[1][:, 0:JC].unsqueeze(1).to_broadcast([P, HALVES, JC]),
                                            ALU.subtract).then_inc(ln_d, 1)
                    dve.wait_ge(ln_sd, j + 1)
                    nc.vector.reciprocal(ring_b[:, 1, :], ring_b[:, 0, :]).then_inc(own_n, 1)
                    dve.wait_ge(own_n, OWN * j + 3)
                    nc.vector.tensor_tensor(d, d, ring_b[:, 1, :].unsqueeze(1).to_broadcast([P, HALVES, JC]),
                                            ALU.mult).then_inc(own_n, 1)
                    wait_apart(dve, own_n, OWN * j + 4)
                    nc.vector.tensor_copy(hT[:, :, cols], d).then_inc(own_n, 1)
                n = 0
                for to in (dinv_b, invdeg_b):
                    for g in range(CG):
                        dve.wait_ge(bc_mm, n + 1)
                        cols = chunk_group(g)
                        nc.vector.tensor_copy(to[:, cols], ps[3 + n % 2][:, 0:cols.stop - cols.start]).then_inc(bc_copy, 1)
                        n += 1

        BN_LINKS = 6 * HALVES
        with nc.Fori(0, L) as l:
            with nc.Block() as block:
                @block.sync
                def _(sp):
                    sp.dma_start(wA[:], W[ds(l, 1), :, :].rearrange("l (h p) n -> p (l h) n", p=P)).then_inc(lw_in, 16)
                    sp.dma_start(wB[:, 0, :], We[ds(l, 1), :, :].rearrange("l p n -> (l p) n")).then_inc(lw_in, 16)
                    for i, v in enumerate((b, be)):
                        sp.dma_start(rowbias[:, i, :], v[ds(l, 1), :].to_broadcast([P, D])).then_inc(lw_in, 16)
                    with sp.Fori(0, JT) as j:
                        for q in range(2):
                            n = 2 * (l * JT + j) + q
                            sp.wait_ge(lt_row, of(n, 2))
                            sp.dma_start(gcn_table[ds((2 * j + q) * P, P), :], stage[:, q, 0:D]).then_inc(lt_out[q], 16)
                    with sp.Fori(0, KT) as k:
                        for g in range(NG):
                            n = (l * KT + k) * NG + g
                            sp.wait_ge(c_ee, G * n + G)
                            sp.dma_start(attr_in[:, g, :, :].rearrange("p j e -> p (j e)"),
                                         attr_T[ds(k * NG + g, 1), :, :].rearrange("k p e -> (k p) e")
                                         ).then_inc(cat_in[g], 16)

                @block.gpsimd
                def _(pool):
                    with pool.Fori(0, JT) as j:
                        for q in range(2):
                            n = 2 * (l * JT + j) + q
                            wait_apart(pool, lt_mm, reuse(n))
                            nc.gpsimd.tensor_copy(tiles[:, q, :, :], hT[:, :, ds((2 * j + q) * P, P)]).then_inc(lt_tile, 1)
                    gathers(pool, gcn_table, D, cidx_ready, cxg_in, l)

                @block.tensor
                def _(pe):
                    pe.wait_ge(lw_in, 64 * (l + 1))
                    nc.tensor.transpose(ps[7][0:1, 0:P], ident[:, 0:1], ident[:])
                    with pe.Fori(0, JT) as j:
                        for q in range(2):
                            n = 2 * (l * JT + j) + q
                            pe.wait_ge(lt_tile, of(n, 2))
                            pe.wait_ge(lt_row, reuse(n))
                            for a in range(HALVES):
                                last = nc.tensor.matmul(ps[q][:, 0:D], tiles[:, q, a, :], wA[:, a, :],
                                                        start=(a == 0), stop=(a == HALVES - 1))
                            last.then_inc(lt_mm, 1)
                        for o in range(HALVES):
                            n = 2 * (l * JT + j) + o
                            pe.wait_ge(lr_relu, reuse(n))
                            for a in range(HALVES):
                                last = nc.tensor.matmul(ps[2 + o][:, 0:JC], wA[:, a, o * P:o * P + P],
                                                        hT[:, a, ds(j * JC, JC)],
                                                        start=(a == 0), stop=(a == HALVES - 1))
                            last.then_inc(lr_mm, 1)

                    def edge_term(k, c):
                        n = (l * KT + k) * NC + c
                        pe.wait_ge(cat_in[c // G], 16 * ((l) * KT + k + 1))
                        nc.tensor.matmul(ps[c % RING][:, 0:D], attr_in[:, c // G, c % G, :], wB[:, 0, :],
                                         start=True, stop=True).then_inc(c_ee, 1)

                    def sums(k, c):
                        n = (l * KT + k) * NC + c
                        pe.wait_ge(c_msg, of(n))
                        pe.wait_ge(c_acc, reuse(n))
                        o = ps[RING + c % RING]
                        for a in range(HALVES):
                            last = nc.tensor.matmul(o[:, a * P:a * P + P], ring_b[:, c % RING, a * P:a * P + P],
                                                    S[:, c % RING, :], start=True, stop=True)
                        last.then_inc(c_mm, 1)

                    for o in range(HALVES):
                        pe.wait_ge(lt_row, of(2 * (l * JT + JT - 1) + o, 2))
                        pe.wait_ge(lr_relu, of(2 * (l * JT + JT - 1) + o, 2))
                    pipelined(pe, [(3, edge_term), (0, sums)])

                @block.scalar
                def _(act):
                    with act.Fori(0, JT) as j:
                        for o in range(HALVES):
                            wait_apart(act, lr_mm, of(2 * (l * JT + j) + o, 2))
                            nc.scalar.activation(conv0[:, o, ds(j * JC, JC)], ps[2 + o][:, 0:JC], ACT.Relu,
                                                 bias=b_root[:, ds(2 * l + o, 1)]).then_inc(lr_relu, 1)

                    def message(k, c):
                        wait_apart(act, c_sum, of((l * KT + k) * NC + c))
                        nc.scalar.activation(ring_b[:, c % RING, :], ring_a[:, c % RING, :], ACT.Relu,
                                             scale=dinv_src[:, ds(k * NC + c, 1)]).then_inc(c_msg, 1)

                    pipelined(act, [(0, message)])
                    for a in range(HALVES):
                        act.wait_ge(bn_var, HALVES * l + a + 1)
                        nc.scalar.activation(small[:, 4 * a:4 * a + 1], mv[:, a, 1:2], ACT.Sqrt,
                                             bias=eps[:]).then_inc(bn_sd, 1)
                        act.wait_ge(bn_shift, HALVES * l + a + 1)
                        nc.scalar.activation(acc[:, a, 0:N], acc[:, a, 0:N], ACT.Identity,
                                             scale=small[:, 4 * a + 2:4 * a + 3],
                                             bias=small[:, 4 * a + 3:4 * a + 4]).then_inc(bn_norm, 1)

                @block.vector
                def _(dve):
                    nc.vector.memset(acc[:], 0.0)
                    dve.wait_ge(lw_in, 64 * (l + 1))
                    nc.vector.tensor_tensor(rowbias[:, 0, :], rowbias[:, 0, :], rowbias[:, 1, :], ALU.add).then_inc(lbias, 1)
                    dve.wait_ge(lbias, l + 1)
                    nc.vector.memset(small[:, 62:63], 0.0)
                    with dve.Fori(0, JT) as j:
                        for q in range(2):
                            n = 2 * (l * JT + j) + q
                            dve.wait_ge(lt_mm, of(n, 2))
                            dve.wait_ge(lt_out[q], 16 * (l * JT + j + 1))
                            nc.vector.tensor_tensor(stage[:, q, 0:D], ps[q][:, 0:D], rowbias[:, 0, :],
                                                    ALU.add).then_inc(lt_row, 1)
                        dve.wait_ge(lr_relu, of(2 * (l * JT + j) + 1, 2))
                        root_term = conv0[:, :, ds(j * JC, JC)]
                        nc.vector.tensor_tensor(root_term, root_term,
                                                invdeg_b[:, ds(j * JC, JC)].unsqueeze(1).to_broadcast([P, HALVES, JC]),
                                                ALU.mult)
                    for q in range(2):
                        dve.wait_ge(lt_out[q], 16 * (JT * (l + 1) + 1))

                    def add_rows(k, c):
                        n, g = (l * KT + k) * NC + c, c // G
                        dve.wait_ge(c_mm, reuse(n))
                        nc.vector.tensor_scalar(S[:, c % RING, :], iota_f[:], dst_rel[:, ds(k * NC + c, 1)], None,
                                                ALU.is_equal)
                        dve.wait_ge(c_ee, of(n, NC))
                        dve.wait_ge(cxg_in[g], 16 * G * ((l) * KT + k + 1))
                        nc.vector.tensor_tensor(ring_a[:, c % RING, :], ps[c % RING][:, 0:D], xg[:, c, 0:D],
                                                ALU.add).then_inc(c_sum, 1)
                        if c % G == G - 1:
                            next_indices(k, g, cidx_ready)

                    base_of = [None] * NC

                    def load_bases(k, c):
                        if c == 0:
                            base_of[:] = bases(DVE, k)

                    def add(k, c):
                        n = (l * KT + k) * NC + c
                        dve.wait_ge(c_mm, of(n))
                        dve.wait_ge(c_acc, of(n - 1))
                        to = acc[:, :, ds(base_of[c], P)]
                        nc.vector.tensor_tensor(to, to, halves(RING + c % RING, P),
                                                ALU.add).then_inc(c_acc, 1)

                    first_indices(cidx_ready)
                    pipelined(dve, [(2, add_rows), (0, load_bases), (0, add)])

                    chain = [0]

                    def link(ins):
                        chain[0] += 1
                        ins.then_inc(own_bn, 1)
                        dve.wait_ge(own_bn, BN_LINKS * l + chain[0])

                    dve.wait_ge(c_acc, of((l + 1) * NT - 1))

                    def moments(a):
                        link(nc.vector.tensor_tensor(acc[:, a, :], acc[:, a, :], dinv_b[:, 0:NP], ALU.mult))
                        link(nc.vector.tensor_tensor(acc[:, a, :], acc[:, a, :], conv0[:, a, :], ALU.add))
                        for i in range(-(-N // 512)):
                            last = nc.vector.bn_stats(stats[:, a, i, :], acc[:, a, i * 512:min(N, i * 512 + 512)])
                        chain[0] += 1
                        last.then_inc(own_bn, 1)
                        wait_apart(dve, own_bn, BN_LINKS * l + chain[0])
                        nc.vector.bn_aggr(mv[:, a, :], stats[:, a, 0:-(-N // 512), :]).then_inc(bn_var, 1)

                    def scales(a):
                        sd, rs, scale, shift = (small[:, 4 * a + i:4 * a + i + 1] for i in range(4))
                        dve.wait_ge(bn_sd, HALVES * l + a + 1)
                        link(nc.vector.reciprocal(rs, sd))
                        link(nc.vector.tensor_tensor(scale, rs, prm[:, ds(PCOL["gamma"] + 2 * l + a, 1)], ALU.mult))
                        link(nc.vector.tensor_tensor(shift, mv[:, a, 0:1], scale, ALU.mult))
                        nc.vector.tensor_tensor(shift, prm[:, ds(PCOL["beta"] + 2 * l + a, 1)], shift,
                                                ALU.subtract).then_inc(bn_shift, 1)

                    def update(a):
                        dve.wait_ge(bn_norm, HALVES * l + a + 1)
                        nc.vector.scalar_tensor_tensor(hT[:, a, 0:N], acc[:, a, 0:N], floor_l[:, ds(l, 1)],
                                                       hT[:, a, 0:N], ALU.max, ALU.add)

                    moments(0)
                    scales(0)
                    moments(1)
                    scales(1)
                    update(0)
                    update(1)
                    assert chain[0] == BN_LINKS

        with nc.Block() as block:
            WHOLE = N // P

            def each(eng, step):
                with eng.Fori(0, WHOLE // 2) as j:
                    step(j, 0, P)
                    step(j, 1, P)
                step(WHOLE // 2, 0, N - WHOLE * P)

            @block.gpsimd
            def _(pool):
                def tile(j, q, rows):
                    wait_apart(pool, f_T, reuse(2 * j + q))
                    cols = ds((2 * j + q) * P, P)
                    nc.gpsimd.tensor_tensor(tiles[:, q, :, :], hT[:, :, cols], x1T[:, :, cols], ALU.add).then_inc(f_tile, 1)
                each(pool, tile)

            @block.tensor
            def _(pe):
                def turn(j, q, rows):
                    pe.wait_ge(f_tile, of(2 * j + q, 2))
                    pe.wait_ge(f_row, reuse(2 * j + q))
                    for a in range(HALVES):
                        last = nc.tensor.transpose(ps[q][:, a * P:a * P + P], tiles[:, q, a, :], ident[:])
                    last.then_inc(f_T, 1)
                each(pe, turn)

            @block.scalar
            def _(act):
                def root_of(j, q, rows):
                    act.wait_ge(f_var, 2 * j + q + 1)
                    nc.scalar.activation(small[:, 8 + q:9 + q], mv[:, q, 1:2], ACT.Sqrt, bias=eps[:]).then_inc(f_sd, 1)
                each(act, root_of)

            @block.vector
            def _(dve):
                def normal(j, q, rows):
                    n = 2 * j + q
                    dve.wait_ge(f_T, of(n, 2))
                    nc.vector.bn_stats(stats[:, q, 0, :], ps[q][:, 0:D]).then_inc(own_f, 1)
                    wait_apart(dve, own_f, 2 * n + 1)
                    nc.vector.bn_aggr(mv[:, q, :], stats[:, q, 0:1, :]).then_inc(f_var, 1)
                    dve.wait_ge(f_sd, n + 1)
                    nc.vector.reciprocal(small[:, 12 + q:13 + q], small[:, 8 + q:9 + q]).then_inc(own_f, 1)
                    dve.wait_ge(own_f, 2 * n + 2)
                    dve.wait_ge(f_out[q], 16 * (j + 1))
                    nc.vector.tensor_scalar(stage[:, q, 0:D], ps[q][:, 0:D], mv[:, q, 0:1], small[:, 12 + q:13 + q],
                                            ALU.subtract, ALU.mult).then_inc(f_row, 1)
                each(dve, normal)

            @block.sync
            def _(sp):
                def store(j, q, rows):
                    sp.wait_ge(f_row, of(2 * j + q, 2))
                    sp.dma_start(out[ds((2 * j + q) * P, rows), :], stage[0:rows, q, 0:D]).then_inc(f_out[q], 16)
                each(sp, store)
                sp.wait_ge(f_out[0], 16 * (WHOLE // 2 + 2))
                sp.wait_ge(f_out[1], 16 * (WHOLE // 2 + 1))


_INS = ["x", "src", "dst", "edge_attr_128", "edge_weight", "L0_gnn_W_l", "L0_gnn_b_l", "L0_gnn_W_r", "L0_gnn_b_r",
        "L0_gnn_att", "L0_gnn_bias", "L1_gnn_W", "L1_gnn_b", "L1_gnn_root", "L1_gnn_We", "L1_gnn_be",
        "L1_gnn_gamma", "L1_gnn_beta"]

def kernel(**inputs):
    import concourse.bacc as bacc
    from concourse.bass_utils import run_bass_kernel_spmd

    nc = bacc.Bacc("TRN2", target_bir_lowering=False, num_devices=1)
    arrays, args = {}, []
    for name in _INS:
        a = np.ascontiguousarray(inputs[name])
        arrays[f"in_{name}"] = a
        args.append(nc.dram_tensor(f"in_{name}", a.shape, mybir.dt.from_np(a.dtype), kind="ExternalInput").ap())
    out = nc.dram_tensor("out", (N, D), F32, kind="ExternalOutput").ap()
    program(nc, *args, out)
    return run_bass_kernel_spmd(nc, [arrays], core_ids=[0]).results[0]["out"]
```

```python
from contextlib import ExitStack

import numpy as np

import concourse.bass as bass
from concourse import mybir

F32, I32, BF16 = mybir.dt.float32, mybir.dt.int32, mybir.dt.bfloat16
ALU = mybir.AluOpType
ACT = mybir.ActivationFunctionType
DVE = mybir.EngineType.DVE
SP = mybir.EngineType.SP

P = 128
N, E, D, ED, H, C, L = 3125, 53125, 256, 128, 8, 32, 5
HALVES = D // P
NC = P // H
KT = -(-E // (P * NC))
NT = NC * KT
CH = KT * P
FULL = E // P
TAIL = E - FULL * P
RB = NT // 4
NP = -(-(N + P) // P) * P
NTILE = NP // P
JC = 2 * P
JT = NP // JC
G = 4
NG = NC // G
RING = 4
S_RING = 8
RESET = -1e38
NO_EDGE = -1e30
LN2_96 = 66.54212933375474
EPS = 1e-5
FAR = 1000000
GW = D + 1
PRM = ["att", "bias", "b", "be", "root", "gamma", "beta"]
PROWS = [2, 2, 2 * L, 2 * L, 2 * L, 2 * L, 2 * L]
PCOL = {n: sum(PROWS[:i]) for i, n in enumerate(PRM)}
NPRM = sum(PROWS)


def pipelined(eng, stages, count=NT, width=NC):
    most = max(lead for lead, _ in stages)

    def at(n, stage):
        if 0 <= n < count:
            stage(n // width, n % width)

    for n in range(-most, 0):
        for lead, stage in stages:
            at(n + lead, stage)
    whole = (count - most) // width
    with eng.Fori(0, whole) as k:
        for c in range(width):
            for lead, stage in stages:
                stage(k + (c + lead) // width, (c + lead) % width)
    for n in range(whole * width, count):
        for lead, stage in stages:
            at(n + lead, stage)


def program(nc, x, src, dst, edge_attr, edge_weight, W_l, b_l, W_r, b_r, att, bias,
            W, b, root, We, be, gamma, beta, out):
    ds = bass.ds
    ctx = ExitStack()
    with ctx:
        ctx.enter_context(nc.allow_non_contiguous_dma(reason="single elements at the chunks' borders"))

        def sb(name, shape, dt=F32):
            return ctx.enter_context(nc.sbuf_tensor(name, shape, dt))

        def sem(name):
            return ctx.enter_context(nc.semaphore(name))

        primed = []

        def ring_sem(name, slots=RING):
            s = sem(name)
            primed.append((s, slots))
            return s

        xl_table = nc.dram_tensor("xl_table", (NP, GW), F32).ap()
        x_l_rows = nc.dram_tensor("x_l_rows", (NP, D), F32).ap()
        xr_table = nc.dram_tensor("xr_table", (NP, D), F32).ap()
        gcn_table = nc.dram_tensor("gcn_table", (NP, D), F32).ap()
        attr_T = nc.dram_tensor("attr_T", (NT // G, P, G * P), F32).ap()

        hT = sb("hT", [P, HALVES, NP])
        acc = sb("acc", [P, HALVES, NP])
        conv0 = sb("conv0", [P, HALVES, NP])
        x1T = sb("x1T", [P, HALVES, NP + 2])
        dinv_b = sb("dinv_b", [P, NP + 2])
        bwd_max = sb("bwd_max", [P, CH])[:]
        scores = conv0[:, 0, :]
        scoresT = conv0[:, 1, :]
        x1flat = x1T[:].rearrange("p a n -> p (a n)")
        breaks = x1flat[:, 0:CH + 1]
        fwd_max = x1flat[:, CH + 2:2 * CH + 2]
        chunk_dst = dinv_b[:, 0:CH + 2].bitcast(I32)
        den = dinv_b[0:H, 0:NP]

        src_idx = sb("src_idx", [P, NT + NC], I32)
        src_hi = sb("src_hi", [P, NT])
        src_lo = sb("src_lo", [P, NT])
        dst_rel = sb("dst_rel", [P, NT])
        log_w = sb("log_w", [P, NT])
        dinv_src = sb("dinv_src", [P, NT])
        base_f = sb("base_f", [1, NT])
        base_i = sb("base_i", [1, NT], I32)

        xg = sb("xg", [P, NC, GW])
        idx = sb("idx", [P, NC], I32)
        S = sb("S", [P, RING, P])
        ring_a = sb("ring_a", [P, RING, D])
        ring_b = sb("ring_b", [P, RING, D])
        ring_c = sb("ring_c", [P, RING, P])
        fifths = sb("fifths", [P, RING, D])
        attr_in = sb("attr_in", [P, NG, G, P])
        attr_out = sb("attr_out", [P, 2, G * P])
        ex_g = sb("ex_g", [P, NG, H, G])
        tiles = sb("tiles", [P, 2, HALVES, P])
        stage = sb("stage", [P, 2, 2 * D])

        wA = sb("wA", [P, HALVES, D])
        wB = sb("wB", [P, HALVES, D])
        rowbias = sb("rowbias", [P, 2, D])
        prm_rows = sb("prm_rows", [NPRM, P])
        prm = sb("prm", [P, NPRM])
        root_be = sb("root_be", [P, 2 * L])
        flat = conv0[:].rearrange("p a n -> p (a n)")
        W_all = flat[:, 0:2 * L * D].rearrange("p (i n) -> p i n", i=2 * L)
        We_all = flat[:, 2 * L * D:3 * L * D].rearrange("p (l n) -> p l n", l=L)
        b_rows, be_rows = flat[:, 3 * L * D:4 * L * D], flat[:, 4 * L * D:5 * L * D]
        b_all = b_rows.rearrange("p (l n) -> p l n", l=L)
        floor_l = sb("floor_l", [P, L])
        ident = sb("ident", [P, P])
        ones = sb("ones", [P, P])
        mean_w = sb("mean_w", [P, P])
        iota_i = sb("iota_i", [P, P], I32)
        iota_f = sb("iota_f", [P, P])
        head_of = sb("head_of", [H, D])
        att_w = sb("att_w", [P, HALVES, H])
        spare = fwd_max.bitcast(BF16)
        onehot_lo = spare[:, 0:NC * P].rearrange("p (c n) -> p c n", c=NC)
        onehot_hi = spare[:, NC * P:NC * (P + NTILE)].rearrange("p (c n) -> p c n", c=NC)
        counts = sb("counts", [P, NTILE])
        dinv_n = sb("dinv_n", [P, NTILE])
        invdeg_n = sb("invdeg_n", [P, NTILE])
        small = sb("small", [P, 64])
        carry = ring_b[0:1, :, :].rearrange("p r d -> p (r d)").rearrange("p (i n) -> p i n", i=8)
        stats = sb("stats", [P, HALVES, 8, 6])
        mv = sb("mv", [P, HALVES, 2])
        eps = sb("eps", [P, 1])

        ps = [ctx.enter_context(nc.psum_tensor(f"ps{i}", [P, 512], F32)) for i in range(8)]

        def halves(bank, n):
            return ps[bank][:, 0:HALVES * n].rearrange("p (a n) -> p a n", a=HALVES)

        def of(n, slots=RING):
            return n + 1 + slots

        def reuse(n):
            return n + 1

        def bases(eng_type, k):
            return nc.values_load_multi_w_load_instructions(base_i[0:1, ds(k * NC, NC)], engines=(eng_type,),
                                                            min_val=0, max_val=N - 1,
                                                            skip_runtime_bounds_check_because="clamped to N - 1")[1]

        def gathers(pool, table, width, idx_ready, arrived, layer):
            with pool.Fori(0, KT) as k:
                for g in range(NG):
                    for c in range(g * G, g * G + G):
                        if c == g * G:
                            wait_apart(pool, idx_ready, (layer * (KT + 1) + k) * NG + g + 1)
                        pool.indirect_dma_start(xg[:, c, 0:width], None, table,
                                                bass.IndirectOffsetOnAxis(ap=idx[:, c:c + 1], axis=0)
                                                ).then_inc(arrived[g], 16)

        def first_indices(idx_ready):
            for g in range(NG):
                nc.vector.tensor_copy(idx[:, g * G:g * G + G], src_idx[:, g * G:g * G + G]).then_inc(idx_ready, 1)

        def next_indices(k, g, idx_ready):
            nc.vector.tensor_copy(idx[:, g * G:g * G + G],
                                  src_idx[:, ds((k + 1) * NC + g * G, G)]).then_inc(idx_ready, 1)

        def wait_apart(eng, s, value):
            value = value if isinstance(value, int) else eng.to_reg(value)
            eng.wait_ge(consts, 1)
            eng.wait_ge(s, value)

        gw_in, gx_in = sem("gw_in"), [sem(f"gx_in{q}") for q in range(2)]
        gx_T, gx_copy, gt_mm, gt_row = [ring_sem(n, 2) for n in ("gx_T", "gx_copy", "gt_mm", "gt_row")]
        gt_out = [ring_sem(f"gt_out{q}", 48) for q in range(2)]

        aidx_ready, axg_in = sem("aidx_ready"), [sem(f"axg_in{g}") for g in range(NG)]
        axr_in = [sem(f"axr_in{c}") for c in range(NC)]
        aS_ready, aT_done, aST_ready, afifth, alk_ready, asc_done = [
            ring_sem(n) for n in ("aS_ready", "aT_done", "aST_ready", "afifth", "alk_ready", "asc_done")]
        gx_done = ring_sem("gx_done", NC)
        asc_copied = ring_sem("asc_copied", 2)
        hist_in, hist_mm, hist_added = sem("hist_in"), sem("hist_mm"), sem("hist_added")

        sm_T, sm_copy, sm_ends, sm_rows, sm_carry, sm_cols, sm_diff, sm_ex, own_s = [
            sem(n) for n in ("sm_T", "sm_copy", "sm_ends", "sm_rows", "sm_carry", "sm_cols", "sm_diff", "sm_ex", "own_s")]
        deg_done, root_done, dinv_done, dinv_out = [sem(n) for n in ("deg_done", "root_done", "dinv_done", "dinv_out")]

        bidx_ready, bxg_in = sem("bidx_ready"), [sem(f"bxg_in{g}") for g in range(NG)]
        bat_in = [sem(f"bat_in{g}") for g in range(NG)]
        b_square, b_S, b_ready, b_mm, b_acc = [ring_sem(n) for n in ("b_square", "b_S", "b_ready", "b_mm", "b_acc")]
        bex_ready = sem("bex_ready")
        bat_T, bat_copy = ring_sem("bat_T", NG), ring_sem("bat_copy", 2)
        bat_out = [ring_sem(f"bat_out{i}", 16) for i in range(2)]

        bc_mm, bc_copy, rden_done, own_n = [sem(n) for n in ("bc_mm", "bc_copy", "rden_done", "own_n")]
        ln_den, ln_z, ln_mean, ln_d, ln_sq, ln_var, ln_sd = [
            sem(n) for n in ("ln_den", "ln_z", "ln_mean", "ln_d", "ln_sq", "ln_var", "ln_sd")]

        lw_in = sem("lw_in")
        lt_tile, lt_mm, lt_row, lr_T, lr_relu, lr_acc = [
            ring_sem(n) for n in ("lt_tile", "lt_mm", "lt_row", "lr_T", "lr_relu", "lr_acc")]
        lt_out = [ring_sem(f"lt_out{q}", 16) for q in range(RING)]
        cidx_ready, cxg_in = sem("cidx_ready"), [sem(f"cxg_in{g}") for g in range(NG)]
        cat_in = [sem(f"cat_in{g}") for g in range(NG)]
        c_ee = ring_sem("c_ee", NC)
        c_sum, c_msg, c_mm, c_acc = [ring_sem(n) for n in ("c_sum", "c_msg", "c_mm", "c_acc")]
        own_bn, bn_var, bn_sd, bn_shift, bn_norm = [sem(n) for n in ("own_bn", "bn_var", "bn_sd", "bn_shift", "bn_norm")]

        f_tile, f_T, f_row = [ring_sem(n, 2) for n in ("f_tile", "f_T", "f_row")]
        f_out = [ring_sem(f"f_out{q}", 16) for q in range(2)]
        own_f, f_var, f_sd = sem("own_f"), sem("f_var"), sem("f_sd")

        rows_i = hT[:].rearrange("p a n -> p (a n)").bitcast(I32)
        rows_f = acc[:].rearrange("p a n -> p (a n)")
        SROW, DROW, WROW = 0, 512, 1024
        rows_in, rows_clear, chunk_in = sem("rows_in"), sem("rows_clear"), sem("chunk_in")
        consts, own_v, rows_T, base_b = sem("consts"), sem("own_v"), sem("rows_T"), sem("base_b")
        log_done, own_p = sem("log_done"), sem("own_p")
        iota_done, rows_float, base_done, scaled_w = sem("iota_done"), sem("rows_float"), sem("base_done"), sem("scaled_w")
        with nc.Block() as block:
            @block.sync
            def _(sp):
                sp.wait_ge(rows_clear, 2)
                for col, a, view in ((SROW, src, rows_i), (DROW, dst, rows_i), (WROW, edge_weight, rows_f)):
                    rows = view[0:RB, col:col + 512].rearrange("p (q e) -> p q e", q=4)
                    whole = a[0:3 * RB * P].rearrange("(q p e) -> p q e", p=RB, e=P)
                    sp.dma_start(rows[:, 0:3, :], whole).then_inc(rows_in, 16)
                    rest = a[3 * RB * P:FULL * P].rearrange("(p e) -> p e", e=P)
                    sp.dma_start(rows[0:RB - 1, 3, :], rest).then_inc(rows_in, 16)
                    last = a[FULL * P:E].rearrange("(a e) -> a e", a=1)
                    sp.dma_start(rows[RB - 1:RB, 3, 0:TAIL], last).then_inc(rows_in, 16)
                lh = "l (h p) -> (l h) p"
                for name, a in zip(PRM, (att.rearrange("(a h) c -> a (h c)", h=4),
                                         bias.rearrange("(a p) -> a p", p=P),
                                         b.rearrange(lh, p=P), be.rearrange(lh, p=P), root.rearrange(lh, p=P),
                                         gamma.rearrange(lh, p=P), beta.rearrange(lh, p=P))):
                    r = PCOL[name]
                    sp.dma_start(prm_rows[r:r + a.shape[0], :], a).then_inc(rows_in, 16)

            ROWS_IN = 16 * (9 + len(PRM))

            @block.scalar
            def _(act):
                act.wait_ge(rows_clear, 2)
                for h in range(H):
                    q = h * NC
                    act.dma_start(chunk_dst[q:q + NC - 1, 1:CH + 1],
                                  dst[0:(NC - 1) * CH].rearrange("(c x) -> c x", x=CH)).then_inc(chunk_in, 16)
                    act.dma_start(chunk_dst[q + NC - 1:q + NC, 1:1 + E - (NC - 1) * CH],
                                  dst[(NC - 1) * CH:E].rearrange("(a x) -> a x", a=1)).then_inc(chunk_in, 16)
                    act.dma_start(chunk_dst[q + 1:q + NC, 0:1],
                                  dst[0:(NC - 1) * CH].rearrange("(c x) -> c x", x=CH)[:, CH - 1:CH]
                                  ).then_inc(chunk_in, 16)
                    act.dma_start(chunk_dst[q:q + NC - 2, CH + 1:CH + 2],
                                  dst[CH:(NC - 1) * CH].rearrange("(c x) -> c x", x=CH)[:, 0:1]
                                  ).then_inc(chunk_in, 16)
                    act.dma_start(chunk_dst[q + NC - 2:q + NC - 1, CH + 1:CH + 2],
                                  dst[(NC - 1) * CH:(NC - 1) * CH + 1].rearrange("(a x) -> a x", a=1)
                                  ).then_inc(chunk_in, 16)
                act.wait_ge(scaled_w, 1)
                nc.scalar.activation(log_w[:], log_w[:], ACT.Ln).then_inc(log_done, 1)

            @block.gpsimd
            def _(pool):
                nc.gpsimd.iota(iota_i[:], pattern=[[1, P]], base=0, channel_multiplier=0).then_inc(iota_done, 1)
                nc.gpsimd.memset(ident[:], 0.0).then_inc(own_p, 1)
                nc.gpsimd.memset(head_of[:], 1.0).then_inc(own_p, 1)
                nc.gpsimd.memset(ones[:], 1.0)
                nc.gpsimd.memset(mean_w[:], 1.0 / D)
                nc.gpsimd.memset(eps[:], EPS)
                nc.gpsimd.memset(floor_l[:, 0:L - 1], 0.0)
                nc.gpsimd.memset(floor_l[:, L - 1:L], -3e38)
                pool.wait_ge(own_p, 2)
                nc.gpsimd.affine_select(out=ident[:], in_=ident[:], compare_op=ALU.not_equal, fill=1.0, base=0,
                                        pattern=[[-1, P]], channel_multiplier=1)
                nc.gpsimd.affine_select(out=head_of[:], in_=head_of[:], compare_op=ALU.is_ge, fill=0.0, base=0,
                                        pattern=[[1, D]], channel_multiplier=-C).then_inc(own_p, 1)
                pool.wait_ge(own_p, 3)
                nc.gpsimd.affine_select(out=head_of[:], in_=head_of[:], compare_op=ALU.is_ge, fill=0.0, base=C - 1,
                                        pattern=[[-1, D]], channel_multiplier=C).then_inc(consts, 1)

            @block.tensor
            def _(pe):
                pe.wait_ge(consts, 1)
                pe.wait_ge(rows_in, ROWS_IN)
                pe.wait_ge(rows_float, 1)
                for i, col in enumerate((SROW, DROW, WROW)):
                    for q in range(4):
                        nc.tensor.transpose(ps[i][:, q * RB:q * RB + RB],
                                            rows_f[0:RB, col + q * P:col + q * P + P], ident[0:RB, 0:RB])
                nc.tensor.transpose(ps[3][:, 0:NPRM], prm_rows[:], ident[0:NPRM, 0:NPRM])
                for a in range(HALVES):
                    last = nc.tensor.transpose(ps[3][:, 64 + a * H:64 + a * H + H], head_of[:, a * P:a * P + P],
                                               ident[0:H, 0:H])
                last.then_inc(rows_T, 1)
                pe.wait_ge(base_done, 1)
                nc.tensor.matmul(ps[4][:, 0:NT], ones[0:1, :], base_f[:], start=True, stop=True).then_inc(base_b, 1)
            @block.vector
            def _(dve):
                chain = [0]

                def link(ins):
                    chain[0] += 1
                    ins.then_inc(own_v, 1)
                    dve.wait_ge(own_v, chain[0])

                link(nc.vector.memset(rows_i[0:RB, SROW:SROW + 512], NTILE * P + P - 1))
                link(nc.vector.memset(rows_i[0:RB, DROW:DROW + 512], FAR))
                nc.vector.memset(rows_f[0:RB, WROW:WROW + 512], 1.0).then_inc(rows_clear, 1)
                nc.vector.memset(chunk_dst, -1).then_inc(rows_clear, 1)
                nc.vector.memset(ring_a[:], 0.0)
                dve.wait_ge(rows_in, ROWS_IN)
                nc.vector.tensor_copy(rows_f[0:RB, SROW:SROW + 512], rows_i[0:RB, SROW:SROW + 512])
                nc.vector.tensor_copy(rows_f[0:RB, DROW:DROW + 512],
                                      rows_i[0:RB, DROW:DROW + 512]).then_inc(rows_float, 1)
                dve.wait_ge(iota_done, 1)
                nc.vector.tensor_copy(iota_f[:], iota_i[:])

                def kc(t):
                    return t.rearrange("p (k c) -> p k c", c=NC)

                def from_ps(i, p=P):
                    return ps[i][0:p, 0:NT].rearrange("p (c k) -> p k c", c=NC)

                raw = rows_i[:, 2048:2048 + NT]
                hi_i = rows_i[:, 2560:2560 + NT]
                lo_i = rows_i[:, 3072:3072 + NT]
                tiny, zero = fwd_max[:, 0:NT], fwd_max[:, 512:512 + NT]
                lifted, weight = fwd_max[:, 1024:1024 + NT], fwd_max[:, 1536:1536 + NT]
                dve.wait_ge(rows_T, 1)
                nc.vector.tensor_copy(kc(dst_rel[:]), from_ps(1))
                link(nc.vector.tensor_scalar(kc(base_f[:]), from_ps(1, 1), float(N - 1), None, ALU.min))
                nc.vector.tensor_copy(base_i[:], base_f[:]).then_inc(base_done, 1)
                nc.vector.tensor_scalar(kc(src_idx[:, 0:NT]), from_ps(0), float(N - 1), None, ALU.min)
                nc.vector.memset(src_idx[:, NT:NT + NC], 0)
                link(nc.vector.tensor_copy(kc(raw), from_ps(0)))
                link(nc.vector.tensor_scalar(hi_i, raw, 7, None, ALU.arith_shift_right))
                link(nc.vector.tensor_scalar(lo_i, raw, P - 1, None, ALU.bitwise_and))
                nc.vector.tensor_copy(src_hi[:], hi_i)
                nc.vector.tensor_copy(src_lo[:], lo_i)
                link(nc.vector.tensor_copy(kc(weight), from_ps(2)))
                link(nc.vector.tensor_scalar(tiny, weight, 2.0 ** -64, None, ALU.is_lt))
                link(nc.vector.tensor_scalar(zero, weight, 0.0, NO_EDGE, ALU.is_equal, ALU.mult))
                link(nc.vector.scalar_tensor_tensor(lifted, tiny, 2.0 ** 96, weight, ALU.mult, ALU.mult))
                link(nc.vector.scalar_tensor_tensor(log_w[:], tiny, 0.0, weight, ALU.is_equal, ALU.mult))
                link(nc.vector.tensor_tensor(log_w[:], log_w[:], lifted, ALU.add))
                nc.vector.tensor_scalar(log_w[:], log_w[:], 2.0 ** -64, None, ALU.max).then_inc(scaled_w, 1)
                dve.wait_ge(base_b, 1)
                link(nc.vector.tensor_tensor(dst_rel[:], dst_rel[:], ps[4][:, 0:NT], ALU.subtract))
                link(nc.vector.tensor_copy(prm[:], ps[3][:, 0:NPRM]))
                for a in range(HALVES):
                    nc.vector.tensor_scalar(att_w[:, a, :], ps[3][:, 64 + a * H:64 + a * H + H],
                                            prm[:, a:a + 1], None, ALU.mult)
                nc.vector.tensor_tensor(root_be[:], prm[:, PCOL["root"]:PCOL["root"] + 2 * L],
                                        prm[:, PCOL["be"]:PCOL["be"] + 2 * L], ALU.subtract)
                dve.wait_ge(log_done, 1)
                link(nc.vector.scalar_tensor_tensor(log_w[:], tiny, -LN2_96, log_w[:], ALU.mult, ALU.add))
                link(nc.vector.tensor_tensor(log_w[:], log_w[:], zero, ALU.add))
                dve.wait_ge(chunk_in, 16 * 5 * H)
                link(nc.vector.tensor_tensor(breaks, chunk_dst[:, 1:CH + 2], chunk_dst[:, 0:CH + 1], ALU.not_equal))
                link(nc.vector.tensor_scalar(breaks, breaks, RESET, None, ALU.mult))
                link(nc.vector.memset(counts[:], 0.0))

            @block.sync
            def _(sp):
                for s, slots in primed:
                    sp.sem_inc(s, slots)

        with nc.Block() as block:
            @block.sync
            def _(sp):
                for w, a in ((wA, W_l), (wB, W_r)):
                    sp.dma_start(w[:], a.rearrange("(h p) n -> p h n", p=P)).then_inc(gw_in, 16)
                for i, a in enumerate((b_l, b_r)):
                    sp.dma_start(rowbias[:, i, :],
                                 a.rearrange("(a n) -> a n", a=1).to_broadcast([P, D])).then_inc(gw_in, 16)

                def store(j, q):
                    sp.wait_ge(gt_row, of(2 * j + q, 2))
                    rows = ds((2 * j + q) * P, P)
                    sp.dma_start(xl_table[rows, 0:D], stage[:, q, 0:D]).then_inc(gt_out[q], 16)
                    sp.dma_start(x_l_rows[rows, :], stage[:, q, 0:D]).then_inc(gt_out[q], 16)
                    sp.dma_start(xr_table[rows, :], stage[:, q, D:2 * D]).then_inc(gt_out[q], 16)

                with sp.Fori(0, JT) as j:
                    for q in range(2):
                        store(j, q)
                for q in range(2):
                    sp.wait_ge(gt_out[q], 48 * (JT + 1))

            @block.gpsimd
            def _(pool):
                def load(j, q, rows=P):
                    pool.wait_ge(gx_T, reuse(2 * j + q))
                    pool.dma_start(ring_a[0:rows, q, :], x[ds((2 * j + q) * P, rows), :]).then_inc(gx_in[q], 16)

                with pool.Fori(0, JT - 1) as j:
                    for q in range(2):
                        load(j, q)
                load(JT - 1, 0, N - N // P * P)
                nc.gpsimd.memset(acc[:], 0.0)

            @block.tensor
            def _(pe):
                pe.wait_ge(gw_in, 64)

                def turn(j, q):
                    pe.wait_ge(gx_in[q], 16 * (j + 1))
                    for a in range(HALVES):
                        last = nc.tensor.transpose(ps[q][:, a * P:a * P + P], ring_a[:, q, a * P:a * P + P], ident[:])
                    last.then_inc(gx_T, 1)

                def products(j, q):
                    pe.wait_ge(gx_copy, of(2 * j + q, 2))
                    pe.wait_ge(gt_row, reuse(2 * j + q))
                    for i, w in enumerate((wA, wB)):
                        for a in range(HALVES):
                            last = nc.tensor.matmul(ps[2 + q][:, i * D:i * D + D], tiles[:, q, a, :], w[:, a, :],
                                                    start=(a == 0), stop=(a == HALVES - 1))
                    last.then_inc(gt_mm, 1)

                turn(0, 0)
                with pe.Fori(0, JT - 1) as j:
                    turn(j, 1)
                    products(j, 0)
                    turn(j + 1, 0)
                    products(j, 1)
                products(JT - 1, 0)
                products(JT - 1, 1)

            @block.scalar
            def _(act):
                def copies(j, q):
                    act.wait_ge(gx_T, of(2 * j + q, 2))
                    act.wait_ge(gt_mm, reuse(2 * j + q))
                    nc.scalar.copy(tiles[:, q, :, :], ps[q][:, 0:D].rearrange("p (a n) -> p a n", a=HALVES))
                    nc.scalar.copy(hT[:, :, ds((2 * j + q) * P, P)],
                                   ps[q][:, 0:D].rearrange("p (a n) -> p a n", a=HALVES)).then_inc(gx_copy, 1)

                with act.Fori(0, JT - 1) as j:
                    copies(j, 0)
                    copies(j, 1)
                copies(JT - 1, 0)
                act.wait_ge(gt_mm, reuse(2 * JT - 1))
                nc.scalar.memzero(hT[:, :, (NTILE - 1) * P:NTILE * P])
                nc.scalar.memzero(tiles[:, 1, :, :]).then_inc(gx_copy, 1)

            @block.vector
            def _(dve):
                dve.wait_ge(gw_in, 64)
                both = rowbias[:].rearrange("p i d -> p (i d)")
                with dve.Fori(0, JT) as j:
                    for q in range(2):
                        dve.wait_ge(gt_mm, of(2 * j + q, 2))
                        dve.wait_ge(gt_out[q], 48 * (j + 1))
                        nc.vector.tensor_tensor(stage[:, q, :], ps[2 + q][:], both, ALU.add).then_inc(gt_row, 1)

        acc_flat = acc[:].rearrange("p a n -> p (a n)")
        xr_ring = acc_flat[:, 0:NC * D].rearrange("p (s d) -> p s d", s=NC)
        S_a = scoresT[:, 0:S_RING * P].rearrange("p (s n) -> p s n", s=S_RING)
        ST_a = scoresT[:, S_RING * P:2 * S_RING * P].rearrange("p (s n) -> p s n", s=S_RING)
        with nc.Block() as block:
            @block.gpsimd
            def _(pool):
                gathers(pool, x_l_rows, D, aidx_ready, axg_in, 0)

            @block.sync
            def _(sp):
                with sp.Fori(0, KT) as k:
                    base = bases(SP, k)
                    for c in range(NC):
                        sp.wait_ge(gx_done, reuse(k * NC + c))
                        sp.dma_start(xr_ring[:, c, :], xr_table[ds(base[c], P), :]).then_inc(axr_in[c], 16)

            @block.tensor
            def _(pe):
                def turn(k, c):
                    n = k * NC + c
                    pe.wait_ge(aS_ready, of(n))
                    pe.wait_ge(aST_ready, of(n - 2))
                    nc.tensor.transpose(ps[c % 2][:, 0:P], S_a[:, c % S_RING, :], ident[:]).then_inc(aT_done, 1)

                def sums(k, c):
                    n = k * NC + c
                    pe.wait_ge(aST_ready, of(n))
                    pe.wait_ge(axr_in[c], 16 * (k + 1))
                    pe.wait_ge(axg_in[c // G], 16 * G * (k + 1))
                    o = ps[2 + c % RING]
                    for a in range(HALVES):
                        nc.tensor.matmul(o[:, a * P:a * P + P], xg[:, c, a * P:a * P + P], ident[:],
                                         start=True, stop=False, is_transpose=True)
                        last = nc.tensor.matmul(o[:, a * P:a * P + P], xr_ring[:, c, a * P:a * P + P],
                                                ST_a[:, c % S_RING, :], start=False, stop=True)
                    last.then_inc(gx_done, 1)

                def score(k, c):
                    pe.wait_ge(alk_ready, of(k * NC + c))
                    if c % 8 == 0:
                        pe.wait_ge(asc_copied, reuse(2 * k + c // 8))
                    if c == 8:
                        pe.wait_ge(hist_added, k + 1)
                    for a in range(HALVES):
                        last = nc.tensor.matmul(ps[6 + c // 8][:, c * H:c * H + H],
                                                ring_a[:, c % RING, a * P:a * P + P], att_w[:, a, :],
                                                start=(a == 0), stop=(a == HALVES - 1))
                    last.then_inc(asc_done, 1)

                def histogram(k, c):
                    if c == 12:
                        pe.wait_ge(hist_in, k + 1)
                        for i in range(NC):
                            last = nc.tensor.matmul(ps[7][:, 256:256 + NTILE], onehot_lo[:, i, :], onehot_hi[:, i, :],
                                                    start=(i == 0), stop=(i == NC - 1))
                        last.then_inc(hist_mm, 1)

                pipelined(pe, [(5, turn), (3, sums), (0, score), (0, histogram)])

            @block.scalar
            def _(act):
                def onehot_T(k, c):
                    act.wait_ge(aT_done, of(k * NC + c))
                    nc.scalar.copy(ST_a[:, c % S_RING, :],
                                   ps[c % 2][:, 0:P]).then_inc(aST_ready, 1)

                def fifth(k, c):
                    act.wait_ge(gx_done, of(k * NC + c, NC))
                    nc.scalar.mul(fifths[:, c % RING, :], ps[2 + c % RING][:, 0:D], 0.2).then_inc(afifth, 1)

                pipelined(act, [(5, onehot_T), (2, fifth)])

            @block.vector
            def _(dve):
                def onehot(k, c):
                    dve.wait_ge(gx_done, of(k * NC + c - S_RING, NC))
                    nc.vector.tensor_scalar(S_a[:, c % S_RING, :], iota_f[:], dst_rel[:, ds(k * NC + c, 1)], None,
                                            ALU.is_equal).then_inc(aS_ready, 1)

                def leaky(k, c):
                    dve.wait_ge(afifth, of(k * NC + c))
                    nc.vector.tensor_tensor(ring_a[:, c % RING, :], ps[2 + c % RING][:, 0:D],
                                            fifths[:, c % RING, :], ALU.max).then_inc(alk_ready, 1)

                def refill(k, c):
                    if c % G == G - 1:
                        next_indices(k, c // G, aidx_ready)

                def keep_scores(k, c):
                    if c % 8 == 7:
                        n, first, cols = k * NC + c, c - 7, ds(k * NC + c - 7, 8)
                        dve.wait_ge(asc_done, of(n))
                        to = scores[:, ds(k * P, P)].rearrange("p (h c) -> p h c", h=H)[:, :, first:first + 8]
                        got = ps[6 + c // 8][:, first * H:first * H + 8 * H].rearrange("p (c h) -> p h c", h=H)
                        nc.vector.tensor_tensor(to, got, log_w[:, cols].unsqueeze(1).to_broadcast([P, H, 8]),
                                                ALU.add).then_inc(asc_copied, 1)

                def add_counts():
                    nc.vector.tensor_tensor(counts[:], counts[:], ps[7][:, 256:256 + NTILE], ALU.add).then_inc(hist_added, 1)

                def histogram(k, c):
                    if c in (2, 4, 6, 8):
                        q = (c // 2 - 1) * 4
                        if c == 2:
                            dve.wait_ge(hist_mm, k + 1)
                            add_counts()
                        for to, part, wd in ((onehot_lo, src_lo, P), (onehot_hi, src_hi, NTILE)):
                            last = nc.vector.tensor_tensor(
                                to[:, q:q + 4, :], part[:, ds(k * NC + q, 4)].unsqueeze(2).to_broadcast([P, 4, wd]),
                                iota_f[:, 0:wd].unsqueeze(1).to_broadcast([P, 4, wd]), ALU.is_equal)
                        if c == 8:
                            last.then_inc(hist_in, 1)

                nc.vector.memset(ps[7][:, 256:256 + NTILE], 0.0).then_inc(hist_mm, 1)
                first_indices(aidx_ready)
                pipelined(dve, [(7, onehot), (1, leaky), (1, refill), (0, keep_scores), (0, histogram)])
                dve.wait_ge(hist_mm, KT + 1)
                add_counts()

        def chunk_group(g):
            return slice(g * 4 * P, min((g + 1) * 4, KT) * P)

        CG = -(-KT // 4)
        with nc.Block() as block:
            @block.tensor
            def _(pe):
                def turn(source, g, first):
                    if g + first >= 2:
                        pe.wait_ge(sm_copy, g + first - 1)
                    for k in range(4 * g, min(4 * g + 4, KT)):
                        last = nc.tensor.transpose(ps[(g + first) % 2][:, k % 4 * P:k % 4 * P + P],
                                                   source[:, k * P:k * P + P], ident[:])
                    last.then_inc(sm_T, 1)

                for g in range(CG):
                    turn(scores, g, 0)
                pe.wait_ge(sm_ends, 1)
                for i in range(4):
                    last = nc.tensor.transpose(ps[2][0:1, i * P:i * P + P], small[:, i:i + 1], ident[:])
                last.then_inc(sm_rows, 1)
                pe.wait_ge(sm_carry, 1)
                for i in range(2):
                    last = nc.tensor.transpose(ps[3][:, i:i + 1], carry[:, 6 + i, :], ident[0:1, 0:1])
                last.then_inc(sm_cols, 1)
                pe.wait_ge(sm_ex, 1)
                for g in range(CG):
                    turn(scoresT, g, CG)

            @block.scalar
            def _(act):
                act.wait_ge(deg_done, 1)
                nc.scalar.activation(dinv_n[:], invdeg_n[:], ACT.Sqrt).then_inc(root_done, 1)
                act.wait_ge(sm_diff, 1)
                nc.scalar.activation(scoresT, scoresT, ACT.Exp).then_inc(sm_ex, 1)

            @block.gpsimd
            def _(pool):
                nc.gpsimd.memset(acc[:], 0.0)
                nc.gpsimd.memset(den, 0.0)

            @block.vector
            def _(dve):
                chain = [0]

                def link(ins):
                    chain[0] += 1
                    ins.then_inc(own_s, 1)
                    dve.wait_ge(own_s, chain[0])

                degree, t = small[:, 8:8 + NTILE], small[:, 36:36 + NTILE]
                link(nc.vector.tensor_scalar(degree, counts[:], 1.0, None, ALU.add))
                nc.vector.reciprocal(invdeg_n[:], degree).then_inc(deg_done, 1)
                dve.wait_ge(root_done, 1)
                link(nc.vector.tensor_tensor(t, dinv_n[:], dinv_n[:], ALU.mult))
                link(nc.vector.tensor_tensor(t, t, degree, ALU.mult))
                link(nc.vector.tensor_scalar(t, t, -0.5, 1.5, ALU.mult, ALU.add))
                nc.vector.tensor_tensor(dinv_n[:], dinv_n[:], t, ALU.mult).then_inc(dinv_done, 1)

                for g in range(CG):
                    dve.wait_ge(sm_T, g + 1)
                    cols = chunk_group(g)
                    nc.vector.tensor_copy(scoresT[:, cols], ps[g % 2][:, 0:cols.stop - cols.start]).then_inc(sm_copy, 1)
                dve.wait_ge(sm_copy, CG)

                def scans(first_f, first_b):
                    nc.vector.tensor_tensor_scan(out=fwd_max, data0=breaks[:, 0:CH], data1=scoresT,
                                                 initial=first_f, op0=ALU.add, op1=ALU.max)
                    link(nc.vector.tensor_tensor_scan(out=bwd_max[:, ::-1], data0=breaks[:, 1:CH + 1][:, ::-1],
                                                      data1=scoresT[:, ::-1], initial=first_b,
                                                      op0=ALU.add, op1=ALU.max))

                scans(RESET, RESET)
                nc.vector.tensor_copy(small[:, 0:1], fwd_max[:, CH - 1:CH])
                nc.vector.tensor_copy(small[:, 1:2], bwd_max[:, 0:1])
                nc.vector.tensor_reduce(small[:, 2:3], breaks[:, 0:CH], mybir.AxisListType.X, ALU.min)
                nc.vector.tensor_reduce(small[:, 3:4], breaks[:, 1:CH + 1], mybir.AxisListType.X,
                                        ALU.min).then_inc(sm_ends, 1)
                dve.wait_ge(sm_rows, 1)
                link(nc.vector.tensor_copy(carry[:, 0:4, :], ps[2][0:1, :].rearrange("p (i n) -> p i n", i=4)))
                nc.vector.memset(carry[:, 6, 0:1], RESET)
                link(nc.vector.memset(carry[:, 7, P - 1:P], RESET))
                link(nc.vector.tensor_tensor_scan(out=carry[:, 4, :], data0=carry[:, 2, :], data1=carry[:, 0, :],
                                                  initial=RESET, op0=ALU.add, op1=ALU.max))
                link(nc.vector.tensor_tensor_scan(out=carry[:, 5, ::-1], data0=carry[:, 3, ::-1],
                                                  data1=carry[:, 1, ::-1], initial=RESET, op0=ALU.add, op1=ALU.max))
                nc.vector.tensor_copy(carry[:, 6, 1:P], carry[:, 4, 0:P - 1])
                nc.vector.tensor_copy(carry[:, 7, 0:P - 1], carry[:, 5, 1:P]).then_inc(sm_carry, 1)
                dve.wait_ge(sm_cols, 1)
                link(nc.vector.tensor_copy(small[:, 4:6], ps[3][:, 0:2]))
                scans(small[:, 4:5], small[:, 5:6])
                link(nc.vector.tensor_tensor(fwd_max, fwd_max, bwd_max, ALU.max))
                nc.vector.tensor_tensor(scoresT, scoresT, fwd_max, ALU.subtract).then_inc(sm_diff, 1)
                for g in range(CG):
                    dve.wait_ge(sm_T, CG + g + 1)
                    cols = chunk_group(g)
                    nc.vector.tensor_copy(scores[:, cols],
                                          ps[(g + CG) % 2][:, 0:cols.stop - cols.start]).then_inc(sm_copy, 1)

            @block.sync
            def _(sp):
                sp.wait_ge(dinv_done, 1)
                sp.dma_start(xl_table[:, D:GW].rearrange("(i p) w -> p i w", p=P),
                             dinv_n[:].unsqueeze(2)).then_inc(dinv_out, 16)
                sp.wait_ge(dinv_out, 16)

        with nc.Block() as block:
            @block.gpsimd
            def _(pool):
                gathers(pool, xl_table, GW, bidx_ready, bxg_in, 0)

            @block.sync
            def _(sp):
                by_chunk = edge_attr[0:(NC - 1) * CH, :].rearrange("(c k p) f -> k p c f", k=KT, p=P)

                def loads(k, last):
                    for g in range(NG):
                        sp.wait_ge(bat_T, reuse(k * NG + g))
                        whole = G if g < NG - 1 else G - 1
                        sp.dma_start(attr_in[:, g, 0:whole, :],
                                     by_chunk[ds(k, 1), :, g * G:g * G + whole, :].rearrange("k p c f -> (k p) c f")
                                     ).then_inc(bat_in[g], 16)
                    rows = TAIL if last else P
                    sp.dma_start(attr_in[0:rows, NG - 1, G - 1, :],
                                 edge_attr[ds(((NC - 1) * KT + k) * P, rows), :]).then_inc(bat_in[NG - 1], 16)

                with sp.Fori(0, KT - 1) as k:
                    loads(k, False)
                loads(KT - 1, True)

            @block.tensor
            def _(pe):
                def turn(k, c):
                    if c % G == 1:
                        g = c // G
                        pe.wait_ge(bat_in[g], (32 if g == NG - 1 else 16) * (k + 1))
                        pe.wait_ge(bat_copy, reuse(k * NG + g))
                        for j in range(G):
                            last = nc.tensor.transpose(ps[RING + g % 2][:, j * P:j * P + P], attr_in[:, g, j, :], ident[:])
                        last.then_inc(bat_T, 1)

                def product(k, c):
                    n = k * NC + c
                    pe.wait_ge(b_S, of(n))
                    pe.wait_ge(b_ready, of(n))
                    pe.wait_ge(b_acc, reuse(n))
                    o = ps[c % RING]
                    for a in range(HALVES):
                        nc.tensor.matmul(o[:, a * P:a * P + P], ring_a[:, c % RING, a * P:a * P + P],
                                         S[:, c % RING, :], start=True, stop=True)
                    nc.tensor.matmul(ps[c % RING][0:H, D:D + P], ex_g[:, c // G, :, c % G],
                                     S[:, c % RING, :], start=True, stop=True).then_inc(b_mm, 1)

                pipelined(pe, [(0, turn), (0, product)])

            @block.scalar
            def _(act):
                def keep(k, c):
                    if c % G == 1:
                        g = c // G
                        n = k * NG + g
                        act.wait_ge(bat_T, of(n, NG))
                        act.wait_ge(bat_out[g % 2], 16 * (2 * k + g // 2 + 1))
                        nc.scalar.copy(attr_out[:, g % 2, :], ps[RING + g % 2][:]).then_inc(bat_copy, 1)
                        act.wait_ge(bat_copy, of(n, 2))
                        act.dma_start(attr_T[ds(k * NG + g, 1), :, :].rearrange("k p e -> (k p) e"),
                                      attr_out[:, g % 2, :]).then_inc(bat_out[g % 2], 16)

                def square(k, c):
                    n = k * NC + c
                    wait_apart(act, b_S, reuse(n))
                    nc.scalar.activation(ring_c[:, c % RING, :], iota_f[:], ACT.Square, scale=-1.0,
                                         bias=dst_rel[:, ds(n, 1)]).then_inc(b_square, 1)

                def onehot(k, c):
                    n = k * NC + c
                    act.wait_ge(b_mm, reuse(n))
                    act.wait_ge(b_square, of(n))
                    nc.scalar.activation(S[:, c % RING, :], ring_c[:, c % RING, :], ACT.Relu, scale=-1.0,
                                         bias=ones[:, 0:1]).then_inc(b_S, 1)

                pipelined(act, [(4, square), (2, onehot), (0, keep)])
                for i in range(2):
                    act.wait_ge(bat_out[i], 16 * (2 * KT + 1))

            @block.vector
            def _(dve):
                def weigh(k, c):
                    n, g = k * NC + c, c // G
                    wait_apart(dve, b_mm, reuse(n))
                    if c % G == 0:
                        nc.vector.tensor_copy(
                            ex_g[:, g, :, :],
                            scores[:, ds(k * P, P)].rearrange("p (h c) -> p h c", h=H)[:, :, c:c + G]
                        ).then_inc(bex_ready, 1)
                        dve.wait_ge(bxg_in[g], 16 * G * (k + 1))
                        dve.wait_ge(bex_ready, k * NG + g + 1)
                    nc.vector.tensor_tensor(ring_a[:, c % RING, :].rearrange("p (h d) -> p h d", h=H),
                                            xg[:, c, 0:D].rearrange("p (h d) -> p h d", h=H),
                                            ex_g[:, g, :, c % G].unsqueeze(2).to_broadcast([P, H, C]),
                                            ALU.mult).then_inc(b_ready, 1)
                    if c % G == G - 1:
                        nc.vector.tensor_copy(dinv_src[:, ds(k * NC + g * G, G)].unsqueeze(2),
                                              xg[:, g * G:g * G + G, D:GW])
                        next_indices(k, g, bidx_ready)

                def add(k, c):
                    n = k * NC + c
                    dve.wait_ge(b_mm, of(n))
                    dve.wait_ge(b_acc, of(n - 1))
                    to = acc[:, :, ds(base_of[c], P)]
                    nc.vector.tensor_tensor(to, to, halves(c % RING, P),
                                            ALU.add)
                    to = den[:, ds(base_of[c], P)]
                    nc.vector.tensor_tensor(to, to, ps[c % RING][0:H, D:D + P],
                                            ALU.add).then_inc(b_acc, 1)

                base_of = [None] * NC

                def load_bases(k, c):
                    if c == 0:
                        base_of[:] = bases(DVE, k)

                first_indices(bidx_ready)
                pipelined(dve, [(2, weigh), (0, load_bases), (0, add)])

        with nc.Block() as block:
            @block.sync
            def _(sp):
                sp.dma_start(W_all, W.rearrange("l (h p) n -> p (l h) n", p=P)).then_inc(lw_in, 16)
                sp.dma_start(We_all, We.rearrange("l p n -> p l n")).then_inc(lw_in, 16)
                for to, v in ((b_rows, b), (be_rows, be)):
                    sp.dma_start(to, v.rearrange("(a l) n -> a (l n)", a=1).to_broadcast([P, L * D])).then_inc(lw_in, 16)

            @block.tensor
            def _(pe):
                pe.wait_ge(rden_done, 1)
                with pe.Fori(0, JT) as j:
                    cols = ds(j * JC, JC)
                    for a in range(HALVES):
                        last = nc.tensor.matmul(ps[0][:, a * JC:a * JC + JC], head_of[:, a * P:a * P + P],
                                                den[:, cols], start=True, stop=True)
                    last.then_inc(ln_den, 1)
                    pe.wait_ge(ln_z, j + 1)
                    for a in range(HALVES):
                        last = nc.tensor.matmul(ps[1][:, 0:JC], mean_w[:], acc[:, a, cols],
                                                start=(a == 0), stop=(a == HALVES - 1))
                    last.then_inc(ln_mean, 1)
                    pe.wait_ge(ln_sq, j + 1)
                    for a in range(HALVES):
                        last = nc.tensor.matmul(ps[2][:, 0:JC], mean_w[:], ring_a[:, a, :],
                                                start=(a == 0), stop=(a == HALVES - 1))
                    last.then_inc(ln_var, 1)
                n = 0
                for what in (dinv_n,):
                    for g in range(CG):
                        if n >= 2:
                            pe.wait_ge(bc_copy, n - 1)
                        for i in range(4 * g, min(4 * g + 4, NTILE)):
                            last = nc.tensor.matmul(ps[3 + n % 2][:, i % 4 * P:i % 4 * P + P],
                                                    what[:, i:i + 1].to_broadcast([P, P]), ident[:],
                                                    start=True, stop=True)
                        last.then_inc(bc_mm, 1)
                        n += 1

            @block.scalar
            def _(act):
                with act.Fori(0, JT) as j:
                    wait_apart(act, ln_d, j + 1)
                    nc.scalar.activation(ring_a[:, 0:HALVES, :], x1T[:, :, ds(j * JC, JC)], ACT.Square).then_inc(ln_sq, 1)
                    act.wait_ge(ln_var, j + 1)
                    nc.scalar.activation(ring_b[:, 0, :], ps[2][:, 0:JC], ACT.Sqrt, bias=eps[:]).then_inc(ln_sd, 1)

            @block.vector
            def _(dve):
                nc.vector.tensor_scalar(den, den, 1e-16, None, ALU.add).then_inc(own_n, 1)
                dve.wait_ge(own_n, 1)
                nc.vector.reciprocal(den, den).then_inc(rden_done, 1)
                OWN = 4
                with dve.Fori(0, JT) as j:
                    cols = ds(j * JC, JC)
                    z, d = acc[:, :, cols], x1T[:, :, cols]
                    dve.wait_ge(ln_den, j + 1)
                    nc.vector.tensor_tensor(z, z, ps[0][:].rearrange("p (a n) -> p a n", a=HALVES),
                                            ALU.mult).then_inc(own_n, 1)
                    dve.wait_ge(own_n, OWN * j + 2)
                    for a in range(HALVES):
                        col = PCOL["bias"] + a
                        last = nc.vector.scalar_tensor_tensor(acc[:, a, cols], acc[:, a, cols], prm[:, col:col + 1],
                                                              hT[:, a, cols], ALU.add, ALU.add)
                    last.then_inc(ln_z, 1)
                    dve.wait_ge(ln_mean, j + 1)
                    nc.vector.tensor_tensor(d, z, ps[1][:, 0:JC].unsqueeze(1).to_broadcast([P, HALVES, JC]),
                                            ALU.subtract).then_inc(ln_d, 1)
                    dve.wait_ge(ln_sd, j + 1)
                    nc.vector.reciprocal(ring_b[:, 1, :], ring_b[:, 0, :]).then_inc(own_n, 1)
                    dve.wait_ge(own_n, OWN * j + 3)
                    nc.vector.tensor_tensor(d, d, ring_b[:, 1, :].unsqueeze(1).to_broadcast([P, HALVES, JC]),
                                            ALU.mult).then_inc(own_n, 1)
                    wait_apart(dve, own_n, OWN * j + 4)
                    nc.vector.tensor_copy(hT[:, :, cols], d).then_inc(own_n, 1)
                n = 0
                for to in (dinv_b,):
                    for g in range(CG):
                        dve.wait_ge(bc_mm, n + 1)
                        cols = chunk_group(g)
                        nc.vector.tensor_copy(to[:, cols], ps[3 + n % 2][:, 0:cols.stop - cols.start]).then_inc(bc_copy, 1)
                        n += 1
                dve.wait_ge(lw_in, 64)
                nc.vector.tensor_tensor(b_rows, b_rows, be_rows, ALU.add)

        BN_LINKS = 5 * HALVES
        node_tiles = fifths[:].rearrange("p s (a n) -> p s a n", a=HALVES)
        rows_out = stage[:].rearrange("p q (i n) -> p (q i) n", i=2)
        with nc.Fori(0, L) as l:
            with nc.Block() as block:
                @block.sync
                def _(sp):
                    def store(k, q):
                        sp.wait_ge(lt_row, of(l * NTILE + k * RING + q))
                        sp.dma_start(gcn_table[ds((k * RING + q) * P, P), :], rows_out[:, q, :]).then_inc(lt_out[q], 16)

                    pipelined(sp, [(0, store)], NTILE, RING)
                    with sp.Fori(0, KT) as k:
                        for g in range(NG):
                            n = (l * KT + k) * NG + g
                            sp.wait_ge(c_ee, G * n + G)
                            sp.dma_start(attr_in[:, g, :, :].rearrange("p j e -> p (j e)"),
                                         attr_T[ds(k * NG + g, 1), :, :].rearrange("k p e -> (k p) e")
                                         ).then_inc(cat_in[g], 16)

                @block.gpsimd
                def _(pool):
                    gathers(pool, gcn_table, D, cidx_ready, cxg_in, l)

                @block.tensor
                def _(pe):
                    def table(k, q):
                        n = l * NTILE + k * RING + q
                        pe.wait_ge(lt_tile, of(n))
                        pe.wait_ge(lt_row, reuse(n))
                        for a in range(HALVES):
                            last = nc.tensor.matmul(ps[q][:, 0:D], node_tiles[:, q, a, :],
                                                    W_all[:, ds(HALVES * l + a, 1), :].rearrange("p i n -> p (i n)"),
                                                    start=(a == 0), stop=(a == HALVES - 1))
                        last.then_inc(lt_mm, 1)

                    def turn(k, q):
                        n = l * NTILE + k * RING + q
                        pe.wait_ge(lt_row, of(n))
                        pe.wait_ge(lr_relu, reuse(n))
                        for a in range(HALVES):
                            last = nc.tensor.transpose(ps[RING + q][:, a * P:a * P + P],
                                                       rows_out[:, q, a * P:a * P + P], ident[:])
                        last.then_inc(lr_T, 1)

                    pipelined(pe, [(3, table), (1, turn)], NTILE, RING)

                    def edge_term(k, c):
                        n = (l * KT + k) * NC + c
                        pe.wait_ge(cat_in[c // G], 16 * ((l) * KT + k + 1))
                        nc.tensor.matmul(ps[c % RING][:, 0:D], attr_in[:, c // G, c % G, :],
                                         We_all[:, ds(l, 1), :].rearrange("p i n -> p (i n)"),
                                         start=True, stop=True).then_inc(c_ee, 1)

                    def sums(k, c):
                        n = (l * KT + k) * NC + c
                        pe.wait_ge(c_msg, of(n))
                        pe.wait_ge(c_acc, reuse(n))
                        o = ps[RING + c % RING]
                        for a in range(HALVES):
                            last = nc.tensor.matmul(o[:, a * P:a * P + P], ring_b[:, c % RING, a * P:a * P + P],
                                                    S[:, c % RING, :], start=True, stop=True)
                        last.then_inc(c_mm, 1)

                    pe.wait_ge(lt_row, of((l + 1) * NTILE - 1))
                    pe.wait_ge(lr_relu, of((l + 1) * NTILE - 1))
                    pipelined(pe, [(3, edge_term), (0, sums)])

                @block.scalar
                def _(act):
                    def tile_copy(k, q):
                        wait_apart(act, lt_mm, reuse(l * NTILE + k * RING + q))
                        nc.scalar.copy(node_tiles[:, q, :, :], hT[:, :, ds((k * RING + q) * P, P)]).then_inc(lt_tile, 1)

                    def root_term(k, q):
                        n = l * NTILE + k * RING + q
                        wait_apart(act, lr_T, of(n))
                        wait_apart(act, lr_acc, reuse(n))
                        for a in range(HALVES):
                            last = nc.scalar.activation(ring_b[:, q, a * P:a * P + P], ps[RING + q][:, a * P:a * P + P],
                                                        ACT.Relu, bias=root_be[:, ds(2 * l + a, 1)])
                        last.then_inc(lr_relu, 1)

                    pipelined(act, [(4, tile_copy), (0, root_term)], NTILE, RING)

                    def message(k, c):
                        wait_apart(act, c_sum, of((l * KT + k) * NC + c))
                        nc.scalar.activation(ring_b[:, c % RING, :], ring_a[:, c % RING, :], ACT.Relu,
                                             scale=dinv_src[:, ds(k * NC + c, 1)]).then_inc(c_msg, 1)

                    pipelined(act, [(0, message)])
                    for a in range(HALVES):
                        act.wait_ge(bn_var, HALVES * l + a + 1)
                        nc.scalar.activation(small[:, 4 * a:4 * a + 1], mv[:, a, 1:2], ACT.Sqrt,
                                             bias=eps[:]).then_inc(bn_sd, 1)
                        act.wait_ge(bn_shift, HALVES * l + a + 1)
                        nc.scalar.activation(acc[:, a, 0:N], acc[:, a, 0:N], ACT.Identity,
                                             scale=small[:, 4 * a + 2:4 * a + 3],
                                             bias=small[:, 4 * a + 3:4 * a + 4]).then_inc(bn_norm, 1)

                @block.vector
                def _(dve):
                    nc.vector.memset(small[:, 62:63], 0.0)

                    def rows(k, q):
                        n = l * NTILE + k * RING + q
                        stores = -(-(NTILE - q) // RING)
                        dve.wait_ge(lt_mm, of(n))
                        dve.wait_ge(lr_T, reuse(n))
                        dve.wait_ge(lt_out[q], 16 * (l * stores + k + 1))
                        nc.vector.tensor_tensor(rows_out[:, q, :], ps[q][:, 0:D],
                                                b_all[:, ds(l, 1), :].rearrange("p l n -> p (l n)"),
                                                ALU.add).then_inc(lt_row, 1)

                    def root(k, q):
                        n, cols = l * NTILE + k * RING + q, ds((k * RING + q) * P, P)
                        dve.wait_ge(lr_relu, of(n))
                        nc.vector.tensor_tensor(acc[:, :, cols], ring_b[:, q, :].rearrange("p (a n) -> p a n", a=HALVES),
                                                dinv_b[:, cols].unsqueeze(1).to_broadcast([P, HALVES, P]),
                                                ALU.mult).then_inc(lr_acc, 1)

                    pipelined(dve, [(2, rows), (0, root)], NTILE, RING)
                    for q in range(RING):
                        dve.wait_ge(lt_out[q], 16 * ((l + 1) * -(-(NTILE - q) // RING) + 1))
                    dve.wait_ge(lr_acc, of((l + 1) * NTILE - 1))
                    first_indices(cidx_ready)

                    def add_rows(k, c):
                        n, g = (l * KT + k) * NC + c, c // G
                        dve.wait_ge(c_mm, reuse(n))
                        nc.vector.tensor_scalar(S[:, c % RING, :], iota_f[:], dst_rel[:, ds(k * NC + c, 1)], None,
                                                ALU.is_equal)
                        dve.wait_ge(c_ee, of(n, NC))
                        dve.wait_ge(cxg_in[g], 16 * G * ((l) * KT + k + 1))
                        nc.vector.tensor_tensor(ring_a[:, c % RING, :], ps[c % RING][:, 0:D], xg[:, c, 0:D],
                                                ALU.add).then_inc(c_sum, 1)
                        if c % G == G - 1:
                            next_indices(k, g, cidx_ready)

                    base_of = [None] * NC

                    def load_bases(k, c):
                        if c == 0:
                            base_of[:] = bases(DVE, k)

                    def add(k, c):
                        n = (l * KT + k) * NC + c
                        dve.wait_ge(c_mm, of(n))
                        dve.wait_ge(c_acc, of(n - 1))
                        to = acc[:, :, ds(base_of[c], P)]
                        nc.vector.tensor_tensor(to, to, halves(RING + c % RING, P),
                                                ALU.add).then_inc(c_acc, 1)

                    pipelined(dve, [(2, add_rows), (0, load_bases), (0, add)])

                    chain = [0]

                    def link(ins):
                        chain[0] += 1
                        ins.then_inc(own_bn, 1)
                        dve.wait_ge(own_bn, BN_LINKS * l + chain[0])

                    dve.wait_ge(c_acc, of((l + 1) * NT - 1))

                    def moments(a):
                        link(nc.vector.tensor_tensor(acc[:, a, :], acc[:, a, :], dinv_b[:, 0:NP], ALU.mult))
                        for i in range(-(-N // 512)):
                            last = nc.vector.bn_stats(stats[:, a, i, :], acc[:, a, i * 512:min(N, i * 512 + 512)])
                        chain[0] += 1
                        last.then_inc(own_bn, 1)
                        wait_apart(dve, own_bn, BN_LINKS * l + chain[0])
                        nc.vector.bn_aggr(mv[:, a, :], stats[:, a, 0:-(-N // 512), :]).then_inc(bn_var, 1)

                    def scales(a):
                        sd, rs, scale, shift = (small[:, 4 * a + i:4 * a + i + 1] for i in range(4))
                        dve.wait_ge(bn_sd, HALVES * l + a + 1)
                        link(nc.vector.reciprocal(rs, sd))
                        link(nc.vector.tensor_tensor(scale, rs, prm[:, ds(PCOL["gamma"] + 2 * l + a, 1)], ALU.mult))
                        link(nc.vector.tensor_tensor(shift, mv[:, a, 0:1], scale, ALU.mult))
                        nc.vector.tensor_tensor(shift, prm[:, ds(PCOL["beta"] + 2 * l + a, 1)], shift,
                                                ALU.subtract).then_inc(bn_shift, 1)

                    def update(a):
                        dve.wait_ge(bn_norm, HALVES * l + a + 1)
                        nc.vector.scalar_tensor_tensor(hT[:, a, 0:N], acc[:, a, 0:N], floor_l[:, ds(l, 1)],
                                                       hT[:, a, 0:N], ALU.max, ALU.add)

                    moments(0)
                    scales(0)
                    moments(1)
                    scales(1)
                    update(0)
                    update(1)
                    assert chain[0] == BN_LINKS

        with nc.Block() as block:
            WHOLE = N // P

            def each(eng, step):
                with eng.Fori(0, WHOLE // 2) as j:
                    step(j, 0, P)
                    step(j, 1, P)
                step(WHOLE // 2, 0, N - WHOLE * P)

            @block.gpsimd
            def _(pool):
                def tile(j, q, rows):
                    wait_apart(pool, f_T, reuse(2 * j + q))
                    cols = ds((2 * j + q) * P, P)
                    nc.gpsimd.tensor_tensor(tiles[:, q, :, :], hT[:, :, cols], x1T[:, :, cols], ALU.add).then_inc(f_tile, 1)
                each(pool, tile)

            @block.tensor
            def _(pe):
                def turn(j, q, rows):
                    pe.wait_ge(f_tile, of(2 * j + q, 2))
                    pe.wait_ge(f_row, reuse(2 * j + q))
                    for a in range(HALVES):
                        last = nc.tensor.transpose(ps[q][:, a * P:a * P + P], tiles[:, q, a, :], ident[:])
                    last.then_inc(f_T, 1)
                each(pe, turn)

            @block.scalar
            def _(act):
                def root_of(j, q, rows):
                    act.wait_ge(f_var, 2 * j + q + 1)
                    nc.scalar.activation(small[:, 8 + q:9 + q], mv[:, q, 1:2], ACT.Sqrt, bias=eps[:]).then_inc(f_sd, 1)
                each(act, root_of)

            @block.vector
            def _(dve):
                def normal(j, q, rows):
                    n = 2 * j + q
                    dve.wait_ge(f_T, of(n, 2))
                    nc.vector.bn_stats(stats[:, q, 0, :], ps[q][:, 0:D]).then_inc(own_f, 1)
                    wait_apart(dve, own_f, 2 * n + 1)
                    nc.vector.bn_aggr(mv[:, q, :], stats[:, q, 0:1, :]).then_inc(f_var, 1)
                    dve.wait_ge(f_sd, n + 1)
                    nc.vector.reciprocal(small[:, 12 + q:13 + q], small[:, 8 + q:9 + q]).then_inc(own_f, 1)
                    dve.wait_ge(own_f, 2 * n + 2)
                    dve.wait_ge(f_out[q], 16 * (j + 1))
                    nc.vector.tensor_scalar(stage[:, q, 0:D], ps[q][:, 0:D], mv[:, q, 0:1], small[:, 12 + q:13 + q],
                                            ALU.subtract, ALU.mult).then_inc(f_row, 1)
                each(dve, normal)

            @block.sync
            def _(sp):
                def store(j, q, rows):
                    sp.wait_ge(f_row, of(2 * j + q, 2))
                    sp.dma_start(out[ds((2 * j + q) * P, rows), :], stage[0:rows, q, 0:D]).then_inc(f_out[q], 16)
                each(sp, store)
                sp.wait_ge(f_out[0], 16 * (WHOLE // 2 + 2))
                sp.wait_ge(f_out[1], 16 * (WHOLE // 2 + 1))


_INS = ["x", "src", "dst", "edge_attr_128", "edge_weight", "L0_gnn_W_l", "L0_gnn_b_l", "L0_gnn_W_r", "L0_gnn_b_r",
        "L0_gnn_att", "L0_gnn_bias", "L1_gnn_W", "L1_gnn_b", "L1_gnn_root", "L1_gnn_We", "L1_gnn_be",
        "L1_gnn_gamma", "L1_gnn_beta"]

def kernel(**inputs):
    import concourse.bacc as bacc
    from concourse.bass_utils import run_bass_kernel_spmd

    nc = bacc.Bacc("TRN2", target_bir_lowering=False, num_devices=1)
    arrays, args = {}, []
    for name in _INS:
        a = np.ascontiguousarray(inputs[name])
        arrays[f"in_{name}"] = a
        args.append(nc.dram_tensor(f"in_{name}", a.shape, mybir.dt.from_np(a.dtype), kind="ExternalInput").ap())
    out = nc.dram_tensor("out", (N, D), F32, kind="ExternalOutput").ap()
    program(nc, *args, out)
    return run_bass_kernel_spmd(nc, [arrays], core_ids=[0]).results[0]["out"]
```

```python
from contextlib import ExitStack

import numpy as np

import concourse.bass as bass
from concourse import mybir

F32, I32, BF16 = mybir.dt.float32, mybir.dt.int32, mybir.dt.bfloat16
ALU = mybir.AluOpType
ACT = mybir.ActivationFunctionType
DVE = mybir.EngineType.DVE
SP = mybir.EngineType.SP

P = 128
N, E, D, ED, H, C, L = 3125, 53125, 256, 128, 8, 32, 5
HALVES = D // P
NC = P // H
KT = -(-E // (P * NC))
NT = NC * KT
CH = KT * P
FULL = E // P
TAIL = E - FULL * P
RB = NT // 4
NP = -(-(N + P) // P) * P
NTILE = NP // P
JC = 2 * P
JT = NP // JC
G = 4
NG = NC // G
RING = 4
BANKS = 8
S_RING = 8
RESET = -1e38
NO_EDGE = -1e30
LN2_96 = 66.54212933375474
EPS = 1e-5
FAR = 1000000
GW = D + 1
PRM = ["att", "bias", "b", "be", "root", "gamma", "beta"]
PROWS = [2, 2, 2 * L, 2 * L, 2 * L, 2 * L, 2 * L]
PCOL = {n: sum(PROWS[:i]) for i, n in enumerate(PRM)}
NPRM = sum(PROWS)


def pipelined(eng, stages, count=NT, width=NC):
    most = max(lead for lead, _ in stages)

    def at(n, stage):
        if 0 <= n < count:
            stage(n // width, n % width)

    for n in range(-most, 0):
        for lead, stage in stages:
            at(n + lead, stage)
    whole = (count - most) // width
    with eng.Fori(0, whole) as k:
        for c in range(width):
            for lead, stage in stages:
                stage(k + (c + lead) // width, (c + lead) % width)
    for n in range(whole * width, count):
        for lead, stage in stages:
            at(n + lead, stage)


def program(nc, x, src, dst, edge_attr, edge_weight, W_l, b_l, W_r, b_r, att, bias,
            W, b, root, We, be, gamma, beta, out):
    ds = bass.ds
    ctx = ExitStack()
    with ctx:
        ctx.enter_context(nc.allow_non_contiguous_dma(reason="single elements at the chunks' borders"))

        def sb(name, shape, dt=F32):
            return ctx.enter_context(nc.sbuf_tensor(name, shape, dt))

        def sem(name):
            return ctx.enter_context(nc.semaphore(name))

        primed = []

        def ring_sem(name, slots=RING):
            s = sem(name)
            primed.append((s, slots))
            return s

        xl_table = nc.dram_tensor("xl_table", (NP, GW), F32).ap()
        x_l_rows = nc.dram_tensor("x_l_rows", (NP, D), F32).ap()
        xr_table = nc.dram_tensor("xr_table", (NP, D), F32).ap()
        gcn_table = nc.dram_tensor("gcn_table", (NP, D), F32).ap()
        attr_T = nc.dram_tensor("attr_T", (NT // G, P, G * P), F32).ap()

        hT = sb("hT", [P, HALVES, NP])
        acc = sb("acc", [P, HALVES, NP])
        conv0 = sb("conv0", [P, HALVES, NP])
        x1T = sb("x1T", [P, HALVES, NP + 2])
        dinv_b = sb("dinv_b", [P, NP + 2])
        bwd_max = sb("bwd_max", [P, CH])[:]
        scores = conv0[:, 0, :]
        scoresT = conv0[:, 1, :]
        x1flat = x1T[:].rearrange("p a n -> p (a n)")
        breaks = x1flat[:, 0:CH + 1]
        fwd_max = x1flat[:, CH + 2:2 * CH + 2]
        chunk_dst = dinv_b[:, 0:CH + 2].bitcast(I32)
        den = dinv_b[0:H, 0:NP]

        src_idx = sb("src_idx", [P, NT + NC], I32)
        src_hi = sb("src_hi", [P, NT])
        src_lo = sb("src_lo", [P, NT])
        dst_rel = sb("dst_rel", [P, NT])
        log_w = sb("log_w", [P, NT])
        dinv_src = sb("dinv_src", [P, NT])
        base_f = sb("base_f", [1, NT])
        base_i = sb("base_i", [1, NT], I32)

        xg = sb("xg", [P, NC, GW])
        idx = sb("idx", [P, NC], I32)
        S = sb("S", [P, RING, P])
        ring_a = sb("ring_a", [P, RING, D])
        ring_b = sb("ring_b", [P, RING, D])
        ring_c = sb("ring_c", [P, RING, P])
        fifths = sb("fifths", [P, RING, D])
        attr_in = sb("attr_in", [P, NG, G, P])
        attr_out = sb("attr_out", [P, 2, G * P])
        ex_g = sb("ex_g", [P, NG, H, G])
        tiles = sb("tiles", [P, 2, HALVES, P])
        stage = sb("stage", [P, 2, 2 * D])

        wA = sb("wA", [P, HALVES, D])
        wB = sb("wB", [P, HALVES, D])
        rowbias = sb("rowbias", [P, 2, D])
        prm_rows = sb("prm_rows", [NPRM, P])
        prm = sb("prm", [P, NPRM])
        root_be = sb("root_be", [P, 2 * L])
        flat = conv0[:].rearrange("p a n -> p (a n)")
        W_all = flat[:, 0:2 * L * D].rearrange("p (i n) -> p i n", i=2 * L)
        We_all = flat[:, 2 * L * D:3 * L * D].rearrange("p (l n) -> p l n", l=L)
        b_rows, be_rows = flat[:, 3 * L * D:4 * L * D], flat[:, 4 * L * D:5 * L * D]
        b_all = b_rows.rearrange("p (l n) -> p l n", l=L)
        floor_l = sb("floor_l", [P, L])
        ident = sb("ident", [P, P])
        ident_bf = sb("ident_bf", [P, P], BF16)
        ones = sb("ones", [P, P])
        mean_w = sb("mean_w", [P, P])
        iota_i = sb("iota_i", [P, P], I32)
        iota_f = sb("iota_f", [P, P])
        head_of = sb("head_of", [H, D])
        att_w = sb("att_w", [P, HALVES, H])
        spare = fwd_max.bitcast(BF16)
        onehot_lo = spare[:, 0:NC * P].rearrange("p (c n) -> p c n", c=NC)
        onehot_hi = spare[:, NC * P:NC * (P + NTILE)].rearrange("p (c n) -> p c n", c=NC)
        counts = sb("counts", [P, NTILE])
        dinv_n = sb("dinv_n", [P, NTILE])
        invdeg_n = sb("invdeg_n", [P, NTILE])
        small = sb("small", [P, 64])
        carry = ring_b[0:1, :, :].rearrange("p r d -> p (r d)").rearrange("p (i n) -> p i n", i=8)
        stats = sb("stats", [P, HALVES, 8, 6])
        mv = sb("mv", [P, HALVES, 2])
        eps = sb("eps", [P, 1])

        ps = [ctx.enter_context(nc.psum_tensor(f"ps{i}", [P, 512], F32)) for i in range(8)]

        def halves(bank, n):
            return ps[bank][:, 0:HALVES * n].rearrange("p (a n) -> p a n", a=HALVES)

        def of(n, slots=RING):
            return n + 1 + slots

        def reuse(n):
            return n + 1

        def bases(eng_type, k):
            return nc.values_load_multi_w_load_instructions(base_i[0:1, ds(k * NC, NC)], engines=(eng_type,),
                                                            min_val=0, max_val=N - 1,
                                                            skip_runtime_bounds_check_because="clamped to N - 1")[1]

        def gathers(pool, table, width, idx_ready, arrived, layer):
            with pool.Fori(0, KT) as k:
                for g in range(NG):
                    for c in range(g * G, g * G + G):
                        if c == g * G:
                            wait_apart(pool, idx_ready, (layer * (KT + 1) + k) * NG + g + 1)
                        pool.indirect_dma_start(xg[:, c, 0:width], None, table,
                                                bass.IndirectOffsetOnAxis(ap=idx[:, c:c + 1], axis=0)
                                                ).then_inc(arrived[g], 16)

        def first_indices(idx_ready):
            for g in range(NG):
                nc.vector.tensor_copy(idx[:, g * G:g * G + G], src_idx[:, g * G:g * G + G]).then_inc(idx_ready, 1)

        def next_indices(k, g, idx_ready):
            nc.vector.tensor_copy(idx[:, g * G:g * G + G],
                                  src_idx[:, ds((k + 1) * NC + g * G, G)]).then_inc(idx_ready, 1)

        def wait_apart(eng, s, value):
            value = value if isinstance(value, int) else eng.to_reg(value)
            eng.wait_ge(consts, 1)
            eng.wait_ge(s, value)

        gw_in, gx_in = sem("gw_in"), [sem(f"gx_in{q}") for q in range(2)]
        gx_T, gx_copy, gt_mm, gt_row = [ring_sem(n, 2) for n in ("gx_T", "gx_copy", "gt_mm", "gt_row")]
        gt_out = [ring_sem(f"gt_out{q}", 48) for q in range(2)]

        aidx_ready, axg_in = sem("aidx_ready"), [sem(f"axg_in{g}") for g in range(NG)]
        axr_in = [sem(f"axr_in{c}") for c in range(NC)]
        aS_ready, aT_done, aST_ready, afifth, alk_ready, asc_done = [
            ring_sem(n) for n in ("aS_ready", "aT_done", "aST_ready", "afifth", "alk_ready", "asc_done")]
        gx_done = ring_sem("gx_done", NC)
        asc_copied = ring_sem("asc_copied", 2)
        ident_done = sem("ident_done")
        hist_in, hist_mm, hist_added = sem("hist_in"), sem("hist_mm"), sem("hist_added")

        sm_T, sm_copy, sm_ends, sm_rows, sm_carry, sm_cols, sm_diff, sm_ex, own_s = [
            sem(n) for n in ("sm_T", "sm_copy", "sm_ends", "sm_rows", "sm_carry", "sm_cols", "sm_diff", "sm_ex", "own_s")]
        deg_done, root_done, dinv_done, dinv_out = [sem(n) for n in ("deg_done", "root_done", "dinv_done", "dinv_out")]

        bidx_ready, bxg_in = sem("bidx_ready"), [sem(f"bxg_in{g}") for g in range(NG)]
        bat_in = [sem(f"bat_in{g}") for g in range(NG)]
        b_square, b_S, b_ready, b_mm, b_acc = [ring_sem(n) for n in ("b_square", "b_S", "b_ready", "b_mm", "b_acc")]
        bex_ready = sem("bex_ready")
        bat_T, bat_copy = ring_sem("bat_T", NG), ring_sem("bat_copy", 2)
        bat_out = [ring_sem(f"bat_out{i}", 16) for i in range(2)]

        bc_mm, bc_copy = sem("bc_mm"), sem("bc_copy")
        ln_rden, ln_den, ln_part, ln_z, ln_mean, ln_d, ln_sq, ln_var, ln_sd, ln_rs, ln_out = [
            ring_sem(n, 2) for n in ("ln_rden", "ln_den", "ln_part", "ln_z", "ln_mean", "ln_d", "ln_sq", "ln_var",
                                     "ln_sd", "ln_rs", "ln_out")]

        lw_in = sem("lw_in")
        lt_tile, lt_mm, lt_row, lr_T, lr_relu, lr_acc = [
            ring_sem(n) for n in ("lt_tile", "lt_mm", "lt_row", "lr_T", "lr_relu", "lr_acc")]
        lt_out = [ring_sem(f"lt_out{q}", 16) for q in range(RING)]
        cidx_ready, cxg_in = sem("cidx_ready"), [sem(f"cxg_in{g}") for g in range(NG)]
        cat_in = [sem(f"cat_in{g}") for g in range(NG)]
        c_ee = ring_sem("c_ee", NC)
        c_sum, c_msg, c_mm, c_acc = [ring_sem(n) for n in ("c_sum", "c_msg", "c_mm", "c_acc")]
        GROUPS = -(-NTILE // RING)
        bn_update = ring_sem("bn_update", GROUPS)
        own_bn, bn_var, bn_sd, bn_shift, bn_norm = [sem(n) for n in ("own_bn", "bn_var", "bn_sd", "bn_shift", "bn_norm")]

        f_tile, f_T, f_stats, f_var, f_sd, f_rs = [
            ring_sem(n) for n in ("f_tile", "f_T", "f_stats", "f_var", "f_sd", "f_rs")]
        f_row = ring_sem("f_row", BANKS)
        f_out = [ring_sem(f"f_out{q}", 16) for q in range(RING)]

        rows_i = flat[:, 0:3584].bitcast(I32)
        rows_f = flat[:, 3584:3584 + 1536]
        SROW, DROW, WROW = 0, 512, 1024
        rows_in, chunk_in = sem("rows_in"), sem("chunk_in")
        consts, own_v, rows_T, base_b = sem("consts"), sem("own_v"), sem("rows_T"), sem("base_b")
        log_done, own_p = sem("log_done"), sem("own_p")
        rows_float, base_done, scaled_w = sem("rows_float"), sem("base_done"), sem("scaled_w")
        with nc.Block() as block:
            @block.scalar
            def _(act):
                for w, a in ((wA, W_l), (wB, W_r)):
                    act.dma_start(w[:], a.rearrange("(h p) n -> p h n", p=P)).then_inc(gw_in, 16)
                for i, a in enumerate((b_l, b_r)):
                    act.dma_start(rowbias[:, i, :],
                                 a.rearrange("(a n) -> a n", a=1).to_broadcast([P, D])).then_inc(gw_in, 16)

            @block.gpsimd
            def _(pool):
                nc.gpsimd.iota(iota_i[:], pattern=[[1, P]], base=0, channel_multiplier=0)
                nc.gpsimd.memset(ident[:], 0.0).then_inc(own_p, 1)
                nc.gpsimd.memset(head_of[:], 1.0).then_inc(own_p, 1)
                nc.gpsimd.memset(ones[:], 1.0)
                nc.gpsimd.memset(mean_w[:], 1.0 / D)
                nc.gpsimd.memset(eps[:], EPS)
                nc.gpsimd.memset(floor_l[:, 0:L - 1], 0.0)
                nc.gpsimd.memset(floor_l[:, L - 1:L], -3e38)
                pool.wait_ge(own_p, 2)
                nc.gpsimd.affine_select(out=ident[:], in_=ident[:], compare_op=ALU.not_equal, fill=1.0, base=0,
                                        pattern=[[-1, P]], channel_multiplier=1)
                nc.gpsimd.affine_select(out=head_of[:], in_=head_of[:], compare_op=ALU.is_ge, fill=0.0, base=0,
                                        pattern=[[1, D]], channel_multiplier=-C).then_inc(own_p, 1)
                pool.wait_ge(own_p, 3)
                nc.gpsimd.affine_select(out=head_of[:], in_=head_of[:], compare_op=ALU.is_ge, fill=0.0, base=C - 1,
                                        pattern=[[-1, D]], channel_multiplier=C).then_inc(consts, 1)

            @block.sync
            def _(sp):
                for s, slots in primed:
                    sp.sem_inc(s, slots)

            @block.vector
            def _(dve):
                nc.vector.memset(ring_a[:], 0.0)
                nc.vector.memset(rows_i[0:RB, SROW:SROW + 512], NTILE * P + P - 1)
                nc.vector.memset(rows_i[0:RB, DROW:DROW + 512], FAR)
                nc.vector.memset(rows_f[0:RB, WROW:WROW + 512], 1.0)
                nc.vector.memset(chunk_dst, -1)

        with nc.Block() as block:
            @block.sync
            def _(sp):
                lh = "l (h p) -> (l h) p"
                for name, a in zip(PRM, (att.rearrange("(a h) c -> a (h c)", h=4),
                                         bias.rearrange("(a p) -> a p", p=P),
                                         b.rearrange(lh, p=P), be.rearrange(lh, p=P), root.rearrange(lh, p=P),
                                         gamma.rearrange(lh, p=P), beta.rearrange(lh, p=P))):
                    r = PCOL[name]
                    sp.dma_start(prm_rows[r:r + a.shape[0], :], a).then_inc(rows_in, 16)
                for col, a, view in ((SROW, src, rows_i), (DROW, dst, rows_i), (WROW, edge_weight, rows_f)):
                    rows = view[0:RB, col:col + 512].rearrange("p (q e) -> p q e", q=4)
                    whole = a[0:3 * RB * P].rearrange("(q p e) -> p q e", p=RB, e=P)
                    sp.dma_start(rows[:, 0:3, :], whole).then_inc(rows_in, 16)
                    rest = a[3 * RB * P:FULL * P].rearrange("(p e) -> p e", e=P)
                    sp.dma_start(rows[0:RB - 1, 3, :], rest).then_inc(rows_in, 16)
                    last = a[FULL * P:E].rearrange("(a e) -> a e", a=1)
                    sp.dma_start(rows[RB - 1:RB, 3, 0:TAIL], last).then_inc(rows_in, 16)

                def store(j, q):
                    sp.wait_ge(gt_row, of(2 * j + q, 2))
                    rows = ds((2 * j + q) * P, P)
                    sp.dma_start(xl_table[rows, 0:D], stage[:, q, 0:D]).then_inc(gt_out[q], 16)
                    sp.dma_start(x_l_rows[rows, :], stage[:, q, 0:D]).then_inc(gt_out[q], 16)
                    sp.dma_start(xr_table[rows, :], stage[:, q, D:2 * D]).then_inc(gt_out[q], 16)

                with sp.Fori(0, JT) as j:
                    for q in range(2):
                        store(j, q)
                for q in range(2):
                    sp.wait_ge(gt_out[q], 48 * (JT + 1))
                sp.wait_ge(rows_in, 16 * (9 + len(PRM)))

            @block.gpsimd
            def _(pool):
                def load(j, q, rows=P):
                    pool.wait_ge(gx_T, reuse(2 * j + q))
                    pool.dma_start(ring_a[0:rows, q, :], x[ds((2 * j + q) * P, rows), :]).then_inc(gx_in[q], 16)

                with pool.Fori(0, JT - 1) as j:
                    for q in range(2):
                        load(j, q)
                load(JT - 1, 0, N - N // P * P)

            @block.tensor
            def _(pe):
                pe.wait_ge(gw_in, 64)

                def turn(j, q):
                    pe.wait_ge(gx_in[q], 16 * (j + 1))
                    for a in range(HALVES):
                        last = nc.tensor.transpose(ps[q][:, a * P:a * P + P], ring_a[:, q, a * P:a * P + P], ident[:])
                    last.then_inc(gx_T, 1)

                def products(j, q):
                    pe.wait_ge(gx_copy, of(2 * j + q, 2))
                    pe.wait_ge(gt_row, reuse(2 * j + q))
                    for i, w in enumerate((wA, wB)):
                        for a in range(HALVES):
                            last = nc.tensor.matmul(ps[2 + q][:, i * D:i * D + D], tiles[:, q, a, :], w[:, a, :],
                                                    start=(a == 0), stop=(a == HALVES - 1))
                    last.then_inc(gt_mm, 1)

                turn(0, 0)
                with pe.Fori(0, JT - 1) as j:
                    turn(j, 1)
                    products(j, 0)
                    turn(j + 1, 0)
                    products(j, 1)
                products(JT - 1, 0)
                products(JT - 1, 1)

            @block.scalar
            def _(act):
                def copies(j, q):
                    act.wait_ge(gx_T, of(2 * j + q, 2))
                    act.wait_ge(gt_mm, reuse(2 * j + q))
                    nc.scalar.copy(tiles[:, q, :, :], ps[q][:, 0:D].rearrange("p (a n) -> p a n", a=HALVES))
                    nc.scalar.copy(hT[:, :, ds((2 * j + q) * P, P)],
                                   ps[q][:, 0:D].rearrange("p (a n) -> p a n", a=HALVES)).then_inc(gx_copy, 1)

                with act.Fori(0, JT - 1) as j:
                    copies(j, 0)
                    copies(j, 1)
                copies(JT - 1, 0)
                act.wait_ge(gt_mm, reuse(2 * JT - 1))
                nc.scalar.memzero(hT[:, :, (NTILE - 1) * P:NTILE * P])
                nc.scalar.memzero(tiles[:, 1, :, :]).then_inc(gx_copy, 1)

            @block.vector
            def _(dve):
                dve.wait_ge(gw_in, 64)
                both = rowbias[:].rearrange("p i d -> p (i d)")
                with dve.Fori(0, JT) as j:
                    for q in range(2):
                        dve.wait_ge(gt_mm, of(2 * j + q, 2))
                        dve.wait_ge(gt_out[q], 48 * (j + 1))
                        nc.vector.tensor_tensor(stage[:, q, :], ps[2 + q][:], both, ALU.add).then_inc(gt_row, 1)

        with nc.Block() as block:
            @block.sync
            def _(sp):
                for c in range(NC):
                    first, end = max(0, c * CH - 1), min(E, c * CH + CH + 1)
                    col = first - (c * CH - 1)
                    sp.dma_start(chunk_dst[c::NC, col:col + end - first],
                                 dst[first:end].rearrange("(a e) -> a e", a=1).to_broadcast([H, end - first])
                                 ).then_inc(chunk_in, 16)

            @block.scalar
            def _(act):
                act.wait_ge(scaled_w, 1)
                nc.scalar.activation(log_w[:], log_w[:], ACT.Ln).then_inc(log_done, 1)

            @block.tensor
            def _(pe):
                pe.wait_ge(rows_float, 1)
                for i, col in enumerate((SROW, DROW, WROW)):
                    for q in range(4):
                        nc.tensor.transpose(ps[i][:, q * RB:q * RB + RB],
                                            rows_f[0:RB, col + q * P:col + q * P + P], ident[0:RB, 0:RB])
                nc.tensor.transpose(ps[3][:, 0:NPRM], prm_rows[:], ident[0:NPRM, 0:NPRM])
                for a in range(HALVES):
                    last = nc.tensor.transpose(ps[3][:, 64 + a * H:64 + a * H + H], head_of[:, a * P:a * P + P],
                                               ident[0:H, 0:H])
                last.then_inc(rows_T, 1)
                pe.wait_ge(base_done, 1)
                nc.tensor.matmul(ps[4][:, 0:NT], ones[0:1, :], base_f[:], start=True, stop=True).then_inc(base_b, 1)
            @block.vector
            def _(dve):
                chain = [0]

                def link(ins):
                    chain[0] += 1
                    ins.then_inc(own_v, 1)
                    dve.wait_ge(own_v, chain[0])

                nc.vector.tensor_copy(rows_f[0:RB, SROW:SROW + 512], rows_i[0:RB, SROW:SROW + 512])
                nc.vector.tensor_copy(rows_f[0:RB, DROW:DROW + 512],
                                      rows_i[0:RB, DROW:DROW + 512]).then_inc(rows_float, 1)
                nc.vector.tensor_copy(iota_f[:], iota_i[:])

                def kc(t):
                    return t.rearrange("p (k c) -> p k c", c=NC)

                def from_ps(i, p=P):
                    return ps[i][0:p, 0:NT].rearrange("p (c k) -> p k c", c=NC)

                raw = rows_i[:, 2048:2048 + NT]
                hi_i = rows_i[:, 2560:2560 + NT]
                lo_i = rows_i[:, 3072:3072 + NT]
                tiny, zero = fwd_max[:, 0:NT], fwd_max[:, 512:512 + NT]
                lifted, weight = fwd_max[:, 1024:1024 + NT], fwd_max[:, 1536:1536 + NT]
                dve.wait_ge(rows_T, 1)
                nc.vector.tensor_copy(kc(dst_rel[:]), from_ps(1))
                link(nc.vector.tensor_scalar(kc(base_f[:]), from_ps(1, 1), float(N - 1), None, ALU.min))
                nc.vector.tensor_copy(base_i[:], base_f[:]).then_inc(base_done, 1)
                nc.vector.tensor_scalar(kc(src_idx[:, 0:NT]), from_ps(0), float(N - 1), None, ALU.min)
                nc.vector.memset(src_idx[:, NT:NT + NC], 0)
                link(nc.vector.tensor_copy(kc(raw), from_ps(0)))
                link(nc.vector.tensor_scalar(hi_i, raw, 7, None, ALU.arith_shift_right))
                link(nc.vector.tensor_scalar(lo_i, raw, P - 1, None, ALU.bitwise_and))
                nc.vector.tensor_copy(src_hi[:], hi_i)
                nc.vector.tensor_copy(src_lo[:], lo_i)
                link(nc.vector.tensor_copy(kc(weight), from_ps(2)))
                link(nc.vector.tensor_scalar(tiny, weight, 2.0 ** -64, None, ALU.is_lt))
                link(nc.vector.tensor_scalar(zero, weight, 0.0, NO_EDGE, ALU.is_equal, ALU.mult))
                link(nc.vector.scalar_tensor_tensor(lifted, tiny, 2.0 ** 96, weight, ALU.mult, ALU.mult))
                link(nc.vector.scalar_tensor_tensor(log_w[:], tiny, 0.0, weight, ALU.is_equal, ALU.mult))
                link(nc.vector.tensor_tensor(log_w[:], log_w[:], lifted, ALU.add))
                nc.vector.tensor_scalar(log_w[:], log_w[:], 2.0 ** -64, None, ALU.max).then_inc(scaled_w, 1)
                dve.wait_ge(base_b, 1)
                link(nc.vector.tensor_tensor(dst_rel[:], dst_rel[:], ps[4][:, 0:NT], ALU.subtract))
                link(nc.vector.tensor_copy(prm[:], ps[3][:, 0:NPRM]))
                for a in range(HALVES):
                    nc.vector.tensor_scalar(att_w[:, a, :], ps[3][:, 64 + a * H:64 + a * H + H],
                                            prm[:, a:a + 1], None, ALU.mult)
                nc.vector.tensor_tensor(root_be[:], prm[:, PCOL["root"]:PCOL["root"] + 2 * L],
                                        prm[:, PCOL["be"]:PCOL["be"] + 2 * L], ALU.subtract)
                dve.wait_ge(log_done, 1)
                link(nc.vector.scalar_tensor_tensor(log_w[:], tiny, -LN2_96, log_w[:], ALU.mult, ALU.add))
                link(nc.vector.tensor_tensor(log_w[:], log_w[:], zero, ALU.add))
                dve.wait_ge(chunk_in, 16 * NC)
                link(nc.vector.tensor_tensor(breaks, chunk_dst[:, 1:CH + 2], chunk_dst[:, 0:CH + 1], ALU.not_equal))
                link(nc.vector.tensor_scalar(breaks, breaks, RESET, None, ALU.mult))
                link(nc.vector.tensor_tensor(small[:, 2:4], chunk_dst[:, CH:CH + 2], chunk_dst[:, 0:2], ALU.not_equal))
                link(nc.vector.tensor_scalar(small[:, 2:4], small[:, 2:4], RESET, None, ALU.mult))
                link(nc.vector.memset(counts[:], 0.0))

        acc_flat = acc[:].rearrange("p a n -> p (a n)")
        xr_ring = acc_flat[:, 0:NC * D].rearrange("p (s d) -> p s d", s=NC)
        S_a = scoresT[:, 0:S_RING * P // 2].bitcast(BF16).rearrange("p (s n) -> p s n", s=S_RING)
        ST_a = scoresT[:, S_RING * P:2 * S_RING * P].rearrange("p (s n) -> p s n", s=S_RING)
        with nc.Block() as block:
            @block.gpsimd
            def _(pool):
                gathers(pool, x_l_rows, D, aidx_ready, axg_in, 0)

            @block.sync
            def _(sp):
                with sp.Fori(0, KT) as k:
                    base = bases(SP, k)
                    for c in range(NC):
                        sp.wait_ge(gx_done, reuse(k * NC + c))
                        sp.dma_start(xr_ring[:, c, :], xr_table[ds(base[c], P), :]).then_inc(axr_in[c], 16)

            @block.tensor
            def _(pe):
                def turn(k, c):
                    n = k * NC + c
                    pe.wait_ge(aS_ready, of(n))
                    pe.wait_ge(aST_ready, of(n - 2))
                    nc.tensor.transpose(ps[c % 2][:, 0:P // 2].bitcast(BF16), S_a[:, c % S_RING, :], ident_bf[:]
                                        ).then_inc(aT_done, 1)

                def sums(k, c):
                    n = k * NC + c
                    pe.wait_ge(aST_ready, of(n))
                    pe.wait_ge(axr_in[c], 16 * (k + 1))
                    pe.wait_ge(axg_in[c // G], 16 * G * (k + 1))
                    o = ps[2 + c % RING]
                    for a in range(HALVES):
                        nc.tensor.matmul(o[:, a * P:a * P + P], xg[:, c, a * P:a * P + P], ident[:],
                                         start=True, stop=False, is_transpose=True)
                        last = nc.tensor.matmul(o[:, a * P:a * P + P], xr_ring[:, c, a * P:a * P + P],
                                                ST_a[:, c % S_RING, :], start=False, stop=True)
                    last.then_inc(gx_done, 1)

                def score(k, c):
                    pe.wait_ge(alk_ready, of(k * NC + c))
                    if c % 8 == 0:
                        pe.wait_ge(asc_copied, reuse(2 * k + c // 8))
                    if c == 8:
                        pe.wait_ge(hist_added, k + 1)
                    for a in range(HALVES):
                        last = nc.tensor.matmul(ps[6 + c // 8][:, c * H:c * H + H],
                                                ring_a[:, c % RING, a * P:a * P + P], att_w[:, a, :],
                                                start=(a == 0), stop=(a == HALVES - 1))
                    last.then_inc(asc_done, 1)

                def histogram(k, c):
                    if c == 12:
                        pe.wait_ge(hist_in, k + 1)
                        for i in range(NC):
                            last = nc.tensor.matmul(ps[7][:, 256:256 + NTILE], onehot_lo[:, i, :], onehot_hi[:, i, :],
                                                    start=(i == 0), stop=(i == NC - 1))
                        last.then_inc(hist_mm, 1)

                pe.wait_ge(ident_done, 1)
                pipelined(pe, [(5, turn), (3, sums), (0, score), (0, histogram)])

            @block.scalar
            def _(act):
                def onehot_T(k, c):
                    act.wait_ge(aT_done, of(k * NC + c))
                    nc.scalar.copy(ST_a[:, c % S_RING, :],
                                   ps[c % 2][:, 0:P // 2].bitcast(BF16)).then_inc(aST_ready, 1)

                def fifth(k, c):
                    act.wait_ge(gx_done, of(k * NC + c, NC))
                    nc.scalar.mul(fifths[:, c % RING, :], ps[2 + c % RING][:, 0:D], 0.2).then_inc(afifth, 1)

                pipelined(act, [(5, onehot_T), (2, fifth)])

            @block.vector
            def _(dve):
                def onehot(k, c):
                    dve.wait_ge(gx_done, of(k * NC + c - S_RING, NC))
                    nc.vector.tensor_scalar(S_a[:, c % S_RING, :], iota_f[:], dst_rel[:, ds(k * NC + c, 1)], None,
                                            ALU.is_equal).then_inc(aS_ready, 1)

                def leaky(k, c):
                    dve.wait_ge(afifth, of(k * NC + c))
                    nc.vector.tensor_tensor(ring_a[:, c % RING, :], ps[2 + c % RING][:, 0:D],
                                            fifths[:, c % RING, :], ALU.max).then_inc(alk_ready, 1)

                def refill(k, c):
                    if c % G == G - 1:
                        next_indices(k, c // G, aidx_ready)

                def keep_scores(k, c):
                    if c % 8 == 7:
                        n, first, cols = k * NC + c, c - 7, ds(k * NC + c - 7, 8)
                        dve.wait_ge(asc_done, of(n))
                        to = scores[:, ds(k * P, P)].rearrange("p (h c) -> p h c", h=H)[:, :, first:first + 8]
                        got = ps[6 + c // 8][:, first * H:first * H + 8 * H].rearrange("p (c h) -> p h c", h=H)
                        nc.vector.tensor_tensor(to, got, log_w[:, cols].unsqueeze(1).to_broadcast([P, H, 8]),
                                                ALU.add).then_inc(asc_copied, 1)

                def add_counts():
                    nc.vector.tensor_tensor(counts[:], counts[:], ps[7][:, 256:256 + NTILE], ALU.add).then_inc(hist_added, 1)

                def histogram(k, c):
                    if c in (2, 4, 6, 8):
                        q = (c // 2 - 1) * 4
                        if c == 2:
                            dve.wait_ge(hist_mm, k + 1)
                            add_counts()
                        for to, part, wd in ((onehot_lo, src_lo, P), (onehot_hi, src_hi, NTILE)):
                            last = nc.vector.tensor_tensor(
                                to[:, q:q + 4, :], part[:, ds(k * NC + q, 4)].unsqueeze(2).to_broadcast([P, 4, wd]),
                                iota_f[:, 0:wd].unsqueeze(1).to_broadcast([P, 4, wd]), ALU.is_equal)
                        if c == 8:
                            last.then_inc(hist_in, 1)

                nc.vector.memset(ps[7][:, 256:256 + NTILE], 0.0).then_inc(hist_mm, 1)
                nc.vector.tensor_copy(ident_bf[:], ident[:]).then_inc(ident_done, 1)
                first_indices(aidx_ready)
                pipelined(dve, [(7, onehot), (1, leaky), (1, refill), (0, keep_scores), (0, histogram)])
                dve.wait_ge(hist_mm, KT + 1)
                add_counts()

        def chunk_group(g):
            return slice(g * 4 * P, min((g + 1) * 4, KT) * P)

        CG = -(-KT // 4)
        with nc.Block() as block:
            @block.tensor
            def _(pe):
                def turn(source, g, first):
                    if g + first >= 2:
                        pe.wait_ge(sm_copy, g + first - 1)
                    for k in range(4 * g, min(4 * g + 4, KT)):
                        last = nc.tensor.transpose(ps[(g + first) % 2][:, k % 4 * P:k % 4 * P + P],
                                                   source[:, k * P:k * P + P], ident[:])
                    last.then_inc(sm_T, 1)

                for g in range(CG):
                    turn(scores, g, 0)
                pe.wait_ge(sm_ends, 1)
                for i in range(4):
                    last = nc.tensor.transpose(ps[2][0:1, i * P:i * P + P], small[:, i:i + 1], ident[:])
                last.then_inc(sm_rows, 1)
                pe.wait_ge(sm_carry, 1)
                for i in range(2):
                    last = nc.tensor.transpose(ps[3][:, i:i + 1], carry[:, 6 + i, :], ident[0:1, 0:1])
                last.then_inc(sm_cols, 1)
                for g in range(CG):
                    pe.wait_ge(sm_ex, g + 1)
                    turn(scoresT, g, CG)

            @block.scalar
            def _(act):
                for a in range(HALVES):
                    col = PCOL["bias"] + a
                    nc.scalar.activation(hT[:, a, :], hT[:, a, :], ACT.Identity, bias=prm[:, col:col + 1])
                act.wait_ge(deg_done, 1)
                nc.scalar.activation(dinv_n[:], invdeg_n[:], ACT.Sqrt).then_inc(root_done, 1)
                for g in range(CG):
                    cols = chunk_group(g)
                    act.wait_ge(sm_diff, g + 1)
                    nc.scalar.activation(scoresT[:, cols], scoresT[:, cols], ACT.Exp).then_inc(sm_ex, 1)

            @block.gpsimd
            def _(pool):
                nc.gpsimd.memset(acc[:], 0.0)
                nc.gpsimd.memset(den, 1e-16)

            @block.vector
            def _(dve):
                chain = [0]

                def link(ins):
                    chain[0] += 1
                    ins.then_inc(own_s, 1)
                    dve.wait_ge(own_s, chain[0])

                for g in range(CG):
                    dve.wait_ge(sm_T, g + 1)
                    cols = chunk_group(g)
                    nc.vector.tensor_copy(scoresT[:, cols], ps[g % 2][:, 0:cols.stop - cols.start]).then_inc(sm_copy, 1)
                dve.wait_ge(sm_copy, CG)

                def scans(first_f, first_b):
                    nc.vector.tensor_tensor_scan(out=fwd_max, data0=breaks[:, 0:CH], data1=scoresT,
                                                 initial=first_f, op0=ALU.add, op1=ALU.max)
                    link(nc.vector.tensor_tensor_scan(out=bwd_max[:, ::-1], data0=breaks[:, 1:CH + 1][:, ::-1],
                                                      data1=scoresT[:, ::-1], initial=first_b,
                                                      op0=ALU.add, op1=ALU.max))

                scans(RESET, RESET)
                nc.vector.tensor_copy(small[:, 0:1], fwd_max[:, CH - 1:CH])
                nc.vector.tensor_copy(small[:, 1:2], bwd_max[:, 0:1]).then_inc(sm_ends, 1)
                degree, t = small[:, 8:8 + NTILE], small[:, 36:36 + NTILE]
                link(nc.vector.tensor_scalar(degree, counts[:], 1.0, None, ALU.add))
                nc.vector.reciprocal(invdeg_n[:], degree).then_inc(deg_done, 1)
                dve.wait_ge(root_done, 1)
                link(nc.vector.tensor_tensor(t, dinv_n[:], dinv_n[:], ALU.mult))
                link(nc.vector.tensor_tensor(t, t, degree, ALU.mult))
                link(nc.vector.tensor_scalar(t, t, -0.5, 1.5, ALU.mult, ALU.add))
                nc.vector.tensor_tensor(dinv_n[:], dinv_n[:], t, ALU.mult).then_inc(dinv_done, 1)

                dve.wait_ge(sm_rows, 1)
                link(nc.vector.tensor_copy(carry[:, 0:4, :], ps[2][0:1, :].rearrange("p (i n) -> p i n", i=4)))
                nc.vector.memset(carry[:, 6, 0:1], RESET)
                link(nc.vector.memset(carry[:, 7, P - 1:P], RESET))
                link(nc.vector.tensor_tensor_scan(out=carry[:, 4, :], data0=carry[:, 2, :], data1=carry[:, 0, :],
                                                  initial=RESET, op0=ALU.add, op1=ALU.max))
                link(nc.vector.tensor_tensor_scan(out=carry[:, 5, ::-1], data0=carry[:, 3, ::-1],
                                                  data1=carry[:, 1, ::-1], initial=RESET, op0=ALU.add, op1=ALU.max))
                nc.vector.tensor_copy(carry[:, 6, 1:P], carry[:, 4, 0:P - 1])
                nc.vector.tensor_copy(carry[:, 7, 0:P - 1], carry[:, 5, 1:P]).then_inc(sm_carry, 1)
                dve.wait_ge(sm_cols, 1)
                link(nc.vector.tensor_copy(small[:, 4:6], ps[3][:, 0:2]))
                scans(small[:, 4:5], small[:, 5:6])
                link(nc.vector.tensor_tensor(fwd_max, fwd_max, bwd_max, ALU.max))
                for g in range(CG):
                    cols = chunk_group(g)
                    nc.vector.tensor_tensor(scoresT[:, cols], scoresT[:, cols], fwd_max[:, cols],
                                            ALU.subtract).then_inc(sm_diff, 1)
                for g in range(CG):
                    dve.wait_ge(sm_T, CG + g + 1)
                    cols = chunk_group(g)
                    nc.vector.tensor_copy(scores[:, cols],
                                          ps[(g + CG) % 2][:, 0:cols.stop - cols.start]).then_inc(sm_copy, 1)

            @block.sync
            def _(sp):
                sp.wait_ge(dinv_done, 1)
                sp.dma_start(xl_table[:, D:GW].rearrange("(i p) w -> p i w", p=P),
                             dinv_n[:].unsqueeze(2)).then_inc(dinv_out, 16)
                sp.wait_ge(dinv_out, 16)

        with nc.Block() as block:
            @block.gpsimd
            def _(pool):
                gathers(pool, xl_table, GW, bidx_ready, bxg_in, 0)

            @block.sync
            def _(sp):
                by_chunk = edge_attr[0:(NC - 1) * CH, :].rearrange("(c k p) f -> k p c f", k=KT, p=P)

                def loads(k, last):
                    for g in range(NG):
                        sp.wait_ge(bat_T, reuse(k * NG + g))
                        whole = G if g < NG - 1 else G - 1
                        sp.dma_start(attr_in[:, g, 0:whole, :],
                                     by_chunk[ds(k, 1), :, g * G:g * G + whole, :].rearrange("k p c f -> (k p) c f")
                                     ).then_inc(bat_in[g], 16)
                    rows = TAIL if last else P
                    sp.dma_start(attr_in[0:rows, NG - 1, G - 1, :],
                                 edge_attr[ds(((NC - 1) * KT + k) * P, rows), :]).then_inc(bat_in[NG - 1], 16)

                with sp.Fori(0, KT - 1) as k:
                    loads(k, False)
                loads(KT - 1, True)

            @block.tensor
            def _(pe):
                def turn(k, c):
                    if c % G == 1:
                        g = c // G
                        pe.wait_ge(bat_in[g], (32 if g == NG - 1 else 16) * (k + 1))
                        pe.wait_ge(bat_copy, reuse(k * NG + g))
                        for j in range(G):
                            last = nc.tensor.transpose(ps[RING + g % 2][:, j * P:j * P + P], attr_in[:, g, j, :], ident[:])
                        last.then_inc(bat_T, 1)

                def product(k, c):
                    n = k * NC + c
                    pe.wait_ge(b_S, of(n))
                    pe.wait_ge(b_ready, of(n))
                    pe.wait_ge(b_acc, reuse(n))
                    o = ps[c % RING]
                    for a in range(HALVES):
                        nc.tensor.matmul(o[:, a * P:a * P + P], ring_a[:, c % RING, a * P:a * P + P],
                                         S[:, c % RING, :], start=True, stop=True)
                    nc.tensor.matmul(ps[c % RING][0:H, D:D + P], ex_g[:, c // G, :, c % G],
                                     S[:, c % RING, :], start=True, stop=True).then_inc(b_mm, 1)

                pipelined(pe, [(0, turn), (0, product)])

            @block.scalar
            def _(act):
                def keep(k, c):
                    if c % G == 1:
                        g = c // G
                        n = k * NG + g
                        act.wait_ge(bat_T, of(n, NG))
                        act.wait_ge(bat_out[g % 2], 16 * (2 * k + g // 2 + 1))
                        nc.scalar.copy(attr_out[:, g % 2, :], ps[RING + g % 2][:]).then_inc(bat_copy, 1)
                        act.wait_ge(bat_copy, of(n, 2))
                        act.dma_start(attr_T[ds(k * NG + g, 1), :, :].rearrange("k p e -> (k p) e"),
                                      attr_out[:, g % 2, :]).then_inc(bat_out[g % 2], 16)

                def square(k, c):
                    n = k * NC + c
                    wait_apart(act, b_S, reuse(n))
                    nc.scalar.activation(ring_c[:, c % RING, :], iota_f[:], ACT.Square, scale=-1.0,
                                         bias=dst_rel[:, ds(n, 1)]).then_inc(b_square, 1)

                def onehot(k, c):
                    n = k * NC + c
                    act.wait_ge(b_mm, reuse(n))
                    act.wait_ge(b_square, of(n))
                    nc.scalar.activation(S[:, c % RING, :], ring_c[:, c % RING, :], ACT.Relu, scale=-1.0,
                                         bias=ones[:, 0:1]).then_inc(b_S, 1)

                pipelined(act, [(4, square), (2, onehot), (0, keep)])
                for i in range(2):
                    act.wait_ge(bat_out[i], 16 * (2 * KT + 1))

            @block.vector
            def _(dve):
                def weigh(k, c):
                    n, g = k * NC + c, c // G
                    wait_apart(dve, b_mm, reuse(n))
                    if c % G == 0:
                        nc.vector.tensor_copy(
                            ex_g[:, g, :, :],
                            scores[:, ds(k * P, P)].rearrange("p (h c) -> p h c", h=H)[:, :, c:c + G]
                        ).then_inc(bex_ready, 1)
                        dve.wait_ge(bxg_in[g], 16 * G * (k + 1))
                        dve.wait_ge(bex_ready, k * NG + g + 1)
                    nc.vector.tensor_tensor(ring_a[:, c % RING, :].rearrange("p (h d) -> p h d", h=H),
                                            xg[:, c, 0:D].rearrange("p (h d) -> p h d", h=H),
                                            ex_g[:, g, :, c % G].unsqueeze(2).to_broadcast([P, H, C]),
                                            ALU.mult).then_inc(b_ready, 1)
                    if c % G == G - 1:
                        nc.vector.tensor_copy(dinv_src[:, ds(k * NC + g * G, G)].unsqueeze(2),
                                              xg[:, g * G:g * G + G, D:GW])
                        next_indices(k, g, bidx_ready)

                def add(k, c):
                    n = k * NC + c
                    dve.wait_ge(b_mm, of(n))
                    dve.wait_ge(b_acc, of(n - 1))
                    to = acc[:, :, ds(base_of[c], P)]
                    nc.vector.tensor_tensor(to, to, halves(c % RING, P),
                                            ALU.add)
                    to = den[:, ds(base_of[c], P)]
                    nc.vector.tensor_tensor(to, to, ps[c % RING][0:H, D:D + P],
                                            ALU.add).then_inc(b_acc, 1)

                base_of = [None] * NC

                def load_bases(k, c):
                    if c == 0:
                        base_of[:] = bases(DVE, k)

                first_indices(bidx_ready)
                pipelined(dve, [(2, weigh), (0, load_bases), (0, add)])

        with nc.Block() as block:
            @block.sync
            def _(sp):
                sp.dma_start(W_all, W.rearrange("l (h p) n -> p (l h) n", p=P)).then_inc(lw_in, 16)
                sp.dma_start(We_all, We.rearrange("l p n -> p l n")).then_inc(lw_in, 16)
                for to, v in ((b_rows, b), (be_rows, be)):
                    sp.dma_start(to, v.rearrange("(a l) n -> a (l n)", a=1).to_broadcast([P, L * D])).then_inc(lw_in, 16)

            @block.tensor
            def _(pe):

                def denominators(k, q):
                    j = 2 * k + q
                    pe.wait_ge(ln_rden, of(j, 2))
                    pe.wait_ge(ln_part, reuse(j))
                    for a in range(HALVES):
                        last = nc.tensor.matmul(ps[q][:, a * JC:a * JC + JC], head_of[:, a * P:a * P + P],
                                                den[:, ds(j * JC, JC)], start=True, stop=True)
                    last.then_inc(ln_den, 1)

                def mean(k, q):
                    j = 2 * k + q
                    pe.wait_ge(ln_z, of(j, 2))
                    pe.wait_ge(ln_d, reuse(j))
                    for a in range(HALVES):
                        last = nc.tensor.matmul(ps[2 + q][:, 0:JC], mean_w[:], acc[:, a, ds(j * JC, JC)],
                                                start=(a == 0), stop=(a == HALVES - 1))
                    last.then_inc(ln_mean, 1)

                def variance(k, q):
                    j = 2 * k + q
                    pe.wait_ge(ln_sq, of(j, 2))
                    pe.wait_ge(ln_sd, reuse(j))
                    for a in range(HALVES):
                        last = nc.tensor.matmul(ps[4 + q][:, 0:JC], mean_w[:], ring_a[:, 2 * q + a, :],
                                                start=(a == 0), stop=(a == HALVES - 1))
                    last.then_inc(ln_var, 1)

                pipelined(pe, [(4, denominators), (2, mean), (1, variance)], JT, 2)
                for g in range(CG):
                    if g >= 2:
                        pe.wait_ge(bc_copy, g - 1)
                    for i in range(4 * g, min(4 * g + 4, NTILE)):
                        last = nc.tensor.matmul(ps[6 + g % 2][:, i % 4 * P:i % 4 * P + P],
                                                dinv_n[:, i:i + 1].to_broadcast([P, P]), ident[:],
                                                start=True, stop=True)
                    last.then_inc(bc_mm, 1)

            @block.gpsimd
            def _(pool):
                def normal(k, q):
                    j = 2 * k + q
                    d = x1T[:, :, ds(j * JC, JC)]
                    wait_apart(pool, ln_rs, of(j, 2))
                    nc.gpsimd.tensor_tensor(d, d, ring_b[:, 2 + q, :].unsqueeze(1).to_broadcast([P, HALVES, JC]),
                                            ALU.mult).then_inc(ln_out, 1)

                def total(k, q):
                    j = 2 * k + q
                    z = acc[:, :, ds(j * JC, JC)]
                    wait_apart(pool, ln_part, of(j, 2))
                    nc.gpsimd.tensor_tensor(z, z, hT[:, :, ds(j * JC, JC)], ALU.add).then_inc(ln_z, 1)

                pipelined(pool, [(3, total), (0, normal)], JT, 2)

            @block.scalar
            def _(act):
                def square(k, q):
                    j = 2 * k + q
                    wait_apart(act, ln_var, reuse(j))
                    wait_apart(act, ln_d, of(j, 2))
                    nc.scalar.activation(ring_a[:, 2 * q:2 * q + 2, :], x1T[:, :, ds(j * JC, JC)],
                                         ACT.Square).then_inc(ln_sq, 1)

                def deviation(k, q):
                    j = 2 * k + q
                    act.wait_ge(ln_rs, reuse(j))
                    act.wait_ge(ln_var, of(j, 2))
                    nc.scalar.activation(ring_b[:, q, :], ps[4 + q][:, 0:JC], ACT.Sqrt, bias=eps[:]).then_inc(ln_sd, 1)

                def keep(k, q):
                    j = 2 * k + q
                    wait_apart(act, ln_out, of(j, 2))
                    nc.scalar.copy(hT[:, :, ds(j * JC, JC)], x1T[:, :, ds(j * JC, JC)])

                pipelined(act, [(2, square), (1, deviation), (0, keep)], JT, 2)
                for g in range(CG):
                    cols = chunk_group(g)
                    act.wait_ge(bc_mm, g + 1)
                    nc.scalar.copy(dinv_b[:, cols], ps[6 + g % 2][:, 0:cols.stop - cols.start]).then_inc(bc_copy, 1)

            @block.vector
            def _(dve):

                def inverse(k, q):
                    cols = ds((2 * k + q) * JC, JC)
                    nc.vector.reciprocal(den[:, cols], den[:, cols]).then_inc(ln_rden, 1)

                def part(k, q):
                    j = 2 * k + q
                    z = acc[:, :, ds(j * JC, JC)]
                    dve.wait_ge(ln_den, of(j, 2))
                    nc.vector.tensor_tensor(z, z, ps[q][:].rearrange("p (a n) -> p a n", a=HALVES),
                                            ALU.mult).then_inc(ln_part, 1)

                def centre(k, q):
                    j = 2 * k + q
                    cols = ds(j * JC, JC)
                    dve.wait_ge(ln_mean, of(j, 2))
                    nc.vector.tensor_tensor(x1T[:, :, cols], acc[:, :, cols],
                                            ps[2 + q][:, 0:JC].unsqueeze(1).to_broadcast([P, HALVES, JC]),
                                            ALU.subtract).then_inc(ln_d, 1)

                def rooted(k, q):
                    j = 2 * k + q
                    dve.wait_ge(ln_sd, of(j, 2))
                    dve.wait_ge(ln_out, reuse(j))
                    nc.vector.reciprocal(ring_b[:, 2 + q, :], ring_b[:, q, :]).then_inc(ln_rs, 1)

                pipelined(dve, [(5, inverse), (4, part), (2, centre), (0, rooted)], JT, 2)
                dve.wait_ge(lw_in, 64)
                nc.vector.tensor_tensor(b_rows, b_rows, be_rows, ALU.add)

        BN_LINKS = 5 * HALVES
        GROUP = RING * P
        node_tiles = fifths[:].rearrange("p s (a n) -> p s a n", a=HALVES)
        rows_out = stage[:].rearrange("p q (i n) -> p (q i) n", i=2)
        with nc.Block() as block:
            @block.sync
            def _(sp):
                with sp.Fori(0, L) as l:
                    def store(k, q):
                        sp.wait_ge(lt_row, of(l * NTILE + k * RING + q))
                        sp.dma_start(gcn_table[ds((k * RING + q) * P, P), :], rows_out[:, q, :]).then_inc(lt_out[q], 16)

                    pipelined(sp, [(0, store)], NTILE, RING)
                    with sp.Fori(0, KT) as k:
                        for g in range(NG):
                            n = (l * KT + k) * NG + g
                            sp.wait_ge(c_ee, G * n + G)
                            sp.dma_start(attr_in[:, g, :, :].rearrange("p j e -> p (j e)"),
                                         attr_T[ds(k * NG + g, 1), :, :].rearrange("k p e -> (k p) e")
                                         ).then_inc(cat_in[g], 16)

            @block.gpsimd
            def _(pool):
                with pool.Fori(0, L) as l:
                    gathers(pool, gcn_table, D, cidx_ready, cxg_in, l)

            @block.tensor
            def _(pe):
                with pe.Fori(0, L) as l:
                    def table(k, q):
                        n = l * NTILE + k * RING + q
                        pe.wait_ge(lt_tile, of(n))
                        pe.wait_ge(lt_row, reuse(n))
                        for a in range(HALVES):
                            last = nc.tensor.matmul(ps[q][:, 0:D], node_tiles[:, q, a, :],
                                                    W_all[:, ds(HALVES * l + a, 1), :].rearrange("p i n -> p (i n)"),
                                                    start=(a == 0), stop=(a == HALVES - 1))
                        last.then_inc(lt_mm, 1)

                    def turn(k, q):
                        n = l * NTILE + k * RING + q
                        pe.wait_ge(lt_row, of(n))
                        pe.wait_ge(lr_relu, reuse(n))
                        for a in range(HALVES):
                            last = nc.tensor.transpose(ps[RING + q][:, a * P:a * P + P],
                                                       rows_out[:, q, a * P:a * P + P], ident[:])
                        last.then_inc(lr_T, 1)

                    pipelined(pe, [(3, table), (1, turn)], NTILE, RING)

                    def edge_term(k, c):
                        n = (l * KT + k) * NC + c
                        pe.wait_ge(cat_in[c // G], 16 * ((l) * KT + k + 1))
                        nc.tensor.matmul(ps[c % RING][:, 0:D], attr_in[:, c // G, c % G, :],
                                         We_all[:, ds(l, 1), :].rearrange("p i n -> p (i n)"),
                                         start=True, stop=True).then_inc(c_ee, 1)

                    def sums(k, c):
                        n = (l * KT + k) * NC + c
                        pe.wait_ge(c_msg, of(n))
                        pe.wait_ge(c_acc, reuse(n))
                        o = ps[RING + c % RING]
                        for a in range(HALVES):
                            last = nc.tensor.matmul(o[:, a * P:a * P + P], ring_b[:, c % RING, a * P:a * P + P],
                                                    S[:, c % RING, :], start=True, stop=True)
                        last.then_inc(c_mm, 1)

                    pe.wait_ge(lt_row, of((l + 1) * NTILE - 1))
                    pe.wait_ge(lr_relu, of((l + 1) * NTILE - 1))
                    pipelined(pe, [(3, edge_term), (0, sums)])

            @block.scalar
            def _(act):
                with act.Fori(0, L) as l:
                    def tile_copy(k, q):
                        if q == 0:
                            wait_apart(act, bn_update, GROUPS * l + k + 1)
                        wait_apart(act, lt_mm, reuse(l * NTILE + k * RING + q))
                        nc.scalar.copy(node_tiles[:, q, :, :], hT[:, :, ds((k * RING + q) * P, P)]).then_inc(lt_tile, 1)

                    def root_term(k, q):
                        n = l * NTILE + k * RING + q
                        wait_apart(act, lr_T, of(n))
                        wait_apart(act, lr_acc, reuse(n))
                        for a in range(HALVES):
                            last = nc.scalar.activation(ring_b[:, q, a * P:a * P + P], ps[RING + q][:, a * P:a * P + P],
                                                        ACT.Relu, bias=root_be[:, ds(2 * l + a, 1)])
                        last.then_inc(lr_relu, 1)

                    pipelined(act, [(4, tile_copy), (0, root_term)], NTILE, RING)

                    def message(k, c):
                        wait_apart(act, c_sum, of((l * KT + k) * NC + c))
                        nc.scalar.activation(ring_b[:, c % RING, :], ring_a[:, c % RING, :], ACT.Relu,
                                             scale=dinv_src[:, ds(k * NC + c, 1)]).then_inc(c_msg, 1)

                    pipelined(act, [(0, message)])
                    for a in range(HALVES):
                        act.wait_ge(bn_var, HALVES * l + a + 1)
                        nc.scalar.activation(small[:, 4 * a:4 * a + 1], mv[:, a, 1:2], ACT.Sqrt,
                                             bias=eps[:]).then_inc(bn_sd, 1)
                        act.wait_ge(bn_shift, HALVES * l + a + 1)
                        nc.scalar.activation(acc[:, a, 0:N], acc[:, a, 0:N], ACT.Identity,
                                             scale=small[:, 4 * a + 2:4 * a + 3],
                                             bias=small[:, 4 * a + 3:4 * a + 4]).then_inc(bn_norm, 1)

            @block.vector
            def _(dve):
                with dve.Fori(0, L) as l:
                    def rows(k, q):
                        n = l * NTILE + k * RING + q
                        stores = -(-(NTILE - q) // RING)
                        dve.wait_ge(lt_mm, of(n))
                        dve.wait_ge(lr_T, reuse(n))
                        dve.wait_ge(lt_out[q], 16 * (l * stores + k + 1))
                        nc.vector.tensor_tensor(rows_out[:, q, :], ps[q][:, 0:D],
                                                b_all[:, ds(l, 1), :].rearrange("p l n -> p (l n)"),
                                                ALU.add).then_inc(lt_row, 1)

                    def root(k, q):
                        n, cols = l * NTILE + k * RING + q, ds((k * RING + q) * P, P)
                        dve.wait_ge(lr_relu, of(n))
                        nc.vector.tensor_tensor(acc[:, :, cols], ring_b[:, q, :].rearrange("p (a n) -> p a n", a=HALVES),
                                                dinv_b[:, cols].unsqueeze(1).to_broadcast([P, HALVES, P]),
                                                ALU.mult).then_inc(lr_acc, 1)

                    pipelined(dve, [(2, rows), (0, root)], NTILE, RING)
                    for q in range(RING):
                        dve.wait_ge(lt_out[q], 16 * ((l + 1) * -(-(NTILE - q) // RING) + 1))
                    dve.wait_ge(lr_acc, of((l + 1) * NTILE - 1))
                    first_indices(cidx_ready)

                    def add_rows(k, c):
                        n, g = (l * KT + k) * NC + c, c // G
                        dve.wait_ge(c_mm, reuse(n))
                        nc.vector.tensor_scalar(S[:, c % RING, :], iota_f[:], dst_rel[:, ds(k * NC + c, 1)], None,
                                                ALU.is_equal)
                        dve.wait_ge(c_ee, of(n, NC))
                        dve.wait_ge(cxg_in[g], 16 * G * ((l) * KT + k + 1))
                        nc.vector.tensor_tensor(ring_a[:, c % RING, :], ps[c % RING][:, 0:D], xg[:, c, 0:D],
                                                ALU.add).then_inc(c_sum, 1)
                        if c % G == G - 1:
                            next_indices(k, g, cidx_ready)

                    base_of = [None] * NC

                    def load_bases(k, c):
                        if c == 0:
                            base_of[:] = bases(DVE, k)

                    def add(k, c):
                        n = (l * KT + k) * NC + c
                        dve.wait_ge(c_mm, of(n))
                        dve.wait_ge(c_acc, of(n - 1))
                        to = acc[:, :, ds(base_of[c], P)]
                        nc.vector.tensor_tensor(to, to, halves(RING + c % RING, P),
                                                ALU.add).then_inc(c_acc, 1)

                    pipelined(dve, [(2, add_rows), (0, load_bases), (0, add)])

                    chain = [0]

                    def link(ins):
                        chain[0] += 1
                        ins.then_inc(own_bn, 1)
                        dve.wait_ge(own_bn, BN_LINKS * l + chain[0])

                    dve.wait_ge(c_acc, of((l + 1) * NT - 1))

                    def total(a):
                        link(nc.vector.tensor_tensor(acc[:, a, :], acc[:, a, :], dinv_b[:, 0:NP], ALU.mult))

                    def moments(a):
                        for i in range(-(-N // 512)):
                            last = nc.vector.bn_stats(stats[:, a, i, :], acc[:, a, i * 512:min(N, i * 512 + 512)])
                        chain[0] += 1
                        last.then_inc(own_bn, 1)
                        wait_apart(dve, own_bn, BN_LINKS * l + chain[0])
                        nc.vector.bn_aggr(mv[:, a, :], stats[:, a, 0:-(-N // 512), :]).then_inc(bn_var, 1)

                    def scales(a):
                        sd, rs, scale, shift = (small[:, 4 * a + i:4 * a + i + 1] for i in range(4))
                        dve.wait_ge(bn_sd, HALVES * l + a + 1)
                        link(nc.vector.reciprocal(rs, sd))
                        link(nc.vector.tensor_tensor(scale, rs, prm[:, ds(PCOL["gamma"] + 2 * l + a, 1)], ALU.mult))
                        link(nc.vector.tensor_tensor(shift, mv[:, a, 0:1], scale, ALU.mult))
                        nc.vector.tensor_tensor(shift, prm[:, ds(PCOL["beta"] + 2 * l + a, 1)], shift,
                                                ALU.subtract).then_inc(bn_shift, 1)

                    def update(a, cols):
                        return nc.vector.scalar_tensor_tensor(hT[:, a, cols], acc[:, a, cols], floor_l[:, ds(l, 1)],
                                                              hT[:, a, cols], ALU.max, ALU.add)

                    total(0)
                    moments(0)
                    total(1)
                    scales(0)
                    moments(1)
                    scales(1)
                    dve.wait_ge(bn_norm, HALVES * l + 1)
                    update(0, slice(0, N))
                    dve.wait_ge(bn_norm, HALVES * l + 2)
                    for i in range(GROUPS):
                        update(1, slice(i * GROUP, min(N, i * GROUP + GROUP))).then_inc(bn_update, 1)
                    assert chain[0] == BN_LINKS

        with nc.Block() as block:
            NT_OUT = -(-N // P)
            LAST = N - (NT_OUT - 1) * P

            def moments(q):
                return small[:, 16 + 2 * q:18 + 2 * q]

            @block.gpsimd
            def _(pool):
                def tile(k, c):
                    wait_apart(pool, f_T, reuse(k * BANKS + c))
                    cols = ds((k * BANKS + c) * P, P)
                    nc.gpsimd.tensor_tensor(node_tiles[:, c % RING, :, :], hT[:, :, cols], x1T[:, :, cols],
                                            ALU.add).then_inc(f_tile, 1)

                pipelined(pool, [(0, tile)], NT_OUT, BANKS)

            @block.tensor
            def _(pe):
                def turn(k, c):
                    pe.wait_ge(f_tile, of(k * BANKS + c))
                    pe.wait_ge(f_row, reuse(k * BANKS + c))
                    for a in range(HALVES):
                        last = nc.tensor.transpose(ps[c][:, a * P:a * P + P], node_tiles[:, c % RING, a, :], ident[:])
                    last.then_inc(f_T, 1)

                pipelined(pe, [(0, turn)], NT_OUT, BANKS)

            @block.scalar
            def _(act):
                def deviation(k, c):
                    q = c % RING
                    act.wait_ge(f_rs, reuse(k * BANKS + c))
                    act.wait_ge(f_var, of(k * BANKS + c))
                    nc.scalar.activation(small[:, 8 + q:9 + q], moments(q)[:, 1:2], ACT.Sqrt,
                                         bias=eps[:]).then_inc(f_sd, 1)

                pipelined(act, [(0, deviation)], NT_OUT, BANKS)

            @block.vector
            def _(dve):
                def statistics(k, c):
                    n, q = k * BANKS + c, c % RING
                    dve.wait_ge(f_T, of(n))
                    nc.vector.bn_stats(stats[:, 0, q, :], ps[c][:, 0:D]).then_inc(f_stats, 1)

                def aggregate(k, c):
                    n, q = k * BANKS + c, c % RING
                    wait_apart(dve, f_stats, of(n))
                    nc.vector.bn_aggr(moments(q), stats[:, 0, q:q + 1, :]).then_inc(f_var, 1)

                def inverse(k, c):
                    n, q = k * BANKS + c, c % RING
                    dve.wait_ge(f_sd, of(n))
                    nc.vector.reciprocal(small[:, 12 + q:13 + q], small[:, 8 + q:9 + q]).then_inc(f_rs, 1)

                def normal(k, c):
                    n, q = k * BANKS + c, c % RING
                    dve.wait_ge(f_rs, of(n))
                    dve.wait_ge(f_out[q], 16 * (2 * k + c // RING + 1))
                    nc.vector.tensor_scalar(rows_out[:, q, :], ps[c][:, 0:D], moments(q)[:, 0:1],
                                            small[:, 12 + q:13 + q], ALU.subtract, ALU.mult).then_inc(f_row, 1)

                pipelined(dve, [(3, statistics), (2, aggregate), (1, inverse), (0, normal)], NT_OUT, BANKS)

            @block.sync
            def _(sp):
                def store(k, c):
                    n, q = k * BANKS + c, c % RING
                    rows = LAST if isinstance(n, int) and n == NT_OUT - 1 else P
                    sp.wait_ge(f_row, of(n, BANKS))
                    sp.dma_start(out[ds(n * P, rows), :], rows_out[0:rows, q, :]).then_inc(f_out[q], 16)

                pipelined(sp, [(0, store)], NT_OUT, BANKS)
                for q in range(RING):
                    sp.wait_ge(f_out[q], 16 * (-(-(NT_OUT - q) // RING) + 1))


_INS = ["x", "src", "dst", "edge_attr_128", "edge_weight", "L0_gnn_W_l", "L0_gnn_b_l", "L0_gnn_W_r", "L0_gnn_b_r",
        "L0_gnn_att", "L0_gnn_bias", "L1_gnn_W", "L1_gnn_b", "L1_gnn_root", "L1_gnn_We", "L1_gnn_be",
        "L1_gnn_gamma", "L1_gnn_beta"]

def kernel(**inputs):
    import concourse.bacc as bacc
    from concourse.bass_utils import run_bass_kernel_spmd

    nc = bacc.Bacc("TRN2", target_bir_lowering=False, num_devices=1)
    arrays, args = {}, []
    for name in _INS:
        a = np.ascontiguousarray(inputs[name])
        arrays[f"in_{name}"] = a
        args.append(nc.dram_tensor(f"in_{name}", a.shape, mybir.dt.from_np(a.dtype), kind="ExternalInput").ap())
    out = nc.dram_tensor("out", (N, D), F32, kind="ExternalOutput").ap()
    program(nc, *args, out)
    return run_bass_kernel_spmd(nc, [arrays], core_ids=[0]).results[0]["out"]
```
